# Optimizing a Trainium2 kernel written in Bass

```python
import numpy as np
import jax
import jax.numpy as jnp

def _softmax(x, axis=-1):
    return jax.nn.softmax(x, axis=axis)

def _gelu(x):
    return jax.nn.gelu(x, approximate=True)

def _silu(x):
    return jax.nn.silu(x)

def _sigmoid(x):
    return jax.nn.sigmoid(x)

def _layernorm(x, axis=-1, eps=1e-05):
    m = jnp.mean(x, axis=axis, keepdims=True)
    v = jnp.var(x, axis=axis, keepdims=True)
    return (x - m) / jnp.sqrt(v + eps)

def _scatter_add(tgt, idx, src, axis=0):
    return tgt.at[idx].add(src)

def _segment_sum(src, seg, n):
    return jax.ops.segment_sum(src, seg, n)
kernel_name = 'mk_xattn_ffn_d4_seqx_r8_a7314f'

def setup_inputs(seed: int=0):
    np.random.seed(seed)
    _w = jnp.asarray

    def _rec_inputs():
        import jax
        import jax.numpy as jnp
        _rk = jax.random.key(seed)
        x = 7.22e-05 + 1 * jax.random.normal(jax.random.fold_in(_rk, 1), (16, 256, 128), jnp.float32)
        _lenS = 256 - jax.random.randint(jax.random.fold_in(_rk, 7), (16,), 0, max(1, 256 // 4) + 1, jnp.int32)
        _lenS2 = 64 - jax.random.randint(jax.random.fold_in(_rk, 8), (16,), 0, max(1, 64 // 4) + 1, jnp.int32)
        _ctx_1024P = jax.random.normal(jax.random.fold_in(_rk, 11), (16, 16, 128), jnp.float32)
        _ctx_1024c = jax.random.dirichlet(jax.random.fold_in(_rk, 511), 0.3 * jnp.ones((16,), jnp.float32), (16, 64))
        _ctx_1024t = jnp.einsum('bsk,bkd->bsd', _ctx_1024c, _ctx_1024P)
        _ctx_1024t = _ctx_1024t * jax.lax.rsqrt(jnp.mean(jnp.square(_ctx_1024t)) + 1e-12) * 0.953939
        ctx_1024 = 4.13588e-05 + 0.999923 * (_ctx_1024t + 0.3 * jax.random.normal(jax.random.fold_in(_rk, 611), (16, 64, 128), jnp.float32))
        itok_BxS2_0_99 = jax.random.randint(jax.random.fold_in(_rk, 12), (16, 64), 0, 100, jnp.int32)
        _validS = jnp.arange(256)[None, :] < _lenS[:, None]
        _validS2 = jnp.arange(64)[None, :] < _lenS2[:, None]
        _causal = jnp.tril(jnp.ones((256, 256), dtype=bool))
        mask_1x1xSxS2_ik0 = jnp.where(jnp.broadcast_to(_validS2[0:1, None, None, :], (1, 1, 256, 64)), 0, 1).astype(jnp.int32)
        mask_BxS2_bk0 = jnp.logical_not(jnp.broadcast_to(_validS2[:, :], (16, 64)))
        return (x, ctx_1024, itok_BxS2_0_99, mask_1x1xSxS2_ik0, mask_BxS2_bk0)
    x, ctx_1024, itok_BxS2_0_99, mask_1x1xSxS2_ik0, mask_BxS2_bk0 = _rec_inputs()

    def _L0_xattn_setup():
        import jax, jax.numpy as jnp
        import numpy as np
        B, S, D = (4, 256, 128)
        H = 16
        HD = D // H
        NEG = -1000000000.0
        key = jax.random.key(seed)
        ks = jax.random.split(key, 8)
        x = jax.random.normal(ks[0], (B, S, D), dtype=jnp.float32)
        y = jax.random.normal(ks[1], (B, S, D), dtype=jnp.float32)
        log_seqs = jax.random.randint(ks[2], (B, S), 0, 100, dtype=jnp.int64)
        sc = 1.0 / np.sqrt(D)
        Wq = jax.random.normal(ks[3], (D, D), dtype=jnp.float32) * sc
        Wk = jax.random.normal(ks[4], (D, D), dtype=jnp.float32) * sc
        Wv = jax.random.normal(ks[5], (D, D), dtype=jnp.float32) * sc
        Wo = jax.random.normal(ks[6], (D, D), dtype=jnp.float32) * sc
        bo = jnp.zeros((D,), dtype=jnp.float32)
        return {'x': x, 'y': y, 'log_seqs': log_seqs, 'pad_id': 0, 'Wq': Wq, 'Wk': Wk, 'Wv': Wv, 'Wo': Wo, 'bo': bo}
    _L0_xattn_all = _L0_xattn_setup()
    _L0_xattn_in = {k: v for k, v in _L0_xattn_all.items() if k in ('Wq', 'Wk', 'Wv', 'Wo', 'bo')}
    del _L0_xattn_all

    def _L0_ffn_setup():
        import jax, jax.numpy as jnp
        import numpy as np
        B, S, H, I, E, K = (2, 256, 128, 256, 8, 2)
        key = jax.random.key(seed)
        k1, k2, k3, k4, k5 = jax.random.split(key, 5)
        scale_h = 1.0 / np.sqrt(H)
        scale_i = 1.0 / np.sqrt(I)
        return {'x': jax.random.normal(k1, (B, S, H), dtype=jnp.float32), 'Wg': jax.random.normal(k2, (H, E), dtype=jnp.float32) * scale_h, 'W11': jax.random.normal(k3, (E, H, I), dtype=jnp.float32) * scale_h, 'W12': jax.random.normal(k4, (E, H, I), dtype=jnp.float32) * scale_h, 'W2': jax.random.normal(k5, (E, I, H), dtype=jnp.float32) * scale_i}
    _L0_ffn_all = _L0_ffn_setup()
    _L0_ffn_in = {k: v for k, v in _L0_ffn_all.items() if k in ('Wg', 'W11', 'W12', 'W2')}
    del _L0_ffn_all

    def _L1_xattn_setup():
        import jax, jax.numpy as jnp
        import numpy as np
        import math
        B, S, D, H = (2, 256, 128, 16)
        DK = D // H

        def _split_heads(x):
            b, s, _ = x.shape
            return x.reshape(b, s, H, DK).transpose(0, 2, 1, 3)
        key = jax.random.key(seed)
        ks = jax.random.split(key, 12)
        std = 1.0 / math.sqrt(D)
        inp = {'q': jax.random.normal(ks[0], (B, S, D), jnp.float32), 'k': jax.random.normal(ks[1], (B, S, D), jnp.float32), 'v': jax.random.normal(ks[2], (B, S, D), jnp.float32), 'mask': jnp.tril(jnp.ones((S, S), jnp.int32))[None, None, :, :], 'wq': jax.random.normal(ks[3], (D, D), jnp.float32) * std, 'bq': jax.random.normal(ks[4], (D,), jnp.float32) * std, 'wk': jax.random.normal(ks[5], (D, D), jnp.float32) * std, 'bk': jax.random.normal(ks[6], (D,), jnp.float32) * std, 'wv': jax.random.normal(ks[7], (D, D), jnp.float32) * std, 'bv': jax.random.normal(ks[8], (D,), jnp.float32) * std, 'wo': jax.random.normal(ks[9], (D, D), jnp.float32) * std, 'bo': jax.random.normal(ks[10], (D,), jnp.float32) * std}
        return inp
    _L1_xattn_all = _L1_xattn_setup()
    _L1_xattn_in = {k: v for k, v in _L1_xattn_all.items() if k in ('wq', 'bq', 'wk', 'bk', 'wv', 'bv', 'wo', 'bo')}
    del _L1_xattn_all

    def _L1_ffn_setup():
        import jax, jax.numpy as jnp
        import numpy as np
        B, M, D = (4, 256, 128)
        N, P = (64, 32)
        key = jax.random.key(seed)
        k1, k2, k3, k4 = jax.random.split(key, 4)
        x = jax.random.normal(k1, (B, M, D), dtype=jnp.float32)
        phi = jax.random.normal(k2, (D, N, P), dtype=jnp.float32) * (1.0 / np.sqrt(D))
        W = jax.random.normal(k3, (N, D, D), dtype=jnp.float32) * (1.0 / np.sqrt(D))
        b = jax.random.normal(k4, (N, D), dtype=jnp.float32) * 0.01
        return {'x': x, 'phi': phi, 'W': W, 'b': b}
    _L1_ffn_all = _L1_ffn_setup()
    _L1_ffn_in = {k: v for k, v in _L1_ffn_all.items() if k in ('phi', 'W', 'b')}
    del _L1_ffn_all

    def _L2_xattn_setup():
        import jax, jax.numpy as jnp
        import numpy as np
        DIM = 128
        NUM_HEADS = 16
        HEAD_DIM = DIM // NUM_HEADS
        SCALE = HEAD_DIM ** (-0.5)
        EPS = 1e-05

        def _layernorm(x, w, b):
            mu = jnp.mean(x, axis=-1, keepdims=True)
            var = jnp.mean(jnp.square(x - mu), axis=-1, keepdims=True)
            return (x - mu) * jax.lax.rsqrt(var + EPS) * w + b

        def _split_heads(x):
            B, L, _ = x.shape
            return x.reshape(B, L, NUM_HEADS, HEAD_DIM).transpose(0, 2, 1, 3)
        key = jax.random.key(seed)
        ks = jax.random.split(key, 12)
        B, Lq, Lk = (4, 64, 256)
        inp = {'query': jax.random.normal(ks[0], (B, Lq, DIM), jnp.float32), 'context': jax.random.normal(ks[1], (B, Lk, DIM), jnp.float32), 'context_mask': jax.random.randint(ks[2], (B, Lk), 0, 2).astype(bool), 'qn_w': jnp.ones((DIM,), jnp.float32), 'qn_b': jnp.zeros((DIM,), jnp.float32), 'cn_w': jnp.ones((DIM,), jnp.float32), 'cn_b': jnp.zeros((DIM,), jnp.float32)}
        std = DIM ** (-0.5)
        for i, name in enumerate(['q', 'k', 'v', 'o']):
            inp[f'W{name}'] = jax.random.normal(ks[3 + i], (DIM, DIM), jnp.float32) * std
            inp[f'b{name}'] = jnp.zeros((DIM,), jnp.float32)
        return inp
    _L2_xattn_all = _L2_xattn_setup()
    _L2_xattn_in = {k: v for k, v in _L2_xattn_all.items() if k in ('qn_w', 'qn_b', 'cn_w', 'cn_b', 'Wq', 'bq', 'Wk', 'bk', 'Wv', 'bv', 'Wo', 'bo')}
    del _L2_xattn_all

    def _L2_ffn_setup():
        import jax, jax.numpy as jnp
        import numpy as np
        D = 128
        LW = 16
        DEPTH = 8
        NN = 2 ** DEPTH - 1
        NL = 2 ** DEPTH
        B, S = (2, 128)

        def _fff(x, nw, nb, w1, b1, w2, b2, act):
            node = jnp.zeros(x.shape[:2], dtype=jnp.int32)
            for _ in range(DEPTH):
                logit = jnp.einsum('bsd,bsd->bs', x, nw[node]) + nb[node]
                node = 2 * node + 1 + (logit > 0).astype(jnp.int32)
            leaf = node - NN
            h = act(jnp.einsum('bsd,bsdl->bsl', x, w1[leaf]) + b1[leaf])
            return jnp.einsum('bsl,bsld->bsd', h, w2[leaf]) + b2[leaf]

        def _forward(x, q_nw, q_nb, q_w1, q_b1, q_w2, q_b2, k_nw, k_nb, k_w1, k_b1, k_w2, k_b2, v_nw, v_nb, v_w1, v_b1, v_w2, v_b2, f_nw, f_nb, f_w1, f_b1, f_w2, f_b2):
            mu = jnp.mean(x, -1, keepdims=True)
            sd = jnp.std(x, -1, ddof=1, keepdims=True)
            xn = (x - mu) / jnp.sqrt(sd + 1e-05)
            relu = jax.nn.relu
            q = _fff(xn, q_nw, q_nb, q_w1, q_b1, q_w2, q_b2, relu)
            k = _fff(xn, k_nw, k_nb, k_w1, k_b1, k_w2, k_b2, relu)
            v = _fff(xn, v_nw, v_nb, v_w1, v_b1, v_w2, v_b2, relu)
            att = jax.nn.softmax(jnp.einsum('bqd,bkd->bqk', q, k) / jnp.sqrt(jnp.float32(D)), axis=-1)
            y = xn + jnp.einsum('bqk,bkd->bqd', att, v)
            gelu = lambda t: jax.nn.gelu(t, approximate=False)
            return y + _fff(y, f_nw, f_nb, f_w1, f_b1, f_w2, f_b2, gelu)

        def _make_fff_params(key, scale_in, scale_leaf):
            ks = jax.random.split(key, 4)
            nw = jax.random.normal(ks[0], (NN, D), jnp.float32) * scale_in
            nb = jnp.zeros((NN,), jnp.float32)
            w1 = jax.random.normal(ks[1], (NL, D, LW), jnp.float32) * scale_in
            b1 = jax.random.normal(ks[2], (NL, LW), jnp.float32) * 0.01
            w2 = jax.random.normal(ks[3], (NL, LW, D), jnp.float32) * scale_leaf
            b2 = jnp.zeros((NL, D), jnp.float32)
            return (nw, nb, w1, b1, w2, b2)
        key = jax.random.key(seed)
        kx, kq, kk, kv, kf = jax.random.split(key, 5)
        s_in = 1.0 / np.sqrt(D)
        s_lf = 1.0 / np.sqrt(LW)
        inp = {'x': jax.random.normal(kx, (B, S, D), jnp.float32)}
        for name, kk_ in (('q', kq), ('k', kk), ('v', kv), ('f', kf)):
            nw, nb, w1, b1, w2, b2 = _make_fff_params(kk_, s_in, s_lf)
            inp.update({f'{name}_nw': nw, f'{name}_nb': nb, f'{name}_w1': w1, f'{name}_b1': b1, f'{name}_w2': w2, f'{name}_b2': b2})
        return inp
    _L2_ffn_all = _L2_ffn_setup()
    _L2_ffn_in = {k: v for k, v in _L2_ffn_all.items() if k in ('q_nw', 'q_nb', 'q_w1', 'q_b1', 'q_w2', 'q_b2', 'k_nw', 'k_nb', 'k_w1', 'k_b1', 'k_w2', 'k_b2', 'v_nw', 'v_nb', 'v_w1', 'v_b1', 'v_w2', 'v_b2', 'f_nw', 'f_nb', 'f_w1', 'f_b1', 'f_w2', 'f_b2')}
    del _L2_ffn_all

    def _L3_xattn_setup():
        import jax, jax.numpy as jnp
        import numpy as np
        D_MODEL = 128
        NUM_HEADS = 16
        D_K = D_MODEL // NUM_HEADS

        def _split_heads(x):
            B, S, _ = x.shape
            return x.reshape(B, S, NUM_HEADS, D_K).transpose(0, 2, 1, 3)
        key = jax.random.key(seed)
        ks = jax.random.split(key, 11)
        B, S = (2, 256)
        scale = 1.0 / np.sqrt(D_MODEL)
        inp = {'q': jax.random.normal(ks[0], (B, S, D_MODEL), jnp.float32), 'k': jax.random.normal(ks[1], (B, S, D_MODEL), jnp.float32), 'v': jax.random.normal(ks[2], (B, S, D_MODEL), jnp.float32), 'Wq': jax.random.normal(ks[3], (D_MODEL, D_MODEL), jnp.float32) * scale, 'bq': jnp.zeros((D_MODEL,), jnp.float32), 'Wk': jax.random.normal(ks[4], (D_MODEL, D_MODEL), jnp.float32) * scale, 'bk': jnp.zeros((D_MODEL,), jnp.float32), 'Wv': jax.random.normal(ks[5], (D_MODEL, D_MODEL), jnp.float32) * scale, 'bv': jnp.zeros((D_MODEL,), jnp.float32), 'Wo': jax.random.normal(ks[6], (D_MODEL, D_MODEL), jnp.float32) * scale, 'bo': jnp.zeros((D_MODEL,), jnp.float32)}
        return inp
    _L3_xattn_all = _L3_xattn_setup()
    _L3_xattn_in = {k: v for k, v in _L3_xattn_all.items() if k in ('Wq', 'bq', 'Wk', 'bk', 'Wv', 'bv', 'Wo', 'bo')}
    del _L3_xattn_all

    def _L3_ffn_setup():
        import jax, jax.numpy as jnp
        import numpy as np
        B, S, HID, DFF, E, K = (4, 256, 128, 512, 8, 256)
        key = jax.random.key(seed)
        ks = jax.random.split(key, 4)
        sc_h = 1.0 / np.sqrt(HID)
        sc_f = 1.0 / np.sqrt(DFF)
        return {'x': jax.random.normal(ks[0], (B, S, HID), jnp.float32), 'router_w': jax.random.normal(ks[1], (HID, E), jnp.float32) * sc_h, 'router_b': jnp.zeros((E,), jnp.float32), 'w1': jax.random.normal(ks[2], (E, HID, DFF), jnp.float32) * sc_h, 'b1': jnp.zeros((E, DFF), jnp.float32), 'w2': jax.random.normal(ks[3], (E, DFF, HID), jnp.float32) * sc_f, 'b2': jnp.zeros((E, HID), jnp.float32)}
    _L3_ffn_all = _L3_ffn_setup()
    _L3_ffn_in = {k: v for k, v in _L3_ffn_all.items() if k in ('router_w', 'router_b', 'w1', 'b1', 'w2', 'b2')}
    del _L3_ffn_all
    return {'x': x, 'ctx_1024': ctx_1024, 'itok_BxS2_0_99': itok_BxS2_0_99, 'mask_1x1xSxS2_ik0': mask_1x1xSxS2_ik0, 'mask_BxS2_bk0': mask_BxS2_bk0, 'L0_xattn_Wq': _L0_xattn_in['Wq'], 'L0_xattn_Wk': _L0_xattn_in['Wk'], 'L0_xattn_Wv': _L0_xattn_in['Wv'], 'L0_xattn_Wo': _L0_xattn_in['Wo'], 'L0_xattn_bo': _L0_xattn_in['bo'], 'L0_ffn_Wg': _L0_ffn_in['Wg'], 'L0_ffn_W11': _L0_ffn_in['W11'], 'L0_ffn_W12': _L0_ffn_in['W12'], 'L0_ffn_W2': _L0_ffn_in['W2'], 'L1_xattn_wq': _L1_xattn_in['wq'], 'L1_xattn_bq': _L1_xattn_in['bq'], 'L1_xattn_wk': _L1_xattn_in['wk'], 'L1_xattn_bk': _L1_xattn_in['bk'], 'L1_xattn_wv': _L1_xattn_in['wv'], 'L1_xattn_bv': _L1_xattn_in['bv'], 'L1_xattn_wo': _L1_xattn_in['wo'], 'L1_xattn_bo': _L1_xattn_in['bo'], 'L1_ffn_phi': _L1_ffn_in['phi'], 'L1_ffn_W': _L1_ffn_in['W'], 'L1_ffn_b': _L1_ffn_in['b'], 'L2_xattn_qn_w': _L2_xattn_in['qn_w'], 'L2_xattn_qn_b': _L2_xattn_in['qn_b'], 'L2_xattn_cn_w': _L2_xattn_in['cn_w'], 'L2_xattn_cn_b': _L2_xattn_in['cn_b'], 'L2_xattn_Wq': _L2_xattn_in['Wq'], 'L2_xattn_bq': _L2_xattn_in['bq'], 'L2_xattn_Wk': _L2_xattn_in['Wk'], 'L2_xattn_bk': _L2_xattn_in['bk'], 'L2_xattn_Wv': _L2_xattn_in['Wv'], 'L2_xattn_bv': _L2_xattn_in['bv'], 'L2_xattn_Wo': _L2_xattn_in['Wo'], 'L2_xattn_bo': _L2_xattn_in['bo'], 'L2_ffn_q_nw': _L2_ffn_in['q_nw'], 'L2_ffn_q_nb': _L2_ffn_in['q_nb'], 'L2_ffn_q_w1': _L2_ffn_in['q_w1'], 'L2_ffn_q_b1': _L2_ffn_in['q_b1'], 'L2_ffn_q_w2': _L2_ffn_in['q_w2'], 'L2_ffn_q_b2': _L2_ffn_in['q_b2'], 'L2_ffn_k_nw': _L2_ffn_in['k_nw'], 'L2_ffn_k_nb': _L2_ffn_in['k_nb'], 'L2_ffn_k_w1': _L2_ffn_in['k_w1'], 'L2_ffn_k_b1': _L2_ffn_in['k_b1'], 'L2_ffn_k_w2': _L2_ffn_in['k_w2'], 'L2_ffn_k_b2': _L2_ffn_in['k_b2'], 'L2_ffn_v_nw': _L2_ffn_in['v_nw'], 'L2_ffn_v_nb': _L2_ffn_in['v_nb'], 'L2_ffn_v_w1': _L2_ffn_in['v_w1'], 'L2_ffn_v_b1': _L2_ffn_in['v_b1'], 'L2_ffn_v_w2': _L2_ffn_in['v_w2'], 'L2_ffn_v_b2': _L2_ffn_in['v_b2'], 'L2_ffn_f_nw': _L2_ffn_in['f_nw'], 'L2_ffn_f_nb': _L2_ffn_in['f_nb'], 'L2_ffn_f_w1': _L2_ffn_in['f_w1'], 'L2_ffn_f_b1': _L2_ffn_in['f_b1'], 'L2_ffn_f_w2': _L2_ffn_in['f_w2'], 'L2_ffn_f_b2': _L2_ffn_in['f_b2'], 'L3_xattn_Wq': _L3_xattn_in['Wq'], 'L3_xattn_bq': _L3_xattn_in['bq'], 'L3_xattn_Wk': _L3_xattn_in['Wk'], 'L3_xattn_bk': _L3_xattn_in['bk'], 'L3_xattn_Wv': _L3_xattn_in['Wv'], 'L3_xattn_bv': _L3_xattn_in['bv'], 'L3_xattn_Wo': _L3_xattn_in['Wo'], 'L3_xattn_bo': _L3_xattn_in['bo'], 'L3_ffn_router_w': _L3_ffn_in['router_w'], 'L3_ffn_router_b': _L3_ffn_in['router_b'], 'L3_ffn_w1': _L3_ffn_in['w1'], 'L3_ffn_b1': _L3_ffn_in['b1'], 'L3_ffn_w2': _L3_ffn_in['w2'], 'L3_ffn_b2': _L3_ffn_in['b2']}

def reference(x, ctx_1024, itok_BxS2_0_99, mask_1x1xSxS2_ik0, mask_BxS2_bk0, L0_xattn_Wq, L0_xattn_Wk, L0_xattn_Wv, L0_xattn_Wo, L0_xattn_bo, L0_ffn_Wg, L0_ffn_W11, L0_ffn_W12, L0_ffn_W2, L1_xattn_wq, L1_xattn_bq, L1_xattn_wk, L1_xattn_bk, L1_xattn_wv, L1_xattn_bv, L1_xattn_wo, L1_xattn_bo, L1_ffn_phi, L1_ffn_W, L1_ffn_b, L2_xattn_qn_w, L2_xattn_qn_b, L2_xattn_cn_w, L2_xattn_cn_b, L2_xattn_Wq, L2_xattn_bq, L2_xattn_Wk, L2_xattn_bk, L2_xattn_Wv, L2_xattn_bv, L2_xattn_Wo, L2_xattn_bo, L2_ffn_q_nw, L2_ffn_q_nb, L2_ffn_q_w1, L2_ffn_q_b1, L2_ffn_q_w2, L2_ffn_q_b2, L2_ffn_k_nw, L2_ffn_k_nb, L2_ffn_k_w1, L2_ffn_k_b1, L2_ffn_k_w2, L2_ffn_k_b2, L2_ffn_v_nw, L2_ffn_v_nb, L2_ffn_v_w1, L2_ffn_v_b1, L2_ffn_v_w2, L2_ffn_v_b2, L2_ffn_f_nw, L2_ffn_f_nb, L2_ffn_f_w1, L2_ffn_f_b1, L2_ffn_f_w2, L2_ffn_f_b2, L3_xattn_Wq, L3_xattn_bq, L3_xattn_Wk, L3_xattn_bk, L3_xattn_Wv, L3_xattn_bv, L3_xattn_Wo, L3_xattn_bo, L3_ffn_router_w, L3_ffn_router_b, L3_ffn_w1, L3_ffn_b1, L3_ffn_w2, L3_ffn_b2):
    import jax
    import jax.numpy as jnp

    def _L0_xattn_ref(x, y, log_seqs, pad_id, Wq, Wk, Wv, Wo, bo):
        import jax, jax.numpy as jnp
        import numpy as np
        B, S, D = (4, 256, 128)
        H = 16
        HD = D // H
        NEG = -1000000000.0
        b = x.shape[0]
        q = (x @ Wq).reshape(b, -1, H, HD).transpose(0, 2, 1, 3)
        k = (y @ Wk).reshape(b, -1, H, HD).transpose(0, 2, 1, 3)
        v = (y @ Wv).reshape(b, -1, H, HD).transpose(0, 2, 1, 3)
        mask = (log_seqs == pad_id)[:, None, None, :]
        scores = jnp.einsum('bhqd,bhkd->bhqk', q, k)
        scores = jnp.where(mask, NEG, scores)
        probs = jax.nn.softmax(scores / np.sqrt(HD), axis=-1)
        attn = jnp.einsum('bhqk,bhkd->bhqd', probs, v)
        attn = attn.transpose(0, 2, 1, 3).reshape(b, -1, H * HD)
        return attn @ Wo + bo

    def _L0_ffn_ref(x, Wg, W11, W12, W2):
        import jax, jax.numpy as jnp
        import numpy as np
        B, S, H, I, E, K = (2, 256, 128, 256, 8, 2)
        gate_scores = jax.nn.softmax(x @ Wg, axis=-1)
        topk_scores, topk_idx = jax.lax.top_k(gate_scores, K)
        topk_scores = topk_scores / (topk_scores.sum(-1, keepdims=True) + 1e-08)
        gate = jnp.einsum('bsh,ehi->bsei', x, W11)
        value = jnp.einsum('bsh,ehi->bsei', x, W12)
        fused = gate * jax.nn.sigmoid(gate) * value
        expert_out = jnp.einsum('bsei,eih->bseh', fused, W2)
        gathered = jnp.take_along_axis(expert_out, topk_idx[..., None], axis=2)
        out = jnp.sum(topk_scores[..., None] * gathered, axis=2)
        return out

    def _L1_xattn_ref(q, k, v, mask, wq, bq, wk, bk, wv, bv, wo, bo):
        import jax, jax.numpy as jnp
        import numpy as np
        import math
        B, S, D, H = (2, 256, 128, 16)
        DK = D // H

        def _split_heads(x):
            b, s, _ = x.shape
            return x.reshape(b, s, H, DK).transpose(0, 2, 1, 3)
        query = _split_heads(q @ wq.T + bq)
        key_h = _split_heads(k @ wk.T + bk)
        value = _split_heads(v @ wv.T + bv)
        scale = 1.0 / math.sqrt(DK)
        scores = jnp.einsum('bhqd,bhkd->bhqk', query, key_h) * scale
        scores = jnp.where(mask == 0, jnp.float32(-1000000000.0), scores)
        attn = jax.nn.softmax(scores, axis=-1)
        x = jnp.einsum('bhqk,bhkd->bhqd', attn, value)
        x = x.transpose(0, 2, 1, 3).reshape(q.shape[0], -1, H * DK)
        return x @ wo.T + bo

    def _L1_ffn_ref(x, phi, W, b):
        import jax, jax.numpy as jnp
        import numpy as np
        B, M, D = (4, 256, 128)
        N, P = (64, 32)
        logits = jnp.einsum('bmd,dnp->bmnp', x, phi)
        dispatch = jax.nn.softmax(logits, axis=0)
        bsz, m, n, p = logits.shape
        combine = jax.nn.softmax(logits.reshape(bsz, m, n * p), axis=-1).reshape(bsz, m, n, p)
        slots = jnp.einsum('bmd,bmnp->bnpd', x, dispatch)
        y = jnp.einsum('bnpd,nde->bnpe', slots, W) + b[None, :, None, :]
        out = jnp.einsum('bnpd,bmnp->bmd', y, combine)
        return out

    def _L2_xattn_ref(query, context, context_mask, qn_w, qn_b, cn_w, cn_b, Wq, bq, Wk, bk, Wv, bv, Wo, bo):
        import jax, jax.numpy as jnp
        import numpy as np
        DIM = 128
        NUM_HEADS = 16
        HEAD_DIM = DIM // NUM_HEADS
        SCALE = HEAD_DIM ** (-0.5)
        EPS = 1e-05

        def _layernorm(x, w, b):
            mu = jnp.mean(x, axis=-1, keepdims=True)
            var = jnp.mean(jnp.square(x - mu), axis=-1, keepdims=True)
            return (x - mu) * jax.lax.rsqrt(var + EPS) * w + b

        def _split_heads(x):
            B, L, _ = x.shape
            return x.reshape(B, L, NUM_HEADS, HEAD_DIM).transpose(0, 2, 1, 3)
        B, Lq, _ = query.shape
        fully_masked = jnp.all(context_mask, axis=1)
        mask = context_mask.at[:, 0].set(jnp.where(fully_masked, False, context_mask[:, 0]))
        qn = _layernorm(query, qn_w, qn_b)
        cn = _layernorm(context, cn_w, cn_b)
        q = _split_heads(qn @ Wq.T + bq)
        k = _split_heads(cn @ Wk.T + bk)
        v = _split_heads(cn @ Wv.T + bv)
        logits = jnp.einsum('bhqd,bhkd->bhqk', q * SCALE, k)
        logits = jnp.where(mask[:, None, None, :], -jnp.inf, logits)
        attn = jax.nn.softmax(logits, axis=-1)
        out = jnp.einsum('bhqk,bhkd->bhqd', attn, v)
        out = out.transpose(0, 2, 1, 3).reshape(B, Lq, DIM)
        return out @ Wo.T + bo

    def _L2_ffn_ref(x, q_nw, q_nb, q_w1, q_b1, q_w2, q_b2, k_nw, k_nb, k_w1, k_b1, k_w2, k_b2, v_nw, v_nb, v_w1, v_b1, v_w2, v_b2, f_nw, f_nb, f_w1, f_b1, f_w2, f_b2):
        import jax, jax.numpy as jnp
        import numpy as np
        D = 128
        LW = 16
        DEPTH = 8
        NN = 2 ** DEPTH - 1
        NL = 2 ** DEPTH
        B, S = (2, 128)

        def _fff(x, nw, nb, w1, b1, w2, b2, act):
            node = jnp.zeros(x.shape[:2], dtype=jnp.int32)
            for _ in range(DEPTH):
                logit = jnp.einsum('bsd,bsd->bs', x, nw[node]) + nb[node]
                node = 2 * node + 1 + (logit > 0).astype(jnp.int32)
            leaf = node - NN
            h = act(jnp.einsum('bsd,bsdl->bsl', x, w1[leaf]) + b1[leaf])
            return jnp.einsum('bsl,bsld->bsd', h, w2[leaf]) + b2[leaf]

        def _forward(x, q_nw, q_nb, q_w1, q_b1, q_w2, q_b2, k_nw, k_nb, k_w1, k_b1, k_w2, k_b2, v_nw, v_nb, v_w1, v_b1, v_w2, v_b2, f_nw, f_nb, f_w1, f_b1, f_w2, f_b2):
            mu = jnp.mean(x, -1, keepdims=True)
            sd = jnp.std(x, -1, ddof=1, keepdims=True)
            xn = (x - mu) / jnp.sqrt(sd + 1e-05)
            relu = jax.nn.relu
            q = _fff(xn, q_nw, q_nb, q_w1, q_b1, q_w2, q_b2, relu)
            k = _fff(xn, k_nw, k_nb, k_w1, k_b1, k_w2, k_b2, relu)
            v = _fff(xn, v_nw, v_nb, v_w1, v_b1, v_w2, v_b2, relu)
            att = jax.nn.softmax(jnp.einsum('bqd,bkd->bqk', q, k) / jnp.sqrt(jnp.float32(D)), axis=-1)
            y = xn + jnp.einsum('bqk,bkd->bqd', att, v)
            gelu = lambda t: jax.nn.gelu(t, approximate=False)
            return y + _fff(y, f_nw, f_nb, f_w1, f_b1, f_w2, f_b2, gelu)

        def _make_fff_params(key, scale_in, scale_leaf):
            ks = jax.random.split(key, 4)
            nw = jax.random.normal(ks[0], (NN, D), jnp.float32) * scale_in
            nb = jnp.zeros((NN,), jnp.float32)
            w1 = jax.random.normal(ks[1], (NL, D, LW), jnp.float32) * scale_in
            b1 = jax.random.normal(ks[2], (NL, LW), jnp.float32) * 0.01
            w2 = jax.random.normal(ks[3], (NL, LW, D), jnp.float32) * scale_leaf
            b2 = jnp.zeros((NL, D), jnp.float32)
            return (nw, nb, w1, b1, w2, b2)
        return _forward(x, q_nw, q_nb, q_w1, q_b1, q_w2, q_b2, k_nw, k_nb, k_w1, k_b1, k_w2, k_b2, v_nw, v_nb, v_w1, v_b1, v_w2, v_b2, f_nw, f_nb, f_w1, f_b1, f_w2, f_b2)

    def _L3_xattn_ref(q, k, v, Wq, bq, Wk, bk, Wv, bv, Wo, bo):
        import jax, jax.numpy as jnp
        import numpy as np
        D_MODEL = 128
        NUM_HEADS = 16
        D_K = D_MODEL // NUM_HEADS

        def _split_heads(x):
            B, S, _ = x.shape
            return x.reshape(B, S, NUM_HEADS, D_K).transpose(0, 2, 1, 3)
        Q = _split_heads(q @ Wq.T + bq)
        K = _split_heads(k @ Wk.T + bk)
        V = _split_heads(v @ Wv.T + bv)
        scores = jnp.einsum('bhqd,bhkd->bhqk', Q, K) / jnp.sqrt(jnp.float32(D_K))
        attn = jax.nn.softmax(scores, axis=-1)
        ctx = jnp.einsum('bhqk,bhkd->bhqd', attn, V)
        B, H, S, dk = ctx.shape
        ctx = ctx.transpose(0, 2, 1, 3).reshape(B, S, D_MODEL)
        return ctx @ Wo.T + bo

    def _L3_ffn_ref(x, router_w, router_b, w1, b1, w2, b2):
        import jax, jax.numpy as jnp
        import numpy as np
        B, S, HID, DFF, E, K = (4, 256, 128, 512, 8, 256)
        b, s, h = x.shape
        xf = x.reshape(-1, h)
        logits = xf @ router_w + router_b
        scores = jax.nn.softmax(logits, axis=-1)
        G, idx = jax.lax.top_k(scores.T, K)
        toks = xf[idx]
        h1 = jax.nn.relu(jnp.einsum('ekh,ehf->ekf', toks, w1) + b1[:, None, :])
        eo = jnp.einsum('ekf,efh->ekh', h1, w2) + b2[:, None, :]
        contrib = (eo * G[..., None]).reshape(-1, h)
        y = jnp.zeros_like(xf).at[idx.reshape(-1)].add(contrib)
        return y.reshape(b, s, h)
    x = x + _L0_xattn_ref(_layernorm(x, axis=-1), ctx_1024, itok_BxS2_0_99, 0, L0_xattn_Wq, L0_xattn_Wk, L0_xattn_Wv, L0_xattn_Wo, L0_xattn_bo)
    x = x + _L0_ffn_ref(_layernorm(x, axis=-1), L0_ffn_Wg, L0_ffn_W11, L0_ffn_W12, L0_ffn_W2)
    x = x + _L1_xattn_ref(_layernorm(x, axis=-1), ctx_1024, ctx_1024, mask_1x1xSxS2_ik0, L1_xattn_wq, L1_xattn_bq, L1_xattn_wk, L1_xattn_bk, L1_xattn_wv, L1_xattn_bv, L1_xattn_wo, L1_xattn_bo)
    x = x + _L1_ffn_ref(_layernorm(x, axis=-1), L1_ffn_phi, L1_ffn_W, L1_ffn_b)
    x = x + _L2_xattn_ref(_layernorm(x, axis=-1), ctx_1024, mask_BxS2_bk0, L2_xattn_qn_w, L2_xattn_qn_b, L2_xattn_cn_w, L2_xattn_cn_b, L2_xattn_Wq, L2_xattn_bq, L2_xattn_Wk, L2_xattn_bk, L2_xattn_Wv, L2_xattn_bv, L2_xattn_Wo, L2_xattn_bo)
    x = x + _L2_ffn_ref(_layernorm(x, axis=-1), L2_ffn_q_nw, L2_ffn_q_nb, L2_ffn_q_w1, L2_ffn_q_b1, L2_ffn_q_w2, L2_ffn_q_b2, L2_ffn_k_nw, L2_ffn_k_nb, L2_ffn_k_w1, L2_ffn_k_b1, L2_ffn_k_w2, L2_ffn_k_b2, L2_ffn_v_nw, L2_ffn_v_nb, L2_ffn_v_w1, L2_ffn_v_b1, L2_ffn_v_w2, L2_ffn_v_b2, L2_ffn_f_nw, L2_ffn_f_nb, L2_ffn_f_w1, L2_ffn_f_b1, L2_ffn_f_w2, L2_ffn_f_b2)
    x = x + _L3_xattn_ref(_layernorm(x, axis=-1), ctx_1024, ctx_1024, L3_xattn_Wq, L3_xattn_bq, L3_xattn_Wk, L3_xattn_bk, L3_xattn_Wv, L3_xattn_bv, L3_xattn_Wo, L3_xattn_bo)
    x = x + _L3_ffn_ref(_layernorm(x, axis=-1), L3_ffn_router_w, L3_ffn_router_b, L3_ffn_w1, L3_ffn_b1, L3_ffn_w2, L3_ffn_b2)
    return x

_drawn_inputs = setup_inputs


def setup_inputs(seed=0):
    import zlib

    import numpy as np

    out = dict(_drawn_inputs(seed))
    spreads = {'L0_xattn_bo': (0.0, 0.1),
     'L2_xattn_qn_w': (1.0, 0.2),
     'L2_xattn_qn_b': (0.0, 0.1),
     'L2_xattn_cn_w': (1.0, 0.2),
     'L2_xattn_cn_b': (0.0, 0.1),
     'L2_xattn_bq': (0.0, 0.1),
     'L2_xattn_bk': (0.0, 2.0),
     'L2_xattn_bv': (0.0, 0.1),
     'L2_xattn_bo': (0.0, 0.1),
     'L2_ffn_q_nb': (0.0, 0.1),
     'L2_ffn_q_b2': (0.0, 0.332),
     'L2_ffn_k_nb': (0.0, 0.1),
     'L2_ffn_k_b2': (0.0, 0.339),
     'L2_ffn_v_nb': (0.0, 0.1),
     'L2_ffn_v_b2': (0.0, 0.1),
     'L2_ffn_f_nb': (0.0, 0.1),
     'L2_ffn_f_b2': (0.0, 0.1),
     'L3_xattn_bq': (0.0, 0.8),
     'L3_xattn_bk': (0.0, 2.0),
     'L3_xattn_bv': (0.0, 0.317),
     'L3_xattn_bo': (0.0, 0.27),
     'L3_ffn_router_b': (0.0, 0.8),
     'L3_ffn_b1': (0.0, 0.8),
     'L3_ffn_b2': (0.0, 0.8)}
    factors = {'L1_xattn_bk': 64.0,
     'L1_ffn_b': 3.868,
     'L2_ffn_q_b1': 25.682,
     'L2_ffn_k_b1': 31.723,
     'L2_ffn_v_b1': 3.263,
     'L2_ffn_f_b1': 22.836}
    for name, (base, spread) in spreads.items():
        noise = np.random.default_rng([zlib.crc32(name.encode()), seed]).standard_normal(out[name].shape)
        drawn = base * np.exp(spread * noise) if base else spread * noise
        out[name] = jnp.asarray(drawn.astype(out[name].dtype))
    for name, factor in factors.items():
        out[name] = (out[name] * factor).astype(out[name].dtype)
    return out
```

```python
from contextlib import ExitStack

import numpy as np

import concourse.bass as bass
from concourse import mybir

ALU = mybir.AluOpType
ACT = mybir.ActivationFunctionType
AX = mybir.AxisListType
F32 = mybir.dt.float32
BF16 = mybir.dt.bfloat16
I32 = mybir.dt.int32
U8 = mybir.dt.uint8
ds = bass.ds

P = 128
B = 16
SQ = 256
QT = SQ // P
NT = B * QT
SK = 64
NH = 16
HD = P // NH
NG = 4
HG = NH // NG
ARENA = 33300
LN_EPS = 1e-5
MASKED = -1e30
PLAN = ["X0", "F0", "X1", "F1", "X2", "F2", "X3", "F3"]

COLS = ["L1_bq", "L1_bk", "L2_bq", "L2_bk", "L3_bq", "L3_bk", "qn_w", "qn_b", "cn_w", "cn_b"]
ROWS = ["L0_bo", "L1_bv", "L1_bo", "L2_bv", "L2_bo", "L3_bv", "L3_bo"]


class Count:

    def __init__(self, sem, base=0):
        self.sem, self.n = sem, base

    def inc(self, instruction):
        self.n = self.n + 1
        return instruction.then_inc(self.sem, 1)

    def wait(self, eng):
        eng.wait_ge(self.sem, self.n)


def wait(eng, sem, value):
    if not isinstance(value, int) or value > 0:
        eng.wait_ge(sem, value)


def piped(eng, front, back):
    front(0, 0)
    with eng.Fori(0, B // 2 - 1) as j:
        front(j * 2 + 1, 1)
        back(j * 2, 0)
        front(j * 2 + 2, 0)
        back(j * 2 + 1, 1)
    front(B - 1, 1)
    back(B - 2, 0)
    back(B - 1, 1)


def build(nc, A):
    ctx = ExitStack()
    with ctx:
        def sb(name, shape, dt=F32):
            return ctx.enter_context(nc.sbuf_tensor(name, shape, dt))

        def sem(name):
            return ctx.enter_context(nc.semaphore(name))

        x = sb("x", [P, NT, P])
        xc = sb("xc", [P, NT, P])
        wide = sb("wide", [P, NT, P])
        ident = sb("ident", [P, P])
        identb = sb("identb", [P, P], BF16)
        headmask = sb("headmask", [P, HG])
        row0 = sb("row0", [P, P], BF16)
        onesf = sb("onesf", [P, P])
        ctxT = sb("ctxT", [P, B, 2, SK])
        cols = sb("cols", [P, len(COLS)])
        rows = sb("rows", [P, len(ROWS), P])
        wx = sb("wx", [P, 4, 4, P])
        stat = sb("stat", [P, 8, NT])
        bias0 = sb("bias0", [P, B, SK], BF16)
        bias2 = sb("bias2", [P, B, SK], BF16)
        bias1 = sb("bias1", [P, QT, SK], BF16)
        keep0 = sb("keep0", [P, B])
        keep1 = sb("keep1", [P, QT * P])

        zeros = sb("zeros", [P, 4 * (P + 8)])
        arena = sb("arena", [P, ARENA])

        class Carve:

            def __init__(self, at=0):
                self.at = at

            def __call__(self, *shape, dt=F32):
                n = 1
                for d in shape:
                    n *= d
                words = n if dt in (F32, I32) else (n + 1) // 2
                v = arena[:, self.at:self.at + words]
                self.at += words
                assert self.at <= ARENA, self.at
                if dt != F32:
                    v = v.bitcast(dt)
                names = "abcdef"[:len(shape)]
                if len(shape) > 1:
                    v = v.rearrange(f"p ({' '.join(names)}) -> p {' '.join(names)}",
                                    **{c: d for c, d in zip(names, shape)})
                return v

        carve = Carve()
        kT = carve(B, SK)
        kblk = carve(2, HG, SK)
        v2 = carve(B, NH // 2, 2 * (HD + 1))
        xn = carve(2, QT, P)
        xnT = carve(2, SQ)
        qT = carve(2, SQ)
        prob = carve(2, NG, QT * HG * SK)
        pT = carve(2, 4 * P)
        mx = carve(2, NG * QT * HG)
        rs = carve(2, QT * NH)
        on = carve(2, QT, P)
        oT = carve(2, SQ)
        cx = carve(B * SK // P, P)
        cnT = carve(B, 2, SK)
        stat_c = carve(6, 8)

        bank = ctx.enter_context(nc.psum_tensor("bank", [P, 8, 512], F32))

        def col(name):
            n = COLS.index(name)
            return cols[:, n:n + 1]

        def row(name):
            return rows[:, ROWS.index(name), :]

        loaded = sem("loaded")
        LOADS = 10
        stored = sem("stored")
        x_done = sem("x_done")
        cast = sem("cast")
        masks = sem("masks")
        masks_ps = sem("masks_ps")
        SEMS = {}

        SHARED = {("F3", w): ("F0", v) for w, v in
                  dict(loaded=80, xn=B, flip_ps=B, flip=B, router=1, up=128, x_add=64, down=128, less_max=1,
                       exp=1).items()}
        SHARED.update({("F2", w): ("F1", v) for w, v in dict(xn=1, flip_ps=8, flip=8, x_add=NT, exp=4 * NT).items()})

        def at(layer, what):
            first, left = SHARED.get((layer, what), (None, 0))
            return left if first in PLAN else 0

        def S(layer, what):
            layer = SHARED.get((layer, what), (layer, 0))[0]
            name = f"{layer}_{what}"
            if name not in SEMS:
                SEMS[name] = sem(name)
            return SEMS[name]

        NORMS = [t for p in PLAN for t in (["X2c", "X2", "X2q"] if p == "X2" else [p])]

        def norm_stats_dve(tag, src, dst, squares, st, tiles):
            dve = nc.vector
            k = NORMS.index(tag)
            c = Count(S("norm", "ln"), 3 * k)
            c.inc(dve.tensor_reduce(st[:, 0, 0:tiles], src[:, :, :], AX.X, ALU.add))
            c.wait(dve)
            c.inc(dve.tensor_scalar(st[:, 1, 0:tiles], st[:, 0, 0:tiles], -1.0 / P, None, ALU.mult))
            c.wait(dve)
            dve.tensor_tensor(dst[:, :, :], src[:, :, :],
                              st[:, 1, 0:tiles].unsqueeze(2).to_broadcast([P, tiles, P]),
                              ALU.add).then_inc(S("norm", "centred"), 1)
            dve.wait_ge(S("norm", "squares"), k + 1)
            c.inc(dve.tensor_reduce(st[:, 2, 0:tiles], squares[:, :, :], AX.X, ALU.add))
            c.wait(dve)
            dve.tensor_scalar(st[:, 4, 0:tiles], st[:, 2, 0:tiles], 1.0 / P, LN_EPS, ALU.mult,
                              ALU.add).then_inc(S("norm", "var"), 1)
            dve.wait_ge(S("norm", "sd"), k + 1)
            dve.reciprocal(st[:, 3, 0:tiles], st[:, 5, 0:tiles]).then_inc(S("norm", "rstd"), 1)

        def norm_stats_act(tag, dst, squares, st, tiles):
            act = nc.scalar
            k = NORMS.index(tag)
            act.wait_ge(S("norm", "centred"), k + 1)
            act.activation(squares[:, :, :], dst[:, :, :], ACT.Square).then_inc(S("norm", "squares"), 1)
            act.wait_ge(S("norm", "var"), k + 1)
            act.activation(st[:, 5, 0:tiles], st[:, 4, 0:tiles], ACT.Sqrt).then_inc(S("norm", "sd"), 1)

        class Attn:
            def __init__(self, layer):
                self.layer = layer
                self.tag = f"X{layer}"
                self.scale = float(HD) ** -0.5
                self.masked = layer != 3
                self.turn = [p for p in PLAN if p[0] == "X"].index(self.tag)

            def at(self, what):
                return self.turn * PER_LAYER.get(what, 0)

        PER_LAYER = {"k_ps": 1, "v_ps": 1, "v2_zero": 1, "bo": 1, "kT": 3, "v2": 10, "xn": B, "xnT": B, "xnT_ps": B,
                     "q_ps": B, "qT": B, "kblk": B, "exp": B, "rs": B, "on": B, "oT": B, "x_add": B, "dve": 2 * B,
                     "scores": 2 * B, "sub": 2 * B, "pT": 4 * B, "values": 4 * B, "ring_ps": 6 * B}

        def s(a, what):
            return S("X", what)

        def attn_pe(a, before):
            pe = nc.tensor
            L = a.layer
            cT = ctxT
            pe.wait_ge(x_done, before)
            if L == 2:
                pe.wait_ge(s(a, "cn"), a.at("cn") + 1)
                for t in range(B * SK // P):
                    m = pe.transpose(bank[:, 3 + t // 4, (t % 4) * P:(t % 4 + 1) * P], wide[:, t, :], ident[:, :])
                m.then_inc(s(a, "cnT_ps"), 1)
                pe.wait_ge(s(a, "cnT"), a.at("cnT") + 4)
                cT = cnT
            for h in range(2):
                m = pe.matmul(bank[:, 1 + h, :], wx[:, L, 1, :], cT[:, 8 * h:8 * h + 8, 0, :],
                              start=True, stop=True)
            m.then_inc(s(a, "k_ps"), 1)
            for b in range(B):
                lhs = cT[:, b, :, :].rearrange("p c k -> p (c k)")
                m = pe.matmul(bank[:, 3 + b // 4, (b % 4) * P:(b % 4 + 1) * P], lhs, wx[:, L, 2, :],
                              start=True, stop=True)
            m.then_inc(s(a, "v_ps"), 1)

            pe.wait_ge(s(a, "v2"), a.at("v2") + 10)

            def front(i, u):
                pe.wait_ge(s(a, "xn"), a.at("xn") + i + 1)
                wait(pe, s(a, "qT"), a.at("qT") + i)
                for t in range(QT):
                    m = pe.transpose(bank[:, 0, t * P:(t + 1) * P], xn[:, u, t, :], ident[:, :])
                m.then_inc(s(a, "xnT_ps"), 1)
                pe.wait_ge(s(a, "xnT"), a.at("xnT") + i + 1)
                pe.matmul(bank[:, 0, SQ:2 * SQ], wx[:, L, 0, :], xnT[:, u, :],
                          start=True, stop=True).then_inc(s(a, "q_ps"), 1)
                pe.wait_ge(s(a, "qT"), a.at("qT") + i + 1)
                pe.wait_ge(s(a, "kblk"), a.at("kblk") + i + 1)
                for g in range(NG if a.masked else 0):
                    if g % 2 == 0:
                        wait(pe, s(a, "sub"), a.at("sub") + i * 2 + g // 2 - 1)
                    if L == 1:
                        for t in range(QT):
                            pe.matmul(bank[:, 1 + g, t * SQ:(t + 1) * SQ], identb[:, :],
                                      bias1[:, t, :].unsqueeze(1).to_broadcast([P, HG, SK]),
                                      start=(t == 0), stop=False, skip_group_check=True)
                    else:
                        bias = (bias0 if L == 0 else bias2)[:, ds(i, 1), :]
                        pe.matmul(bank[:, 1 + g, :], row0[:, :], bias.to_broadcast([P, QT * HG, SK]),
                                  start=True, stop=False, skip_group_check=True)
                for half in range(2):
                    wait(pe, s(a, "sub"), a.at("sub") + i * 2 + half - 1)
                    for g in (2 * half, 2 * half + 1):
                        for t in range(QT):
                            o = bank[:, 1 + g, t * SQ:(t + 1) * SQ]
                            m = pe.matmul(o, qT[32 * g:32 * g + 32, u, t * P:(t + 1) * P],
                                          kblk[32 * g:32 * g + 32, u, :, :].rearrange("p j k -> p (j k)"),
                                          start=(not a.masked), stop=True, skip_group_check=True)
                    m.then_inc(s(a, "scores"), 1)

            def back(i, u):
                pe.wait_ge(s(a, "exp"), a.at("exp") + i + 1)

                def lot(n):
                    t, r = n // 2, n % 2
                    if n == 0:
                        wait(pe, s(a, "oT"), a.at("oT") + i)
                    elif n == 1:
                        wait(pe, s(a, "x_add"), a.at("x_add") + i)
                    else:
                        pe.wait_ge(s(a, "pT"), a.at("pT") + i * 4 + n - 1)
                    for q in range(4):
                        p = 4 * r + q
                        g, jp = p // 2, p % 2
                        src = prob[:, u, g, (t * 2 + jp) * P:(t * 2 + jp + 1) * P]
                        m = pe.transpose(bank[:, 5 + n % 2, q * P:(q + 1) * P], src, ident[:, :])
                    m.then_inc(s(a, "ring_ps"), 1)

                def values(n):
                    t, r = n // 2, n % 2
                    pe.wait_ge(s(a, "pT"), a.at("pT") + i * 4 + n + 1)
                    if n == 0:
                        wait(pe, s(a, "on"), a.at("on") + i)
                    for q in range(4):
                        p = 4 * r + q
                        c0 = (t * (NH // 2) + p) * 18
                        m = pe.matmul(bank[:, 7, c0:c0 + 18], pT[:, n % 2, q * P:(q + 1) * P],
                                      v2[:, ds(i, 1), p, :].rearrange("p o c -> p (o c)"), start=True, stop=True,
                                      skip_group_check=True)
                    m.then_inc(s(a, "values"), 1)

                lot(0)
                for n in range(1, 4):
                    lot(n)
                    values(n - 1)
                values(3)
                pe.wait_ge(s(a, "on"), a.at("on") + i + 1)
                for t in range(QT):
                    m = pe.transpose(bank[:, 5, t * P:(t + 1) * P], on[:, u, t, :], ident[:, :])
                m.then_inc(s(a, "ring_ps"), 1)
                pe.wait_ge(s(a, "oT"), a.at("oT") + i + 1)
                for t in range(QT):
                    m = pe.matmul(bank[:, 6, t * P:(t + 1) * P], oT[:, u, t * P:(t + 1) * P], wx[:, L, 3, :],
                                  start=True, stop=True)
                m.then_inc(s(a, "ring_ps"), 1)

            piped(pe, front, back)

        def attn_dve(a, before):
            dve = nc.vector
            dve.wait_ge(x_done, before)
            L = a.layer
            if L == 2:
                dve.wait_ge(s(a, "cx"), a.at("cx") + 16)
                norm_stats_dve("X2c", cx, cc, csq, stat_c, B * SK // P)
                dve.wait_ge(S("norm", "rstd"), NORMS.index("X2c") + 1)
                dve.tensor_tensor(wide[:, 0:B * SK // P, :], cc[:, :, :],
                                  stat_c[:, 3, 0:8].unsqueeze(2).to_broadcast([P, 8, P]), ALU.mult).then_inc(s(a, "cn"), 1)
                dve.wait_ge(s(a, "cnT_ps"), a.at("cnT_ps") + 1)
                for h in range(2):
                    for c in range(2):
                        dve.tensor_scalar(cnT[:, 8 * h:8 * h + 8, c, :],
                                          bank[:, 3 + h, :].rearrange("p (b k) -> p b k", b=8),
                                          col("cn_w"), col("cn_b"), ALU.mult, ALU.add).then_inc(s(a, "cnT"), 1)
            norm_stats_dve(a.tag, x, xc, wide, stat, NT)
            if L == 2:
                dve.wait_ge(S("norm", "rstd"), NORMS.index(a.tag) + 1)
                dve.tensor_tensor(wide[:, :, :], xc[:, :, :],
                                  stat[:, 3, :].unsqueeze(2).to_broadcast([P, NT, P]), ALU.mult).then_inc(s(a, "again"), 1)
                dve.wait_ge(s(a, "again"), a.at("again") + 1)
                norm_stats_dve("X2q", wide, xc, wide, stat, NT)
            dve.wait_ge(s(a, "v_ps"), a.at("v_ps") + 1)
            dve.wait_ge(s(a, "v2_zero"), a.at("v2_zero") + 1)
            dve.memset(v2[0:64, :, :, HD:HD + 1], 1.0).then_inc(s(a, "v2"), 1)
            dve.memset(v2[64:128, :, :, 2 * HD + 1:2 * HD + 2], 1.0).then_inc(s(a, "v2"), 1)
            for q in range(4):
                for h in range(2):
                    src = bank[64 * h:64 * h + 64, 3 + q, :].rearrange("k (b p h d) -> k b p h d", b=4, p=8, h=2)[:, :, :, h, :]
                    dst = v2[64 * h:64 * h + 64, 4 * q:4 * q + 4, :, 9 * h:9 * h + 8]
                    if L == 0:
                        dve.tensor_copy(dst, src).then_inc(s(a, "v2"), 1)
                    else:
                        bv = row(f"L{L}_bv")[64 * h:64 * h + 64, :].rearrange("k (p h d) -> k p h d", p=8, h=2)[:, :, h, :]
                        dve.tensor_tensor(dst, src, bv.unsqueeze(1).to_broadcast([64, 4, 8, 8]),
                                          ALU.add).then_inc(s(a, "v2"), 1)
            if L == 0:
                dve.wait_ge(s(a, "kT"), a.at("kT") + 2)
                dve.tensor_tensor(kT[:, :, :], kT[:, :, :], keep0[:, :].unsqueeze(2).to_broadcast([P, B, SK]),
                                  ALU.mult).then_inc(s(a, "kT"), 1)

            def front(i, u):
                dve.wait_ge(s(a, "xnT_ps"), a.at("xnT_ps") + i + 1)
                if L == 2:
                    dve.tensor_scalar(xnT[:, u, :], bank[:, 0, 0:SQ], col("qn_w"), col("qn_b"), ALU.mult,
                                      ALU.add).then_inc(s(a, "xnT"), 1)
                else:
                    dve.tensor_copy(xnT[:, u, :], bank[:, 0, 0:SQ]).then_inc(s(a, "xnT"), 1)
                if L == 1:
                    dve.wait_ge(s(a, "q_ps"), a.at("q_ps") + i + 1)
                    dve.scalar_tensor_tensor(qT[:, u, :], bank[:, 0, SQ:2 * SQ], col("L1_bq"), keep1[:, :],
                                             ALU.add, ALU.mult).then_inc(s(a, "qT"), 1)
                c = Count(s(a, "dve"), a.at("dve") + i * 2)
                for half in range(2):
                    sc = bank[:, 1 + 2 * half:3 + 2 * half, :].rearrange("q g (h k) -> q (g h) k", k=SK)
                    m = mx[:, u, 16 * half:16 * half + 16]
                    dve.wait_ge(s(a, "scores"), a.at("scores") + i * 2 + half + 1)
                    c.inc(dve.tensor_reduce(m, sc, AX.X, ALU.max))
                    c.wait(dve)
                    dve.tensor_tensor(prob[:, u, 2 * half:2 * half + 2, :].rearrange("q g (h k) -> q (g h) k", k=SK), sc,
                                      m.unsqueeze(2).to_broadcast([P, 16, SK]), ALU.subtract).then_inc(s(a, "sub"), 1)

            def back(i, u):
                dve.wait_ge(s(a, "values"), a.at("values") + i * 4 + 4)
                o = bank[:, 7, 0:QT * 8 * 18].rearrange("q (h c) -> q h c", c=HD + 1)
                dve.reciprocal(rs[:, u, :], o[:, :, HD]).then_inc(s(a, "rs"), 1)
                dve.wait_ge(s(a, "rs"), a.at("rs") + i + 1)
                dve.tensor_tensor(on[:, u, :, :].rearrange("q t (h d) -> q (t h) d", d=HD), o[:, :, 0:HD],
                                  rs[:, u, :].unsqueeze(2).to_broadcast([P, QT * NH, HD]), ALU.mult).then_inc(s(a, "on"), 1)
                dve.wait_ge(s(a, "ring_ps"), a.at("ring_ps") + i * 6 + 5)
                dve.tensor_copy(oT[:, u, :], bank[:, 5, 0:SQ]).then_inc(s(a, "oT"), 1)
                dve.wait_ge(s(a, "ring_ps"), a.at("ring_ps") + i * 6 + 6)
                dve.wait_ge(s(a, "bo"), a.at("bo") + 1)
                xb = x[:, ds(i * 2, 2), :]
                dve.tensor_tensor(xb, bank[:, 6, 0:SQ].rearrange("q (t e) -> q t e", t=QT), xb, ALU.add).then_inc(s(a, "x_add"), 1)

            piped(dve, front, back)
            dve.wait_ge(s(a, "x_add"), a.at("x_add") + B)
            dve.sem_inc(x_done, 1)

        def attn_act(a, before):
            act = nc.scalar
            act.wait_ge(x_done, before)
            L = a.layer
            if L == 2:
                norm_stats_act("X2c", cc, csq, stat_c, B * SK // P)
            norm_stats_act(a.tag, xc, wide, stat, NT)
            if L == 2:
                norm_stats_act("X2q", xc, wide, stat, NT)
            act.wait_ge(s(a, "k_ps"), a.at("k_ps") + 1)
            for h in range(2):
                dst = kT[:, 8 * h:8 * h + 8, :].rearrange("p b k -> p (b k)")
                if L == 0:
                    act.activation(dst, bank[:, 1 + h, :], ACT.Identity).then_inc(s(a, "kT"), 1)
                else:
                    act.activation(dst, bank[:, 1 + h, :], ACT.Identity, bias=col(f"L{L}_bk")).then_inc(s(a, "kT"), 1 + h)

            def front(i, u):
                if L != 1:
                    act.wait_ge(s(a, "q_ps"), a.at("q_ps") + i + 1)
                    kw = {} if L == 0 else {"bias": col(f"L{L}_bq")}
                    act.activation(qT[:, u, :], bank[:, 0, SQ:2 * SQ], ACT.Identity, **kw).then_inc(s(a, "qT"), 1)

            def soft(i, u):
                for half in range(2):
                    act.wait_ge(s(a, "sub"), a.at("sub") + i * 2 + half + 1)
                    p = prob[:, u, 2 * half:2 * half + 2, :].rearrange("q g k -> q (g k)")
                    e = act.activation(p, p, ACT.Exp, scale=a.scale)
                e.then_inc(s(a, "exp"), 1)

            def back(i, u):
                for n in range(4):
                    act.wait_ge(s(a, "ring_ps"), a.at("ring_ps") + i * 6 + n + 1)
                    if n >= 2:
                        act.wait_ge(s(a, "values"), a.at("values") + i * 4 + n - 1)
                    act.activation(pT[:, n % 2, :], bank[:, 5 + n % 2, :], ACT.Identity).then_inc(s(a, "pT"), 1)

            front(0, 0)
            soft(0, 0)
            with act.Fori(0, B // 2 - 1) as j:
                front(j * 2 + 1, 1)
                back(j * 2, 0)
                soft(j * 2 + 1, 1)
                front(j * 2 + 2, 0)
                back(j * 2 + 1, 1)
                soft(j * 2 + 2, 0)
            front(B - 1, 1)
            back(B - 2, 0)
            soft(B - 1, 1)
            back(B - 1, 1)

        def attn_pool(a, before):
            pool = nc.gpsimd
            pool.wait_ge(x_done, before)
            pool.memset(v2, 0.0).then_inc(s(a, "v2_zero"), 1)
            L = a.layer
            pool.wait_ge(S("norm", "centred"), NORMS.index(a.tag) + 1)
            pool.tensor_tensor(x[:, :, :], x[:, :, :], row(f"L{L}_bo").unsqueeze(1).to_broadcast([P, NT, P]),
                               ALU.add).then_inc(s(a, "bo"), 1)
            pool.wait_ge(S("norm", "rstd"), NORMS.index("X2q" if L == 2 else a.tag) + 1)
            pool.wait_ge(s(a, "kT"), a.at("kT") + 3)

            def batch(i, u, first=False):
                if not first:
                    pool.wait_ge(s(a, "scores"), a.at("scores") + (i - 1) * 2)
                pool.tensor_tensor(xn[:, u, :, :], xc[:, ds(i * 2, 2), :],
                                   stat[:, 3, ds(i * 2, 2)].unsqueeze(2).to_broadcast([P, QT, P]), ALU.mult).then_inc(s(a, "xn"), 1)
                pool.tensor_tensor(kblk[:, u, :, :], kT[:, ds(i, 1), :].to_broadcast([P, HG, SK]),
                                   headmask[:, :].unsqueeze(2).to_broadcast([P, HG, SK]), ALU.mult).then_inc(s(a, "kblk"), 1)

            batch(0, 0, True)
            batch(1, 1, True)
            with pool.Fori(1, B // 2) as j:
                batch(j * 2, 0)
                batch(j * 2 + 1, 1)

        xnT_all = wide[:, :, :].rearrange("p t e -> p (t e)")

        class Flip:

            def __init__(self, tag, xn2, keep=None):
                self.tag, self.xn2, self.keep = tag, xn2, keep

            def dve(self, dve, before):
                dve.wait_ge(x_done, before)
                norm_stats_dve(self.tag, x, xc, wide, stat, NT)

            def pool(self, pool, before):
                pool.wait_ge(S("norm", "rstd"), NORMS.index(self.tag) + 1)

                def batch(i, u, first=False):
                    if not first:
                        pool.wait_ge(S(self.tag, "flip_ps"), at(self.tag, "flip_ps") + i - 1)
                    pool.tensor_tensor(self.xn2[:, u, :, :], xc[:, ds(i * 2, 2), :],
                                       stat[:, 3, ds(i * 2, 2)].unsqueeze(2).to_broadcast([P, QT, P]),
                                       ALU.mult).then_inc(S(self.tag, "xn"), 1)

                batch(0, 0, True)
                batch(1, 1, True)
                with pool.Fori(1, B // 2) as j:
                    batch(j * 2, 0)
                    batch(j * 2 + 1, 1)

            def pe(self, pe, before):
                def batch(i, u, first=False):
                    pe.wait_ge(S(self.tag, "xn"), at(self.tag, "xn") + i + 1)
                    if not first:
                        pe.wait_ge(S(self.tag, "flip"), at(self.tag, "flip") + i - 1)
                    for t in range(QT):
                        m = pe.transpose(bank[:, u, t * P:(t + 1) * P], self.xn2[:, u, t, :], ident[:, :])
                    m.then_inc(S(self.tag, "flip_ps"), 1)

                batch(0, 0, True)
                batch(1, 1, True)
                with pe.Fori(1, B // 2) as j:
                    batch(j * 2, 0)
                    batch(j * 2 + 1, 1)

            def act(self, act, before):
                act.wait_ge(x_done, before)
                norm_stats_act(self.tag, xc, wide, stat, NT)

                def batch(i, u):
                    act.wait_ge(S(self.tag, "flip_ps"), at(self.tag, "flip_ps") + i + 1)
                    act.activation(xnT_all[:, ds(i * SQ, SQ)], bank[:, u, 0:SQ],
                                   ACT.Identity).then_inc(S(self.tag, "flip"), 1)

                with act.Fori(0, B // 2) as j:
                    batch(j * 2, 0)
                    batch(j * 2 + 1, 1)

        class TopTwo:
            tag = "F0"
            E, IB, CH = 8, 2, 512
            c = Carve()
            wg = c(8)
            w11 = c(8, 2, P)
            w12 = c(8, 2, P)
            w2 = c(8, 2, P)
            tri = c(8, 8)
            xn2 = c(2, QT, P)
            score = c(NT, 8)
            ex = c(NT, 8)
            cmp = c(NT, 8, 8)
            same = c(NT, 8, 8)
            rank = c(NT, 8)
            gate = c(NT, 8)
            one = c(4, NT)
            sg = c(2, 512)
            fu = c(2, 512)
            flip = Flip("F0", xn2)

            def sp(self, sp, before):
                sp.wait_ge(x_done, before)
                for dst, src in ((self.wg, A["F0_wg"]), (self.tri, A["tri8"]), (self.w11, A["F0_w11"]),
                                 (self.w12, A["F0_w12"]), (self.w2, A["F0_w2"])):
                    sp.dma_start(dst, src).then_inc(S("F0", "loaded"), 16)

            def pe(self, pe, before):
                s = lambda what: S("F0", what)
                self.flip.pe(pe, before)
                pe.wait_ge(s("loaded"), 80)
                pe.wait_ge(s("flip"), B)
                for t in range(NT):
                    m = pe.matmul(bank[:, 2, t * 8:t * 8 + 8], xnT_all[:, t * P:(t + 1) * P], self.wg,
                                  start=True, stop=True)
                m.then_inc(s("router"), 1)

                with pe.Fori(0, NT * P // self.CH) as c:
                    def up(k):
                        e, ib = k // 2, k % 2
                        wait(pe, s("fused"), c * 16 + k - 1 if k else c * 16)
                        rhs = xnT_all[:, ds(c * self.CH, self.CH)]
                        pe.matmul(bank[:, 3 + 2 * (k % 2), :], self.w11[:, e, ib, :], rhs, start=True, stop=True)
                        pe.matmul(bank[:, 4 + 2 * (k % 2), :], self.w12[:, e, ib, :], rhs, start=True,
                                  stop=True).then_inc(s("up"), 1)

                    def down(k):
                        e, ib = k // 2, k % 2
                        pe.wait_ge(s("fused"), c * 16 + k + 1)
                        if ib == 0:
                            pe.wait_ge(s("x_add"), c * 8 + e - 1 if e else c * 8)
                        for t in range(4):
                            m = pe.matmul(bank[:, e % 2, t * P:(t + 1) * P], self.fu[:, k % 2, t * P:(t + 1) * P],
                                          self.w2[:, e, ib, :], start=(ib == 0 and t == 0), stop=(ib == 1),
                                          skip_group_check=True)
                        m.then_inc(s("down"), 1)

                    up(0)
                    for k in range(1, 16):
                        up(k)
                        down(k - 1)
                    down(15)

            def dve(self, dve, before):
                s = lambda what: S("F0", what)
                self.flip.dve(dve, before)
                dve.wait_ge(s("router"), 1)
                c = Count(s("gating"))
                one = self.one
                lg = bank[:, 2, 0:NT * 8].rearrange("p (t e) -> p t e", e=8)

                def op(f, *args):
                    c.inc(f(*args))
                    c.wait(dve)

                def wide8(v):
                    return v.unsqueeze(2).to_broadcast([P, NT, 8])

                op(dve.tensor_reduce, one[:, 0, :], lg, AX.X, ALU.max)
                dve.tensor_tensor(self.score, lg, wide8(one[:, 0, :]), ALU.subtract).then_inc(s("less_max"), 1)
                dve.wait_ge(s("exp"), 1)
                op(dve.tensor_reduce, one[:, 1, :], self.ex, AX.X, ALU.add)
                op(dve.reciprocal, one[:, 2, :], one[:, 1, :])
                op(dve.tensor_tensor, self.score, self.ex, wide8(one[:, 2, :]), ALU.mult)
                other = self.score.unsqueeze(2).to_broadcast([P, NT, 8, 8])
                own = self.score.unsqueeze(3).to_broadcast([P, NT, 8, 8])
                op(dve.tensor_tensor, self.cmp, other, own, ALU.is_gt)
                op(dve.tensor_tensor, self.same, other, own, ALU.is_equal)
                op(dve.tensor_tensor, self.same, self.same, self.tri.unsqueeze(1).to_broadcast([P, NT, 8, 8]), ALU.mult)
                op(dve.tensor_tensor, self.cmp, self.cmp, self.same, ALU.add)
                op(dve.tensor_reduce, self.rank, self.cmp, AX.X, ALU.add)
                op(dve.scalar_tensor_tensor, self.gate, self.rank, 2.0, self.score, ALU.is_lt, ALU.mult)
                op(dve.tensor_reduce, one[:, 0, :], self.gate, AX.X, ALU.add)
                op(dve.tensor_scalar, one[:, 1, :], one[:, 0, :], 1e-8, None, ALU.add)
                op(dve.reciprocal, one[:, 2, :], one[:, 1, :])
                op(dve.tensor_tensor, self.gate, self.gate, wide8(one[:, 2, :]), ALU.mult)

                with dve.Fori(0, NT * P // self.CH) as ch:
                    def add(e):
                        dve.wait_ge(s("down"), ch * 16 + 2 * e + 2)
                        for t in range(4):
                            xt = x[:, ds(ch * 4 + t, 1), :].rearrange("p o d -> p (o d)")
                            g = self.gate[:, ds(ch * 4 + t, 1), e:e + 1].rearrange("p o d -> p (o d)")
                            if t == 0:
                                dve.wait_ge(s("x_add"), ch * 8 + e)
                            a = dve.scalar_tensor_tensor(xt, bank[:, e % 2, t * P:(t + 1) * P], g, xt, ALU.mult, ALU.add)
                        a.then_inc(s("x_add"), 1)

                    for k in range(16):
                        dve.wait_ge(s("silu"), ch * 16 + k + 1)
                        dve.wait_ge(s("down"), ch * 16 + k - 1 if k else ch * 16)
                        dve.tensor_tensor(self.fu[:, k % 2, :], bank[:, 4 + 2 * (k % 2), :], self.sg[:, k % 2, :],
                                          ALU.mult).then_inc(s("fused"), 1)
                        if k >= 2 and k % 2 == 0:
                            add(k // 2 - 1)
                    add(7)
                dve.wait_ge(s("x_add"), NT * P // self.CH * 8)
                dve.sem_inc(x_done, 1)

            def act(self, act, before):
                s = lambda what: S("F0", what)
                self.flip.act(act, before)
                act.wait_ge(s("less_max"), 1)
                act.activation(self.ex, self.score, ACT.Exp).then_inc(s("exp"), 1)
                with act.Fori(0, NT * P // self.CH) as ch:
                    for k in range(16):
                        act.wait_ge(s("up"), ch * 16 + k + 1)
                        act.wait_ge(s("fused"), ch * 16 + k - 1 if k else ch * 16)
                        act.activation(self.sg[:, k % 2, :], bank[:, 3 + 2 * (k % 2), :], ACT.Silu).then_inc(s("silu"), 1)

            def pool(self, pool, before):
                pool.wait_ge(x_done, before)
                self.flip.pool(pool, before)

        class ExpertChoice:
            tag = "F3"
            E, FB, CH, K, BITS = 8, 4, 512, 256, 30
            c = Carve()
            rw = c(8)
            w1 = c(8, 4, P)
            w2 = c(8, 4, P)
            b1 = c(8, 4)
            rb = c(8)
            b2 = c(P)
            bits = c(30, dt=I32)
            xn2 = c(2, QT, P)
            score = c(NT, 8)
            ex = c(NT, 8)
            hit = c(NT, 8)
            part = c(8)
            okb = c(8, dt=I32)
            thr = c(8, dt=I32)
            cand = c(8, dt=I32)
            gate = c(NT, 8)
            eq = c(NT, 8)
            eqb = c(NT, 8, dt=BF16)
            tot = c(8, NT)
            run = c(8, NT)
            room = c(8)
            one = c(4, NT)
            ones8 = c(8, NT)
            triu = c(P, dt=BF16)
            oneb = c(P, dt=BF16)
            gT = c(NT * P)
            h = c(2, 512)
            flip = Flip("F3", xn2)

            def sp(self, sp, before):
                sp.wait_ge(x_done, before)
                for dst, src in ((self.rw, A["F3_rw"]), (self.rb, A["F3_rb"].partition_broadcast(P)),
                                 (self.b2[0:8, :], A["F3_b2"]), (self.b1, A["F3_b1"]),
                                 (self.bits, A["bits"].partition_broadcast(P)),
                                 (self.w1, A["F3_w1"]), (self.w2, A["F3_w2"])):
                    sp.dma_start(dst, src).then_inc(S("F3", "loaded"), 16)

            def pe(self, pe, before):
                s = lambda what: S("F3", what)
                self.flip.pe(pe, before)
                pe.wait_ge(s("loaded"), at("F3", "loaded") + 16 * 7)
                pe.wait_ge(s("flip"), at("F3", "flip") + B)
                for t in range(NT):
                    m = pe.matmul(bank[:, 2, t * 8:t * 8 + 8], xnT_all[:, t * P:(t + 1) * P], self.rw,
                                  start=True, stop=True)
                m.then_inc(s("router"), 1)
                with pe.Fori(0, self.BITS) as n:
                    pe.wait_ge(s("part"), n + 1)
                    pe.matmul(bank[:, 0, 0:8], onesf[:, :], self.part, start=True, stop=True).then_inc(s("count"), 1)
                pe.wait_ge(s("part"), self.BITS + 1)
                pe.matmul(bank[:, 0, 0:8], onesf[:, :], self.part, start=True, stop=True).then_inc(s("count"), 1)
                pe.wait_ge(s("eqb"), 1)
                pe.wait_ge(s("tri"), 3)
                eqb = self.eqb.rearrange("p t e -> p (t e)")
                pe.matmul(bank[:, 3, 0:NT * 8], self.triu, eqb, start=True, stop=True)
                pe.matmul(bank[:, 4, 0:NT * 8], self.oneb, eqb, start=True, stop=True).then_inc(s("eq_ps"), 1)
                pe.wait_ge(s("gate"), 1)
                for t in range(NT):
                    m = pe.transpose(bank[0:8, t // 4, (t % 4) * P:(t % 4 + 1) * P], self.gate[:, t, :], ident[:, :])
                m.then_inc(s("gT_ps"), 1)
                for q in range(8):
                    pe.wait_ge(s("gT"), q + 1)
                    for t in range(4 * q, 4 * q + 4):
                        m = pe.matmul(bank[:, t // 4, (t % 4) * P:(t % 4 + 1) * P], self.gT[0:8, t * P:(t + 1) * P],
                                      self.b2[0:8, :], start=True, stop=True)
                    m.then_inc(s("b2_ps"), 1)
                pe.wait_ge(s("b2_add"), 8)

                with pe.Fori(0, NT * P // self.CH) as c:
                    def up(k):
                        e, f = k // 4, k % 4
                        wait(pe, s("h"), c * 32 + k - 1 if k else c * 32)
                        pe.matmul(bank[:, 2 + k % 2, :], self.w1[:, e, f, :], xnT_all[:, ds(c * self.CH, self.CH)],
                                  start=True, stop=True).then_inc(s("up"), 1)

                    def down(k):
                        e, f = k // 4, k % 4
                        pe.wait_ge(s("h"), c * 32 + k + 1)
                        if f == 0:
                            pe.wait_ge(s("x_add"), at("F3", "x_add") + (c * 8 + e - 1 if e else c * 8))
                        for t in range(4):
                            m = pe.matmul(bank[:, e % 2, t * P:(t + 1) * P], self.h[:, k % 2, t * P:(t + 1) * P],
                                          self.w2[:, e, f, :], start=(f == 0 and t == 0), stop=(f == 3),
                                          skip_group_check=True)
                        m.then_inc(s("down"), 1)

                    up(0)
                    for k in range(1, 32):
                        up(k)
                        down(k - 1)
                    down(31)

            def dve(self, dve, before):
                s = lambda what: S("F3", what)
                self.flip.dve(dve, before)
                one = self.one
                lg = bank[:, 2, 0:NT * 8].rearrange("p (t e) -> p t e", e=8)
                c = Count(s("gating"))

                def op(f, *args):
                    c.inc(f(*args))
                    c.wait(dve)

                def wide8(v):
                    return v.unsqueeze(2).to_broadcast([P, NT, 8])

                def tiles(v):
                    return v.unsqueeze(1).to_broadcast([P, NT, 8])

                dve.wait_ge(s("router"), at("F3", "router") + 1)
                dve.wait_ge(s("loaded"), at("F3", "loaded") + 16 * 7)
                op(dve.tensor_tensor, self.ex, lg, tiles(self.rb), ALU.add)
                op(dve.tensor_reduce, one[:, 0, :], self.ex, AX.X, ALU.max)
                dve.tensor_tensor(self.score, self.ex, wide8(one[:, 0, :]), ALU.subtract).then_inc(s("less_max"), 1)
                op(dve.memset, self.thr, 0)
                dve.wait_ge(s("exp"), at("F3", "exp") + 1)
                op(dve.tensor_reduce, one[:, 1, :], self.ex, AX.X, ALU.add)
                op(dve.reciprocal, one[:, 2, :], one[:, 1, :])
                op(dve.tensor_tensor, self.score, self.ex, wide8(one[:, 2, :]), ALU.mult)

                by_expert = self.hit.rearrange("p t e -> p e t")
                with dve.Fori(0, self.BITS) as n:
                    b = Count(s("bit"), n * 5)
                    bit = self.bits[:, ds(n, 1)].to_broadcast([P, 8])
                    b.inc(dve.tensor_tensor(self.cand, self.thr, bit, ALU.bitwise_or))
                    b.wait(dve)
                    b.inc(dve.tensor_tensor(self.hit, self.score, tiles(self.cand.bitcast(F32)), ALU.is_ge))
                    b.wait(dve)
                    dve.tensor_reduce(self.part, by_expert, AX.X, ALU.add).then_inc(s("part"), 1)
                    dve.wait_ge(s("count"), n + 1)
                    b.inc(dve.tensor_scalar(self.okb, bank[:, 0, 0:8], float(self.K), None, ALU.is_ge))
                    b.wait(dve)
                    b.inc(dve.tensor_tensor(self.okb, self.okb, bit, ALU.mult))
                    b.wait(dve)
                    b.inc(dve.tensor_tensor(self.thr, self.thr, self.okb, ALU.bitwise_or))
                    b.wait(dve)
                thr = tiles(self.thr.bitcast(F32))
                op(dve.tensor_tensor, self.hit, self.score, thr, ALU.is_gt)
                dve.tensor_reduce(self.part, by_expert, AX.X, ALU.add).then_inc(s("part"), 1)
                op(dve.tensor_tensor, self.eq, self.score, thr, ALU.is_equal)
                op(dve.memset, self.ones8, 1.0)
                dve.tensor_copy(self.eqb, self.eq).then_inc(s("eqb"), 1)
                dve.wait_ge(s("count"), self.BITS + 1)
                op(dve.tensor_scalar, self.room, bank[:, 0, 0:8], -1.0, float(self.K), ALU.mult, ALU.add)
                dve.wait_ge(s("eq_ps"), 1)
                op(dve.tensor_copy, self.tot, bank[:, 4, 0:NT * 8].rearrange("p (t e) -> p e t", e=8))
                for e in range(8):
                    op(dve.tensor_tensor_scan, self.run[:, e, :], self.ones8[:, e, :], self.tot[:, e, :], 0.0,
                       ALU.mult, ALU.add)
                op(dve.tensor_tensor, self.run, self.run, self.tot, ALU.subtract)
                before_it = self.gate
                op(dve.tensor_tensor, before_it, bank[:, 3, 0:NT * 8].rearrange("p (t e) -> p t e", e=8),
                   self.run.rearrange("p e t -> p t e"), ALU.add)
                op(dve.tensor_tensor, self.gate, before_it, tiles(self.room), ALU.is_lt)
                op(dve.tensor_tensor, self.gate, self.gate, self.eq, ALU.mult)
                op(dve.tensor_tensor, self.gate, self.gate, self.hit, ALU.add)
                dve.tensor_tensor(self.gate, self.gate, self.score, ALU.mult).then_inc(s("gate"), 1)
                dve.wait_ge(s("gate"), 1)
                dve.wait_ge(s("gT_ps"), 1)
                for q in range(8):
                    dve.tensor_copy(self.gT[0:8, q * 512:(q + 1) * 512], bank[0:8, q, :]).then_inc(s("gT"), 1)
                for q in range(8):
                    dve.wait_ge(s("b2_ps"), q + 1)
                    xb = x[:, 4 * q:4 * q + 4, :]
                    dve.tensor_tensor(xb, bank[:, q, :].rearrange("p (t d) -> p t d", t=4), xb,
                                      ALU.add).then_inc(s("b2_add"), 1)

                dve.wait_ge(s("b2_add"), 8)
                with dve.Fori(0, NT * P // self.CH) as ch:
                    for e in range(8):
                        dve.wait_ge(s("down"), at("F3", "down") + ch * 32 + 4 * e + 4)
                        dve.wait_ge(s("x_add"), at("F3", "x_add") + ch * 8 + e)
                        for t in range(4):
                            xt = x[:, ds(ch * 4 + t, 1), :].rearrange("p o d -> p (o d)")
                            g = self.gate[:, ds(ch * 4 + t, 1), e:e + 1].rearrange("p o d -> p (o d)")
                            a = dve.scalar_tensor_tensor(xt, bank[:, e % 2, t * P:(t + 1) * P], g, xt, ALU.mult, ALU.add)
                        a.then_inc(s("x_add"), 1)
                dve.wait_ge(s("x_add"), at("F3", "x_add") + NT * P // self.CH * 8)
                dve.sem_inc(x_done, 1)

            def act(self, act, before):
                s = lambda what: S("F3", what)
                self.flip.act(act, before)
                act.wait_ge(s("less_max"), at("F3", "less_max") + 1)
                act.activation(self.ex, self.score, ACT.Exp).then_inc(s("exp"), 1)
                with act.Fori(0, NT * P // self.CH) as ch:
                    for k in range(32):
                        act.wait_ge(s("up"), at("F3", "up") + ch * 32 + k + 1)
                        act.wait_ge(s("down"), at("F3", "down") + (ch * 32 + k - 1 if k else ch * 32))
                        act.activation(self.h[:, k % 2, :], bank[:, 2 + k % 2, :], ACT.Relu,
                                       bias=self.b1[:, k // 4, k % 4:k % 4 + 1]).then_inc(s("h"), 1)

            def pool(self, pool, before):
                pool.wait_ge(x_done, before)
                pool.memset(self.triu, 1.0).then_inc(S("F3", "tri"), 1)
                pool.memset(self.oneb, 1.0).then_inc(S("F3", "tri"), 1)
                pool.wait_ge(S("F3", "tri"), 2)
                pool.affine_select(self.triu, self.triu, [[1, P]], ALU.is_gt, 0.0, base=0,
                                   channel_multiplier=-1).then_inc(S("F3", "tri"), 1)
                self.flip.pool(pool, before)

        class SoftSlots:
            tag = "F1"
            tag = "F1"
            NC, N4 = 16, 4
            c = Carve()
            phi = c(2048)
            bn = c(64)
            wc = c(2, 4, P)
            sT = c(B, P)
            yT = c(B, P)
            yo = c(B, P)
            top = c(2, 2, P)
            ssum = c(2, 2, P)
            rinv = c(2, 2, P)
            ex = c(2, 2, B, P)
            c = Carve(2048)
            xs = c(2, SQ)
            e2 = c(2, 2048)
            eT = c(2, 4, P)
            yb = c(2, 16, P)
            ntop = c(4)
            part = c(4, 4)
            tot = c(4)
            ri = c(4)

            def s(self, what):
                return S("F1", what)

            def sp(self, sp, before):
                s = self.s
                sp.wait_ge(x_done, before)
                sp.dma_start(self.phi, A["F1_phi"]).then_inc(s("loaded"), 16)
                sp.dma_start(self.bn, A["F1_b"]).then_inc(s("loaded"), 16)

                def chunk(c, u, first=False):
                    if not first:
                        sp.wait_ge(s("yT_ps"), (c - 1) * 4)
                    sp.dma_start(self.wc[:, u, :, :], A["F1_w"][ds(c, 1), :, :].rearrange("o p n -> p (o n)")).then_inc(
                        s("wc%d" % u), 16)

                def store(c):
                    sp.wait_ge(s("yo"), c * 4 + 4)
                    sp.dma_start(A["y_slots"][:, :, ds(c, 1), :].rearrange("b p o d -> p b (o d)"), self.yo).then_inc(s("y_out"), 16)

                chunk(0, 0, True)
                chunk(1, 1, True)
                with sp.Fori(0, self.NC // 2 - 1) as j:
                    chunk(j * 2 + 2, 0)
                    store(j * 2)
                    chunk(j * 2 + 3, 1)
                    store(j * 2 + 1)
                store(self.NC - 2)
                store(self.NC - 1)
                sp.wait_ge(s("y_out"), 16 * self.NC)

                def batch(b, u, first=False):
                    if not first:
                        sp.wait_ge(s("out"), (b - 1) * 2)
                    sp.dma_start(self.yb[:, u, :, :], A["y_slots"][ds(b, 1), :, :, :].rearrange("o p c d -> p (o c) d")).then_inc(
                        s("yb%d" % u), 16)

                sp.wait_ge(s("all_slots"), 1)
                batch(0, 0, True)
                batch(1, 1, True)
                with sp.Fori(1, B // 2) as j:
                    batch(j * 2, 0)
                    batch(j * 2 + 1, 1)

            def pe(self, pe, before):
                s = self.s
                pe.wait_ge(s("xn"), 1)
                for t in range(NT):
                    m = pe.transpose(bank[:, t // 4, (t % 4) * P:(t % 4 + 1) * P], xc[:, t, :], ident[:, :])
                    if t % 4 == 3:
                        m.then_inc(s("flip_ps"), 1)
                pe.wait_ge(s("flip"), 8)
                pe.wait_ge(s("loaded"), 32)

                def logits(c, h):
                    wait(pe, s("sub"), c * 2 + h)
                    for b in range(B):
                        t = 2 * b + h
                        m = pe.matmul(bank[:, b // 4, (b % 4) * P:(b % 4 + 1) * P], xnT_all[:, t * P:(t + 1) * P],
                                      self.phi[:, ds(c * P, P)], start=True, stop=True)
                    m.then_inc(s("logits"), 1)

                def slots(c, u):
                    pe.wait_ge(s("disp"), c * 2 + 2)
                    wait(pe, s("yo"), c * 4)
                    for b in range(B):
                        for h in range(2):
                            m = pe.matmul(bank[:, 4 + b // 4, (b % 4) * P:(b % 4 + 1) * P], xc[:, 2 * b + h, :],
                                          self.ex[:, u, h, b, :], start=(h == 0), stop=(h == 1))
                        if b % 4 == 3:
                            m.then_inc(s("slots"), 1)

                def experts(c, u):
                    pe.wait_ge(s("sT"), c * 4 + 4)
                    pe.wait_ge(s("wc%d" % u), (c // 2 + 1) * 16 if isinstance(c, int) else c * 8 + (16 - 8 * u))
                    for n in range(4):
                        pe.matmul(bank[:, 4 + n, :], self.wc[:, u, n, :], self.sT[:, :, 32 * n:32 * n + 32],
                                  start=True, stop=True).then_inc(s("yT_ps"), 1)
                    pe.wait_ge(s("yT"), c * 4 + 4)
                    for b in range(B):
                        m = pe.transpose(bank[:, 4 + b // 4, (b % 4) * P:(b % 4 + 1) * P], self.yT[:, b, :], ident[:, :])
                        if b % 4 == 3:
                            m.then_inc(s("yo_ps"), 1)

                logits(0, 0)
                logits(0, 1)
                with pe.Fori(0, self.NC // 2 - 1) as j:
                    for u in range(2):
                        c = j * 2 + u
                        logits(c + 1, 0)
                        slots(c, u)
                        logits(c + 1, 1)
                        experts(c, u)
                logits(self.NC - 1, 0)
                slots(self.NC - 2, 0)
                logits(self.NC - 1, 1)
                experts(self.NC - 2, 0)
                slots(self.NC - 1, 1)
                experts(self.NC - 1, 1)

                pe.wait_ge(s("yo"), self.NC * 4)

                def front(t, q):
                    b2 = (q // 2) % 2
                    pe.wait_ge(s("xs"), t // 2 + 1 if isinstance(t, int) else (t - q % 2) // 2 + 1)
                    wait(pe, s("exp"), t * 4)
                    for k in range(4):
                        m = pe.matmul(bank[:, k, :], self.xs[:, b2, (q % 2) * P:(q % 2 + 1) * P],
                                      self.phi[:, k * 512:(k + 1) * 512], start=True, stop=True)
                    m.then_inc(s("lt"), 1)

                def back(t, q):
                    b2 = q // 2
                    if q % 2 == 0:
                        pe.wait_ge(s("yb%d" % b2), ((t // 4 if isinstance(t, int) else (t - q) // 4) + 1) * 16)

                    def lot(k):
                        pe.wait_ge(s("exp"), t * 4 + k + 1)
                        wait(pe, s("eT"), t * 4 + k - 1)
                        for r in range(4):
                            ch = 4 * k + r
                            m = pe.transpose(bank[:, 4 + k % 2, r * P:(r + 1) * P], self.e2[:, q % 2, ch * P:(ch + 1) * P],
                                             ident[:, :])
                        m.then_inc(s("eT_ps"), 1)

                    def mix(k):
                        pe.wait_ge(s("eT"), t * 4 + k + 1)
                        if k == 0:
                            wait(pe, s("x_add"), t - 1)
                        for r in range(4):
                            ch = 4 * k + r
                            m = pe.matmul(bank[:, 6 + q % 2, 0:P], self.eT[:, k % 2, r, :], self.yb[:, b2, ch, :],
                                          start=(ch == 0), stop=(ch == 15))
                        m.then_inc(s("mix"), 1)
                        return m

                    lot(0)
                    for k in range(1, 4):
                        lot(k)
                        mix(k - 1)
                    mix(3)
                    pe.wait_ge(s("mix"), t * 4 + 4)
                    pe.sem_inc(s("out"), 1)

                front(0, 0)
                for q in range(4):
                    front(q + 1, (q + 1) % 4)
                    back(q, q)
                with pe.Fori(1, NT // 4 - 1) as j:
                    for q in range(4):
                        front(j * 4 + q + 1, (q + 1) % 4)
                        back(j * 4 + q, q)
                for q in range(4):
                    if q < 3:
                        front(NT - 4 + q + 1, q + 1)
                    back(NT - 4 + q, q)

            def dve(self, dve, before):
                s = self.s
                dve.wait_ge(x_done, before)
                norm_stats_dve("F1", x, xc, wide, stat, NT)
                dve.wait_ge(S("norm", "rstd"), NORMS.index(self.tag) + 1)
                dve.tensor_tensor(xc[:, :, :], xc[:, :, :], stat[:, 3, :].unsqueeze(2).to_broadcast([P, NT, P]),
                                  ALU.mult).then_inc(s("xn"), 1)
                for q in range(8):
                    dve.wait_ge(s("flip_ps"), q + 1)
                    dve.tensor_copy(xnT_all[:, q * 512:(q + 1) * 512], bank[:, q, :]).then_inc(s("flip"), 1)

                def softmax(c, u, h):
                    d = Count(s("batch_max"), c * 2 + h)
                    lg = bank[:, 0:4, :].rearrange("p k (b n) -> p (k b) n", n=P)
                    dve.wait_ge(s("logits"), c * 2 + h + 1)
                    d.inc(dve.tensor_reduce(self.top[:, u, h, :], lg.rearrange("p b n -> p n b"), AX.X, ALU.max))
                    d.wait(dve)
                    wait(dve, s("slots"), (c - 1) * 4)
                    dve.tensor_tensor(self.ex[:, u, h, :, :], lg, self.top[:, u, h, :].unsqueeze(1).to_broadcast([P, B, P]),
                                      ALU.subtract).then_inc(s("sub"), 1)

                def weights(c, u, h):
                    d = Count(s("batch_sum"), c * 2 + h)
                    dve.wait_ge(s("bexp"), c * 2 + h + 1)
                    d.inc(dve.tensor_reduce(self.ssum[:, u, h, :], self.ex[:, u, h, :, :].rearrange("p b n -> p n b"),
                                            AX.X, ALU.add))
                    d.wait(dve)
                    dve.reciprocal(self.rinv[:, u, h, :], self.ssum[:, u, h, :]).then_inc(s("rinv"), 1)

                softmax(0, 0, 0)
                softmax(0, 0, 1)
                weights(0, 0, 0)
                weights(0, 0, 1)
                softmax(1, 1, 0)
                softmax(1, 1, 1)
                weights(1, 1, 0)
                weights(1, 1, 1)
                with dve.Fori(1, self.NC // 2) as j:
                    for u in range(2):
                        for h in range(2):
                            softmax(j * 2 + u, u, h)
                        for h in range(2):
                            weights(j * 2 + u, u, h)

                def front(t, q):
                    dve.wait_ge(s("lt"), t + 1)
                    dve.tensor_reduce(self.ntop[:, q:q + 1], bank[:, 0:4, :].rearrange("p k n -> p (k n)"), AX.X, ALU.max,
                                      negate=True).then_inc(s("ntop"), 1)

                def back(t, q):
                    for k in (1, 3):
                        dve.wait_ge(s("eT_ps"), t * 4 + k + 1)
                        if k == 3 or not (isinstance(t, int) and t == 0):
                            dve.wait_ge(s("mix"), t * 4 + k - 1)
                        dve.wait_ge(s("eT"), t * 4 + k)
                        dve.tensor_copy(self.eT[:, k % 2, :, :].rearrange("p r m -> p (r m)"),
                                        bank[:, 4 + k % 2, :]).then_inc(s("eT"), 1)
                    d = Count(s("norm"), t * 2)
                    dve.wait_ge(s("exp"), t * 4 + 4)
                    d.inc(dve.tensor_reduce(self.tot[:, q:q + 1], self.part[:, q, :], AX.X, ALU.add))
                    d.wait(dve)
                    d.inc(dve.reciprocal(self.ri[:, q:q + 1], self.tot[:, q:q + 1]))
                    d.wait(dve)
                    dve.wait_ge(s("out"), t + 1)
                    xt = x[:, ds(t, 1), :].rearrange("p o d -> p (o d)")
                    dve.scalar_tensor_tensor(xt, bank[:, 6 + q % 2, 0:P], self.ri[:, q:q + 1], xt, ALU.mult,
                                             ALU.add).then_inc(s("x_add"), 1)

                front(0, 0)
                for q in range(4):
                    front(q + 1, (q + 1) % 4)
                    back(q, q)
                with dve.Fori(1, NT // 4 - 1) as j:
                    for q in range(4):
                        front(j * 4 + q + 1, (q + 1) % 4)
                        back(j * 4 + q, q)
                for q in range(4):
                    if q < 3:
                        front(NT - 4 + q + 1, q + 1)
                    back(NT - 4 + q, q)
                dve.wait_ge(s("x_add"), NT)
                dve.sem_inc(x_done, 1)

            def act(self, act, before):
                s = self.s
                act.wait_ge(x_done, before)
                norm_stats_act("F1", xc, wide, stat, NT)

                def exps(c, u):
                    for h in range(2):
                        act.wait_ge(s("sub"), c * 2 + h + 1)
                        e = self.ex[:, u, h, :, :].rearrange("p b n -> p (b n)")
                        act.activation(e, e, ACT.Exp).then_inc(s("bexp"), 1)

                def evac(c, u):
                    for k in range(4):
                        act.wait_ge(s("slots"), c * 4 + k + 1)
                        act.activation(self.sT[:, 4 * k:4 * k + 4, :].rearrange("p b n -> p (b n)"), bank[:, 4 + k, :],
                                       ACT.Identity).then_inc(s("sT"), 1)
                    for n in range(4):
                        act.wait_ge(s("yT_ps"), c * 4 + n + 1)
                        act.activation(self.yT[:, :, 32 * n:32 * n + 32], bank[:, 4 + n, :].rearrange("p (b q) -> p b q", q=32),
                                       ACT.Identity, bias=self.bn[:, ds(c * 4 + n, 1)]).then_inc(s("yT"), 1)
                    wait(act, s("y_out"), c * 16)
                    for k in range(4):
                        act.wait_ge(s("yo_ps"), c * 4 + k + 1)
                        act.activation(self.yo[:, 4 * k:4 * k + 4, :].rearrange("p b n -> p (b n)"), bank[:, 4 + k, :],
                                       ACT.Identity).then_inc(s("yo"), 1)

                exps(0, 0)
                with act.Fori(0, self.NC // 2 - 1) as j:
                    for u in range(2):
                        exps(j * 2 + u + 1, 1 - u)
                        evac(j * 2 + u, u)
                exps(self.NC - 1, 1)
                evac(self.NC - 2, 0)
                evac(self.NC - 1, 1)

                def front(t, q):
                    act.wait_ge(s("ntop"), t + 1)
                    wait(act, s("eT_ps"), (t - 1) * 4)
                    wait(act, s("x_add"), t - 3)
                    for k in range(4):
                        act.activation(self.e2[:, q % 2, k * 512:(k + 1) * 512], bank[:, k, :], ACT.Exp,
                                       bias=self.ntop[:, q:q + 1], accum_out=self.part[:, q, k:k + 1]).then_inc(s("exp"), 1)

                def back(t, q):
                    for k in (0, 2):
                        act.wait_ge(s("eT_ps"), t * 4 + k + 1)
                        if k == 2 or not (isinstance(t, int) and t == 0):
                            act.wait_ge(s("mix"), t * 4 + k - 1)
                            act.wait_ge(s("eT"), t * 4 + k)
                        act.activation(self.eT[:, k % 2, :, :].rearrange("p r m -> p (r m)"), bank[:, 4 + k % 2, :],
                                       ACT.Identity).then_inc(s("eT"), 1)

                front(0, 0)
                for q in range(4):
                    back(q, q)
                    front(q + 1, (q + 1) % 4)
                with act.Fori(1, NT // 4 - 1) as j:
                    for q in range(4):
                        back(j * 4 + q, q)
                        front(j * 4 + q + 1, (q + 1) % 4)
                for q in range(4):
                    back(NT - 4 + q, q)
                    if q < 3:
                        front(NT - 4 + q + 1, q + 1)

            def pool(self, pool, before):
                s = self.s

                def weights(c, u):
                    for h in range(2):
                        pool.wait_ge(s("rinv"), c * 2 + h + 1)
                        pool.tensor_tensor(self.ex[:, u, h, :, :], self.ex[:, u, h, :, :],
                                           self.rinv[:, u, h, :].unsqueeze(1).to_broadcast([P, B, P]),
                                           ALU.mult).then_inc(s("disp"), 1)

                with pool.Fori(0, self.NC // 2) as j:
                    weights(j * 2, 0)
                    weights(j * 2 + 1, 1)
                pool.wait_ge(s("yo"), self.NC * 4)
                pool.wait_ge(s("y_out"), self.NC * 16)
                pool.sem_inc(s("all_slots"), 1)

                def batch(b, u, first=False):
                    if not first:
                        pool.wait_ge(s("lt"), (b - 1) * 2)
                    pool.tensor_copy(self.xs[:, u, :], xnT_all[:, ds(b * SQ, SQ)]).then_inc(s("xs"), 1)

                batch(0, 0, True)
                batch(1, 1, True)
                with pool.Fori(1, B // 2) as j:
                    batch(j * 2, 0)
                    batch(j * 2 + 1, 1)

        class Trees:
            tag = "F2"
            LEAF, GROUPS, NBLK, IT = 8, 32, 64, 16
            XW = P + 8
            c = Carve()
            w1 = c(GROUPS * P)
            w2 = c(GROUPS * P)
            b1 = c(GROUPS * P)
            b2 = c(GROUPS * P)
            xm = c(NT, XW)
            nw = c(256)
            nb = c(256)
            slot = c(4, NT, dt=I32)
            grp = c(NBLK, dt=I32)
            iota = c(NBLK)
            tri = c(P, dt=BF16)
            oneb = c(P, dt=BF16)
            r0 = c.at
            bits = c(NT, 256, dt=BF16)
            tmp = c(NT * P, dt=BF16)
            G = c(NT, 32, dt=BF16)
            oa = c(NT * 32)
            ob = c(NT * 32)
            totg = c(32, NT)
            incl = c(32, NT)
            sub = c(NT, 7)
            p1 = c(NT, 2)
            p2 = c(NT, 4)
            sm = c(8, 32)
            nbi = c(32, dt=I32)
            slotf = c(NT)
            c = Carve(r0)
            xin = c(2, 4, XW)
            xT = c(2, 512)
            mT = c(2, 512)
            gl = c(2, 512)
            hm = c(2, 512)
            hT = c(2, 512)
            yo = c(2, 4, P)
            c = Carve(r0)
            qkv = c(2, 3, QT, P)
            qkT = c(2, 512)
            e = c(2, QT, SQ)
            eT = c(2, 512)
            yb = c(2, QT, P)
            small = c(8, 2, 2)
            c = Carve(r0)
            out = c(NT, P)

            def __init__(self):
                self.links = 0

            def s(self, what):
                return S("F2", what)

            def sp(self, sp, before):
                s = self.s
                sp.wait_ge(x_done, before)
                sp.dma_start(self.iota, A["iota64"].partition_broadcast(P)).then_inc(s("const"), 16)
                for n in range(4):
                    if n:
                        sp.wait_ge(s("y"), 16 * n)
                    sp.dma_start(self.nw[:, 0:255], A["F2_nw"][n, :, :]).then_inc(s("nw"), 16)
                    sp.dma_start(self.nb[:, 0:255], A["F2_nb"][n, :].partition_broadcast(P)).then_inc(s("nw"), 16)
                    for dst, src in ((self.w1, "w1"), (self.w2, "w2"), (self.b1[0:8, :], "b1"), (self.b2[0:8, :], "b2")):
                        sp.dma_start(dst, A["F2_" + src][n, :, :]).then_inc(s("w"), 16)
                    sp.wait_ge(s("scattered"), 16 * NT * (n + 1))

                    def load(i, u, first=False):
                        if not first:
                            sp.wait_ge(s("hm"), n * 16 + i - 1)
                        sp.dma_start(self.xin[:, u, :, :], A["xs"][ds(i * 4, 4), :, :].rearrange("k p w -> p k w")).then_inc(
                            s("xin%d" % u), 16)

                    def store(i, u):
                        sp.wait_ge(s("yo"), n * 16 + i + 1)
                        sp.dma_start(A["ys%d" % n][ds(i * 4, 4), :, :].rearrange("k p w -> p k w"), self.yo[:, u, :, :]).then_inc(
                            s("ys%d" % u), 16)

                    load(0, 0, True)
                    load(1, 1, True)
                    with sp.Fori(0, self.IT // 2 - 1) as j:
                        store(j * 2, 0)
                        load(j * 2 + 2, 0)
                        store(j * 2 + 1, 1)
                        load(j * 2 + 3, 1)
                    store(self.IT - 2, 0)
                    store(self.IT - 1, 1)
                    sp.wait_ge(s("ys0"), 128 * (n + 1))
                    sp.wait_ge(s("ys1"), 128 * (n + 1))

            def pe(self, pe, before):
                s = self.s
                pe.wait_ge(s("xn"), at("F2", "xn") + 1)
                for t in range(NT):
                    m = pe.transpose(bank[:, t // 4, (t % 4) * P:(t % 4 + 1) * P], xc[:, t, :], ident[:, :])
                    if t % 4 == 3:
                        m.then_inc(s("flip_ps"), 1)
                pe.wait_ge(s("flip"), at("F2", "flip") + 8)
                pe.wait_ge(s("tri"), 3)
                for n in range(4):
                    if n == 3:
                        self.attend_pe(pe)
                    self.tree_pe(pe, n)

            def tree_pe(self, pe, n):
                s = self.s
                pe.wait_ge(s("nw"), 32 * (n + 1))
                if n:
                    pe.wait_ge(s("yo"), 16 * n)
                for tp in range(16):
                    wait(pe, s("bits"), n * 16 + tp - 7)
                    for h in range(2):
                        t = 2 * tp + h
                        m = pe.matmul(bank[:, tp % 8, h * 255:(h + 1) * 255], xnT_all[:, t * P:(t + 1) * P],
                                      self.nw[:, 0:255], start=True, stop=True)
                    m.then_inc(s("nodes"), 1)
                pe.wait_ge(s("G"), n + 1)
                Gf = self.G.rearrange("p t g -> p (t g)")
                for k in range(2):
                    pe.matmul(bank[:, k, :], self.tri, Gf[:, k * 512:(k + 1) * 512], start=True, stop=True)
                    m = pe.matmul(bank[:, 2 + k, :], self.oneb, Gf[:, k * 512:(k + 1) * 512], start=True, stop=True)
                m.then_inc(s("rank"), 1)
                pe.wait_ge(s("w"), 64 * (n + 1))
                pe.wait_ge(s("slots"), n + 1)

                def groups(i):
                    return [pe.value_load(self.grp[0:1, ds(i * 4 + k, 1)], min_val=0, max_val=31 * P) for k in range(4)]

                def front(i, u):
                    turn = i // 2 if isinstance(i, int) else (i - u) // 2
                    pe.wait_ge(s("xin%d" % u), n * 128 + (turn + 1) * 16)
                    for k in range(4):
                        pe.transpose(bank[:, 0, k * P:(k + 1) * P], self.xin[:, u, k, 0:P], ident[:, :])
                    for k in range(4):
                        m = pe.transpose(bank[0:8, 1, k * P:(k + 1) * P], self.xin[:, u, k, P:P + 8], ident[:, :])
                    m.then_inc(s("t1"), 1)
                    off = groups(i)
                    pe.wait_ge(s("xT"), n * 16 + i + 1)
                    pe.wait_ge(s("mT"), n * 16 + i + 1)
                    wait(pe, s("act"), n * 16 + i)
                    for k in range(4):
                        o = bank[:, 2, k * P:(k + 1) * P]
                        pe.matmul(o, self.xT[:, u, k * P:(k + 1) * P], self.w1[:, ds(off[k], P)], start=True, stop=False)
                        m = pe.matmul(o, self.mT[0:8, u, k * P:(k + 1) * P], self.b1[0:8, ds(off[k], P)],
                                      start=False, stop=True)
                    m.then_inc(s("h"), 1)

                def back(i, u):
                    pe.wait_ge(s("hm"), n * 16 + i + 1)
                    for k in range(4):
                        m = pe.transpose(bank[:, 3, k * P:(k + 1) * P], self.hm[:, u, k * P:(k + 1) * P], ident[:, :])
                    m.then_inc(s("t2"), 1)
                    off = groups(i)
                    pe.wait_ge(s("hT"), n * 16 + i + 1)
                    wait(pe, s("yo"), n * 16 + i)
                    for k in range(4):
                        o = bank[:, 4, k * P:(k + 1) * P]
                        pe.matmul(o, self.hT[:, u, k * P:(k + 1) * P], self.w2[:, ds(off[k], P)], start=True, stop=False)
                        m = pe.matmul(o, self.mT[0:8, u, k * P:(k + 1) * P], self.b2[0:8, ds(off[k], P)],
                                      start=False, stop=True)
                    m.then_inc(s("y"), 1)

                piped(pe, front, back)

            def attend_pe(self, pe):
                s = self.s
                pe.wait_ge(s("yo"), 48)

                def front(i, u):
                    turn = i // 2 if isinstance(i, int) else (i - u) // 2
                    pe.wait_ge(s("qkv%d" % u), (turn + 1) * 96)
                    for m3 in range(2):
                        for t in range(QT):
                            m = pe.transpose(bank[:, 0, (m3 * 2 + t) * P:(m3 * 2 + t + 1) * P], self.qkv[:, u, m3, t, :],
                                             ident[:, :])
                    m.then_inc(s("qk_ps"), 1)
                    pe.wait_ge(s("qkT"), i + 1)
                    wait(pe, s("ae"), i)
                    for t in range(QT):
                        m = pe.matmul(bank[:, 1, t * SQ:(t + 1) * SQ], self.qkT[:, u, t * P:(t + 1) * P],
                                      self.qkT[:, u, SQ:2 * SQ], start=True, stop=True)
                    m.then_inc(s("as_ps"), 1)

                def back(i, u):
                    pe.wait_ge(s("ae"), i + 1)
                    for k in range(QT):
                        for t in range(QT):
                            m = pe.transpose(bank[:, 2, (k * 2 + t) * P:(k * 2 + t + 1) * P],
                                             self.e[:, u, t, k * P:(k + 1) * P], ident[:, :])
                    m.then_inc(s("aeT_ps"), 1)
                    pe.wait_ge(s("aeT"), i + 1)
                    wait(pe, s("yb"), i)
                    for t in range(QT):
                        for k in range(QT):
                            m = pe.matmul(bank[:, 3, t * P:(t + 1) * P], self.eT[:, u, (k * 2 + t) * P:(k * 2 + t + 1) * P],
                                          self.qkv[:, u, 2, k, :], start=(k == 0), stop=(k == 1))
                    m.then_inc(s("ao_ps"), 1)
                    pe.wait_ge(s("yb"), i + 1)
                    wait(pe, s("yT"), i)
                    for t in range(QT):
                        m = pe.transpose(bank[:, 4, t * P:(t + 1) * P], self.yb[:, u, t, :], ident[:, :])
                    m.then_inc(s("yT_ps"), 1)

                piped(pe, front, back)
                pe.wait_ge(s("yT"), B)

            def dve(self, dve, before):
                s = self.s
                dve.wait_ge(x_done, before)
                norm_stats_dve("F2", x, xc, wide, stat, NT)
                dve.wait_ge(S("norm", "rstd"), NORMS.index(self.tag) + 1)
                dve.tensor_tensor(wide[:, :, :], xc[:, :, :], stat[:, 3, :].unsqueeze(2).to_broadcast([P, NT, P]),
                                  ALU.mult).then_inc(s("again"), 1)
                dve.wait_ge(s("again"), 1)
                c = self.chain = Count(s("chain"))

                def op(f, *args):
                    c.inc(f(*args))
                    c.wait(dve)

                self.op = op
                op(dve.tensor_reduce, stat[:, 0, :], wide[:, :, :], AX.X, ALU.add)
                op(dve.tensor_scalar, stat[:, 1, :], stat[:, 0, :], -1.0 / P, None, ALU.mult)
                dve.tensor_tensor(xc[:, :, :], wide[:, :, :], stat[:, 1, :].unsqueeze(2).to_broadcast([P, NT, P]),
                                  ALU.add).then_inc(s("centred2"), 1)
                dve.wait_ge(s("squares2"), 1)
                op(dve.tensor_reduce, stat[:, 2, :], wide[:, :, :], AX.X, ALU.add)
                dve.tensor_scalar(stat[:, 4, :], stat[:, 2, :], 1.0 / (P - 1), None, ALU.mult).then_inc(s("var2"), 1)
                dve.wait_ge(s("sd2"), 1)
                dve.tensor_scalar(stat[:, 6, :], stat[:, 5, :], LN_EPS, None, ALU.add).then_inc(s("var2"), 1)
                dve.wait_ge(s("sd2"), 2)
                op(dve.reciprocal, stat[:, 3, :], stat[:, 7, :])
                dve.tensor_tensor(xc[:, :, :], xc[:, :, :], stat[:, 3, :].unsqueeze(2).to_broadcast([P, NT, P]),
                                  ALU.mult).then_inc(s("xn"), 1)
                for q in range(8):
                    dve.wait_ge(s("flip_ps"), at("F2", "flip_ps") + q + 1)
                    dve.tensor_copy(xnT_all[:, q * 512:(q + 1) * 512], bank[:, q, :]).then_inc(s("flip"), 1)
                for n in range(4):
                    if n == 3:
                        self.attend_dve(dve)
                    self.route_dve(dve, n)
                    self.blocks_dve(dve, n)
                dve.wait_ge(s("gathered"), 16 * NT)
                op(dve.tensor_tensor, x[:, :, :], x[:, :, :], self.out, ALU.add)
                dve.sem_inc(x_done, 1)

            def route_dve(self, dve, n):
                s, op = self.s, self.op
                dve.wait_ge(s("nw"), 32 * (n + 1))
                nbn = self.nb[:, 0:255]
                op(dve.tensor_scalar, nbn, nbn, -1.0, None, ALU.mult)
                for tp in range(16):
                    dve.wait_ge(s("nodes"), n * 16 + tp + 1)
                    dve.tensor_tensor(self.bits[:, 2 * tp:2 * tp + 2, 0:255],
                                      bank[:, tp % 8, 0:510].rearrange("p (t n) -> p t n", t=2),
                                      nbn.unsqueeze(1).to_broadcast([P, 2, 255]), ALU.is_gt).then_inc(s("bits"), 1)
                dve.wait_ge(s("bits"), 16 * (n + 1))

                def split(dst, src, bit, w):
                    d = dst.rearrange("p t (j o) -> p t j o", o=2)
                    op(dve.tensor_tensor, d[:, :, :, 1], src, bit, ALU.mult)
                    op(dve.tensor_tensor, d[:, :, :, 0], src, d[:, :, :, 1], ALU.subtract)

                def ind(buf, w):
                    return buf[:, 0:NT * w].rearrange("p (t j) -> p t j", j=w)

                one = onesf[:, 0:1].unsqueeze(1).to_broadcast([P, NT, 1])
                split(ind(self.oa, 2), one, self.bits[:, :, 0:1], 1)
                src, dst = self.oa, self.ob
                for l in range(1, 5):
                    w = 1 << l
                    out = self.G if l == 4 else ind(dst, 2 * w)
                    split(out, ind(src, w), self.bits[:, :, w - 1:2 * w - 1], w)
                    src, dst = dst, src
                dve.engine_nop().then_inc(s("G"), 1) if False else dve.sem_inc(s("G"), 1)
                for l, (c0, w) in enumerate(((0, 1), (1, 2), (3, 4))):
                    n0 = 31 * w + (w - 1)
                    lev = self.bits[:, :, n0:n0 + 32 * w].rearrange("p t (g c) -> p t c g", c=w)
                    tm = self.tmp[:, 0:NT * w * 32].rearrange("p (t c g) -> p t c g", t=NT, c=w)
                    op(dve.tensor_tensor, tm, lev, self.G.unsqueeze(2).to_broadcast([P, NT, w, 32]), ALU.mult)
                    op(dve.tensor_reduce, self.sub[:, :, c0:c0 + w], tm, AX.X, ALU.add)
                if n:
                    dve.wait_ge(s("scattered"), 16 * NT * n)
                split(self.p1, one, self.sub[:, :, 0:1], 1)
                split(self.p2, self.p1, self.sub[:, :, 1:3], 2)
                split(self.xm[:, :, P:P + 8], self.p2, self.sub[:, :, 3:7], 4)
                dve.wait_ge(s("rank"), n + 1)
                op(dve.tensor_copy, self.totg, bank[:, 2:4, :].rearrange("p k (t g) -> p g (k t)", g=32))
                tf, inf = self.totg.rearrange("p g t -> p (g t)"), self.incl.rearrange("p g t -> p (g t)")
                op(dve.tensor_tensor_scan, inf, onesf[:, 0:1].to_broadcast([P, 1024]), tf, 0.0, ALU.mult, ALU.add)
                op(dve.tensor_tensor, tf, inf, tf, ALU.subtract)
                sm = self.sm
                op(dve.tensor_tensor, sm[:, 0, :], self.incl[:, :, NT - 1], self.totg[:, :, 0], ALU.subtract)
                op(dve.tensor_scalar, self.nbi, sm[:, 0, :], 127.0, None, ALU.add)
                op(dve.tensor_scalar, self.nbi, self.nbi, 7, None, ALU.logical_shift_right)
                op(dve.tensor_copy, sm[:, 1, :], self.nbi)
                op(dve.tensor_tensor_scan, sm[:, 2, :], onesf[:, 0:1].to_broadcast([P, 32]), sm[:, 1, :], 0.0,
                   ALU.mult, ALU.add)
                op(dve.tensor_tensor, sm[:, 3, :], sm[:, 2, :], sm[:, 1, :], ALU.subtract)
                op(dve.scalar_tensor_tensor, sm[:, 4, :], sm[:, 3, :], 128.0, self.totg[:, :, 0], ALU.mult, ALU.subtract)
                op(dve.tensor_tensor, self.incl, self.totg, sm[:, 4, :].unsqueeze(2).to_broadcast([P, 32, NT]), ALU.add)
                sl = ind(self.oa, 32)
                op(dve.tensor_tensor, sl, bank[:, 0:2, :].rearrange("p k (t g) -> p (k t) g", g=32),
                   self.incl.rearrange("p g t -> p t g"), ALU.add)
                op(dve.tensor_tensor, sl, sl, self.G, ALU.mult)
                op(dve.tensor_reduce, self.slotf, sl, AX.X, ALU.add)
                op(dve.tensor_copy, self.slot[:, n, :], self.slotf)
                cmp = self.tmp[0:1, 0:64 * 32].rearrange("p (j g) -> p j g", g=32)
                dve.wait_ge(s("const"), 16)
                op(dve.tensor_tensor, cmp, self.iota[0:1, :].unsqueeze(2).to_broadcast([1, 64, 32]),
                   sm[0:1, 2, :].unsqueeze(1).to_broadcast([1, 64, 32]), ALU.is_ge)
                op(dve.tensor_reduce, self.ob[0:1, 0:64], cmp, AX.X, ALU.add)
                dve.tensor_scalar(self.grp[0:1, :], self.ob[0:1, 0:64], 31.0, float(P), ALU.min, ALU.mult).then_inc(s("slots"), 1)
                dve.wait_ge(s("slots"), n + 1)

            def blocks_dve(self, dve, n):
                s = self.s

                def front(i, u):
                    dve.wait_ge(s("t1"), n * 16 + i + 1)
                    dve.tensor_copy(self.xT[:, u, :], bank[:, 0, :]).then_inc(s("xT"), 1)
                    mask = self.xin[:, u, :, P:P + 8].unsqueeze(3).to_broadcast([P, 4, 8, 16])
                    out = self.hm[:, u, :].rearrange("p (k l j) -> p k l j", k=4, l=8)
                    dve.wait_ge(s("act"), n * 16 + i + 1)
                    dve.tensor_tensor(out, self.gl[:, u, :].rearrange("p (k l j) -> p k l j", k=4, l=8), mask,
                                      ALU.mult).then_inc(s("hm"), 1)

                def back(i, u):
                    dve.wait_ge(s("y"), n * 16 + i + 1)
                    wait(dve, s("ys%d" % u), n * 128 + (i // 2 if isinstance(i, int) else (i - u) // 2) * 16)
                    dve.tensor_copy(self.yo[:, u, :, :].rearrange("p k d -> p (k d)"), bank[:, 4, :]).then_inc(s("yo"), 1)

                piped(dve, front, back)
                dve.wait_ge(s("ys0"), 128 * (n + 1))
                dve.wait_ge(s("ys1"), 128 * (n + 1))

            def attend_dve(self, dve):
                s = self.s
                sc = float(P) ** -0.5
                sm = self.small

                def front(i, u):
                    dve.wait_ge(s("qk_ps"), i + 1)
                    dve.tensor_copy(self.qkT[:, u, :], bank[:, 0, :]).then_inc(s("qkT"), 1)
                    c = Count(s("amax"), i * 2)
                    dve.wait_ge(s("as_ps"), i + 1)
                    c.inc(dve.tensor_reduce(sm[:, 0, u, :], bank[:, 1, :].rearrange("p (t k) -> p t k", t=QT), AX.X, ALU.max))
                    c.wait(dve)
                    c.inc(dve.tensor_scalar(sm[:, 1, u, :], sm[:, 0, u, :], -sc, None, ALU.mult))

                def back(i, u):
                    dve.wait_ge(s("aeT_ps"), i + 1)
                    dve.tensor_copy(self.eT[:, u, :], bank[:, 2, :]).then_inc(s("aeT"), 1)
                    dve.reciprocal(sm[:, 3, u, :], sm[:, 2, u, :]).then_inc(s("arec"), 1)
                    dve.wait_ge(s("arec"), i + 1)
                    dve.wait_ge(s("ao_ps"), i + 1)
                    for t in range(QT):
                        m = dve.scalar_tensor_tensor(self.yb[:, u, t, :], bank[:, 3, t * P:(t + 1) * P],
                                                     sm[:, 3, u, t:t + 1],
                                                     xc[:, ds(i * 2 + t, 1), :].rearrange("p o d -> p (o d)"), ALU.mult, ALU.add)
                    m.then_inc(s("yb"), 1)
                    dve.wait_ge(s("yb"), i + 1)
                    dve.tensor_tensor(x[:, ds(i * 2, 2), :], x[:, ds(i * 2, 2), :], self.yb[:, u, :, :], ALU.add).then_inc(s("xy"), 1)
                    dve.tensor_copy(self.xm[:, ds(i * 2, 2), 0:P], self.yb[:, u, :, :]).then_inc(s("xy"), 1)

                piped(dve, front, back)
                dve.wait_ge(s("xy"), 2 * B)
                dve.wait_ge(s("yT"), B)

            def act(self, act, before):
                s = self.s
                act.wait_ge(x_done, before)
                norm_stats_act("F2", xc, wide, stat, NT)
                act.wait_ge(s("centred2"), 1)
                act.activation(wide[:, :, :], xc[:, :, :], ACT.Square).then_inc(s("squares2"), 1)
                act.wait_ge(s("var2"), 1)
                act.activation(stat[:, 5, :], stat[:, 4, :], ACT.Sqrt).then_inc(s("sd2"), 1)
                act.wait_ge(s("var2"), 2)
                act.activation(stat[:, 7, :], stat[:, 6, :], ACT.Sqrt).then_inc(s("sd2"), 1)
                for n in range(4):
                    if n == 3:
                        self.attend_act(act)

                    def front(i, u):
                        act.wait_ge(s("t1"), n * 16 + i + 1)
                        if n == 0 and isinstance(i, int) and i == 0:
                            act.wait_ge(s("slots"), 1)
                        act.activation(self.mT[0:8, u, :], bank[0:8, 1, :], ACT.Identity).then_inc(s("mT"), 1)
                        act.wait_ge(s("h"), n * 16 + i + 1)
                        act.activation(self.gl[:, u, :], bank[:, 2, :], ACT.Gelu if n == 3 else ACT.Relu).then_inc(s("act"), 1)

                    def back(i, u):
                        act.wait_ge(s("t2"), n * 16 + i + 1)
                        act.activation(self.hT[:, u, :], bank[:, 3, :], ACT.Identity).then_inc(s("hT"), 1)

                    piped(act, front, back)

            def attend_act(self, act):
                s = self.s
                sm = self.small

                def front(i, u):
                    act.wait_ge(s("amax"), i * 2 + 2)
                    for t in range(QT):
                        m = act.activation(self.e[:, u, t, :], bank[:, 1, t * SQ:(t + 1) * SQ], ACT.Exp,
                                           bias=sm[:, 1, u, t:t + 1], scale=float(P) ** -0.5,
                                           accum_out=sm[:, 2, u, t:t + 1])
                    m.then_inc(s("ae"), 1)

                def back(i, u):
                    act.wait_ge(s("yT_ps"), i + 1)
                    act.activation(xnT_all[:, ds(i * SQ, SQ)], bank[:, 4, 0:SQ], ACT.Identity).then_inc(s("yT"), 1)

                piped(act, front, back)

            def pool(self, pool, before):
                s = self.s
                pool.wait_ge(x_done, before)
                pool.memset(self.tri, 1.0).then_inc(s("tri"), 1)
                pool.memset(self.oneb, 1.0).then_inc(s("tri"), 1)
                pool.wait_ge(s("tri"), 2)
                pool.affine_select(self.tri, self.tri, [[1, P]], ALU.is_gt, 0.0, base=0,
                                   channel_multiplier=-1).then_inc(s("tri"), 1)
                pool.wait_ge(s("xn"), at("F2", "xn") + 1)
                pool.tensor_copy(self.xm[:, :, 0:P], xc[:, :, :]).then_inc(s("xm"), 1)
                pool.wait_ge(s("xm"), 1)
                pool.wait_ge(s("zeroed"), 16 * 16)
                xs = A["xs"].rearrange("k p w -> (k p) w")

                def gather(dst, n, t, done):
                    ys = A["ys%d" % n].rearrange("k p w -> (k p) w")
                    pool.indirect_dma_start(dst, None, ys, bass.IndirectOffsetOnAxis(ap=self.slot[:, n, t:t + 1], axis=0)).then_inc(done, 16)

                for n in range(4):
                    if n == 3:
                        pool.wait_ge(s("ys0"), 128 * 3)
                        pool.wait_ge(s("ys1"), 128 * 3)
                        for i in range(B):
                            if i >= 2:
                                pool.wait_ge(s("ao_ps"), i - 1)
                            for m in range(3):
                                for t in range(QT):
                                    gather(self.qkv[:, i % 2, m, t, :], m, 2 * i + t, s("qkv%d" % (i % 2)))
                    pool.wait_ge(s("slots"), n + 1)
                    for t in range(NT):
                        pool.indirect_dma_start(xs, bass.IndirectOffsetOnAxis(ap=self.slot[:, n, t:t + 1], axis=0),
                                                self.xm[:, t, :], None).then_inc(s("scattered"), 16)
                pool.wait_ge(s("ys0"), 128 * 4)
                pool.wait_ge(s("ys1"), 128 * 4)
                for t in range(NT):
                    gather(self.out[:, t, :], 3, t, s("gathered"))

        FEED = {"F0": TopTwo(), "F1": SoftSlots(), "F2": Trees(), "F3": ExpertChoice()}

        cc = prob[:, 0, :, :].rearrange("p a b -> p (a b)")[:, 0:1024].rearrange("p (t e) -> p t e", t=8)
        csq = prob[:, 1, :, :].rearrange("p a b -> p (a b)")[:, 0:1024].rearrange("p (t e) -> p t e", t=8)

        wflat = wide[:, :, :].rearrange("p t e -> p (t e)")
        m0_raw = wflat[:, 0:1024].bitcast(I32)
        m1_raw = wflat[:, 1024:1152].bitcast(I32).rearrange("p (t k) -> p t k", t=QT)
        m2_raw = wflat[:, 1152:1408].bitcast(U8)
        mf0 = wflat[:, 1408:2432].rearrange("p (b k) -> p b k", b=B)
        mf2 = wflat[:, 2432:3456].rearrange("p (b k) -> p b k", b=B)
        mf1 = wflat[:, 3456:3584].rearrange("p (t k) -> p t k", t=QT)
        al = wflat[:, 3584:3584 + 64]
        diag = wflat[:, 3712:3968].rearrange("p (t q) -> p t q", t=QT)

        block = ctx.enter_context(nc.Block())

        @block.sync
        def _(sp):
            def load(dst, src):
                sp.dma_start(dst, src).then_inc(loaded, 16)

            load(x[:, :, :], A["x"].rearrange("b (t p) d -> p (b t) d", p=P))
            load(ident[:, :], A["ident"])
            load(headmask[:, :], A["headmask"])
            load(ctxT[:, :, :], A["ctxT"])
            load(cols[:, :], A["cols"])
            load(rows[:, :, :].rearrange("p n d -> p (n d)"), A["rows"].rearrange("n d -> (n d)").partition_broadcast(P))
            load(wx[:, :, :, :].rearrange("p l m e -> p (l m e)"), A["wx"])
            load(m0_raw, A["itok"].rearrange("b k -> (b k)").partition_broadcast(P))
            load(m1_raw, A["mask_qk"].rearrange("(t p) k -> p t k", p=P))
            load(m2_raw, A["mask_bk"].rearrange("b k -> (b k)").partition_broadcast(P))
            sp.wait_ge(cast, 3)
            for k in range(16):
                sp.dma_start(A["xs"][4 * k:4 * k + 4, :, :].rearrange("k p w -> p k w"),
                             zeros[:, :].rearrange("p (k w) -> p k w", k=4)).then_inc(S("F2", "zeroed"), 16)
            for n, stage in enumerate(PLAN):
                if stage == "X2":
                    sp.wait_ge(x_done, n + 1)
                    sp.dma_start(cx, A["ctx"].rearrange("(t p) d -> p t d", p=P)).then_inc(S("X", "cx"), 16)
                elif stage[0] == "F":
                    FEED[stage].sp(sp, n + 1)
            sp.wait_ge(x_done, len(PLAN) + 1)
            sp.dma_start(A["out"].rearrange("b (t p) d -> p (b t) d", p=P), x[:, :, :]).then_inc(stored, 16)
            sp.wait_ge(stored, 16)

        def prepare_dve(dve):
            dve.memset(row0[:, :], 0.0).then_inc(cast, 1)
            dve.memset(onesf[:, :], 1.0).then_inc(cast, 1)
            dve.memset(zeros[:, :], 0.0).then_inc(cast, 1)
            dve.wait_ge(cast, 3)
            dve.memset(row0[0:1, :], 1.0).then_inc(cast, 1)
            dve.wait_ge(loaded, 16 * LOADS)
            dve.tensor_copy(identb[:, :], ident[:, :]).then_inc(cast, 1)
            c = Count(masks)

            def op(f, *args):
                c.inc(f(*args))
                c.wait(dve)

            op(dve.tensor_scalar, mf0.rearrange("p b k -> p (b k)"), m0_raw, 0.0, None, ALU.is_equal)
            op(dve.tensor_reduce, al[:, 0:B], mf0, AX.X, ALU.min)
            op(dve.tensor_scalar, keep0[:, :], al[:, 0:B], -1.0, 1.0, ALU.mult, ALU.add)
            op(dve.tensor_tensor, mf0, mf0, keep0[:, :].unsqueeze(2).to_broadcast([P, B, SK]), ALU.mult)
            op(dve.tensor_scalar, bias0[:, :, :], mf0, MASKED, None, ALU.mult)
            op(dve.tensor_copy, mf2.rearrange("p b k -> p (b k)"), m2_raw)
            op(dve.tensor_reduce, al[:, 16:32], mf2, AX.X, ALU.min)
            op(dve.tensor_tensor, mf2[:, :, 0], mf2[:, :, 0], al[:, 16:32], ALU.subtract)
            op(dve.tensor_scalar, bias2[:, :, :], mf2, MASKED, None, ALU.mult)
            op(dve.tensor_scalar, mf1, m1_raw, 0.0, None, ALU.is_equal)
            op(dve.tensor_reduce, al[:, 32:34], mf1, AX.X, ALU.min)
            op(dve.tensor_scalar, al[:, 34:36], al[:, 32:34], -1.0, 1.0, ALU.mult, ALU.add)
            op(dve.tensor_tensor, mf1, mf1, al[:, 34:36].unsqueeze(2).to_broadcast([P, QT, SK]), ALU.mult)
            op(dve.tensor_scalar, bias1[:, :, :], mf1, MASKED, None, ALU.mult)
            for t in range(QT):
                op(dve.tensor_scalar, diag[:, t, :], ident[:, :], al[:, 34 + t:35 + t], None, ALU.mult)
            dve.sem_inc(masks_ps, 1)
            dve.wait_ge(masks_ps, 2)
            dve.tensor_copy(keep1[:, :], bank[:, 0, 0:SQ]).then_inc(masks_ps, 1)
            dve.wait_ge(masks_ps, 3)
            dve.sem_inc(x_done, 1)

        @block.tensor
        def _(pe):
            pe.wait_ge(masks_ps, 1)
            for t in range(QT):
                m = pe.matmul(bank[:, 0, t * P:(t + 1) * P], onesf[:, :], diag[:, t, :], start=True, stop=True,
                              skip_group_check=True)
            m.then_inc(masks_ps, 1)
            for n, stage in enumerate(PLAN):
                if stage[0] == "X":
                    attn_pe(Attn(int(stage[1])), n + 1)
                else:
                    FEED[stage].pe(pe, n + 1)

        @block.vector
        def _(dve):
            prepare_dve(dve)
            for n, stage in enumerate(PLAN):
                if stage[0] == "X":
                    attn_dve(Attn(int(stage[1])), n + 1)
                else:
                    FEED[stage].dve(dve, n + 1)

        @block.scalar
        def _(act):
            act.wait_ge(loaded, 16 * LOADS)
            for n, stage in enumerate(PLAN):
                if stage[0] == "X":
                    attn_act(Attn(int(stage[1])), n + 1)
                else:
                    FEED[stage].act(act, n + 1)

        @block.gpsimd
        def _(pool):
            pool.wait_ge(loaded, 16 * LOADS)
            for n, stage in enumerate(PLAN):
                if stage[0] == "X":
                    attn_pool(Attn(int(stage[1])), n + 1)
                else:
                    FEED[stage].pool(pool, n + 1)


def _in_layout(inputs):
    i = {k: np.asarray(v) for k, v in inputs.items()}
    f = np.float32
    arrays = {"x": i["x"], "itok": i["itok_BxS2_0_99"]}
    arrays["mask_qk"] = i["mask_1x1xSxS2_ik0"].reshape(SQ, SK)
    arrays["mask_bk"] = i["mask_BxS2_bk0"]
    ctx = i["ctx_1024"].reshape(B * SK, P)
    arrays["ctx"] = ctx
    arrays["ctxT"] = np.repeat(ctx.T.reshape(P, B, 1, SK), 2, 2)
    arrays["ident"] = np.eye(P, dtype=f)
    arrays["headmask"] = ((np.arange(P)[:, None] // HD) % HG == np.arange(HG)[None, :]).astype(f)
    X = {0: "L0_xattn_", 1: "L1_xattn_", 2: "L2_xattn_", 3: "L3_xattn_"}
    mats = []
    for L in range(4):
        for m in "qkvo":
            w = i[X[L] + ("w" if L == 1 else "W") + m]
            mats.append(w.T if L else w)
    arrays["wx"] = np.stack(mats, 1).reshape(P, 16 * P)
    arrays["tri8"] = np.broadcast_to(np.tril(np.ones((8, 8), f), -1).reshape(1, 64), (P, 64))
    arrays["F0_wg"] = i["L0_ffn_Wg"]
    arrays["F0_w11"] = i["L0_ffn_W11"].transpose(1, 0, 2).reshape(P, -1)
    arrays["F0_w12"] = i["L0_ffn_W12"].transpose(1, 0, 2).reshape(P, -1)
    arrays["F0_w2"] = i["L0_ffn_W2"].reshape(8, 2, P, P).transpose(2, 0, 1, 3).reshape(P, -1)

    arrays["F3_rw"] = i["L3_ffn_router_w"]
    arrays["F3_rb"] = i["L3_ffn_router_b"]
    arrays["F3_w1"] = i["L3_ffn_w1"].transpose(1, 0, 2).reshape(P, -1)
    arrays["F3_b1"] = i["L3_ffn_b1"].reshape(32, P).T
    arrays["F3_w2"] = i["L3_ffn_w2"].reshape(8, 4, P, P).transpose(2, 0, 1, 3).reshape(P, -1)
    arrays["F3_b2"] = i["L3_ffn_b2"]
    arrays["bits"] = (1 << np.arange(29, -1, -1)).astype(np.int32)

    arrays["F1_phi"] = i["L1_ffn_phi"].reshape(P, -1)
    arrays["F1_w"] = i["L1_ffn_W"].reshape(16, 4, P, P).transpose(0, 2, 1, 3).reshape(16, P, 4 * P)
    arrays["F1_b"] = i["L1_ffn_b"].T

    arrays["iota64"] = np.arange(64, dtype=f)
    T = ["L2_ffn_%s_" % t for t in "qkvf"]
    arrays["F2_nw"] = np.stack([i[t + "nw"].T for t in T])
    arrays["F2_nb"] = np.stack([i[t + "nb"] for t in T])
    arrays["F2_w1"] = np.stack([i[t + "w1"].transpose(1, 0, 2).reshape(P, -1) for t in T])
    arrays["F2_w2"] = np.stack([i[t + "w2"].reshape(32, P, P).transpose(1, 0, 2).reshape(P, -1) for t in T])
    b1 = np.zeros((4, 8, 32, 8, 16), f)
    for n, t in enumerate(T):
        for l in range(8):
            b1[n, l, :, l, :] = i[t + "b1"].reshape(32, 8, 16)[:, l, :]
    arrays["F2_b1"] = b1.reshape(4, 8, -1)
    arrays["F2_b2"] = np.stack([i[t + "b2"].reshape(32, 8, P).transpose(1, 0, 2).reshape(8, -1) for t in T])

    def vec(name):
        if name[:2] in ("qn", "cn"):
            return i["L2_xattn_" + name]
        return i[name[:2] + "_xattn_" + name[3:]]
    arrays["cols"] = np.stack([vec(n) for n in COLS], 1)
    arrays["rows"] = np.stack([vec(n) for n in ROWS], 0)
    return {k: np.ascontiguousarray(v) for k, v in arrays.items()}


def kernel(**inputs):
    import concourse.bacc as _bacc
    from concourse.bass_utils import run_bass_kernel_spmd as _run

    nc = _bacc.Bacc("TRN2", target_bir_lowering=False, num_devices=1)
    arrays = _in_layout(inputs)
    A = {}
    for name, a in arrays.items():
        A[name] = nc.dram_tensor(f"in_{name}", a.shape, mybir.dt.from_np(a.dtype), kind="ExternalInput").ap()
    A["out"] = nc.dram_tensor("out_x", (B, SQ, P), F32, kind="ExternalOutput").ap()
    A["y_slots"] = nc.dram_tensor("y_slots", (B, P, 16, P), F32, kind="Internal").ap()
    A["xs"] = nc.dram_tensor("xs", (64, P, P + 8), F32, kind="Internal").ap()
    for n in range(4):
        A["ys%d" % n] = nc.dram_tensor("ys%d" % n, (64, P, P), F32, kind="Internal").ap()
    build(nc, A)
    r = _run(nc, [{f"in_{k}": a for k, a in arrays.items()}], core_ids=[0])
    return r.results[0]["out_x"]
```

```python
from contextlib import ExitStack

import numpy as np

import concourse.bass as bass
from concourse import mybir

ALU = mybir.AluOpType
ACT = mybir.ActivationFunctionType
AX = mybir.AxisListType
F32 = mybir.dt.float32
BF16 = mybir.dt.bfloat16
I32 = mybir.dt.int32
U8 = mybir.dt.uint8
ds = bass.ds

P = 128
B = 16
SQ = 256
QT = SQ // P
NT = B * QT
SK = 64
NH = 16
HD = P // NH
NG = 4
HG = NH // NG
ARENA = 33300
LN_EPS = 1e-5
MASKED = -1e30
PLAN = ["X0", "F0", "X1", "F1", "X2", "F2", "X3", "F3"]

COLS = ["L1_bq", "L1_bk", "L2_bq", "L2_bk", "L3_bq", "L3_bk", "qn_w", "qn_b", "cn_w", "cn_b"]
ROWS = ["L0_bo", "L1_bv", "L1_bo", "L2_bv", "L2_bo", "L3_bv", "L3_bo"]


class Count:

    def __init__(self, sem, base=0):
        self.sem, self.n = sem, base

    def inc(self, instruction):
        self.n = self.n + 1
        return instruction.then_inc(self.sem, 1)

    def wait(self, eng):
        eng.wait_ge(self.sem, self.n)


def wait(eng, sem, value):
    if not isinstance(value, int) or value > 0:
        eng.wait_ge(sem, value)


def turns(eng, turn):
    turn(0, 0, B - 1)
    with eng.Fori(0, B // 2 - 2) as j:
        turn(j * 2 + 1, 1, 2)
        turn(j * 2 + 2, 0, 2)
    for i in range(B - 3, B):
        turn(i, i % 2, B - 1 - i)


def turns4(eng, turn):
    turn(0, 0, 15)
    with eng.Fori(0, 3) as j:
        for q in range(1, 5):
            turn(j * 4 + q, q % 4, 3)
    for i in range(13, 16):
        turn(i, i % 4, 15 - i)


def part(i, u, n):
    return i // n if isinstance(i, int) else (i - u) // n


def piped(eng, front, back):
    front(0, 0)
    with eng.Fori(0, B // 2 - 1) as j:
        front(j * 2 + 1, 1)
        back(j * 2, 0)
        front(j * 2 + 2, 0)
        back(j * 2 + 1, 1)
    front(B - 1, 1)
    back(B - 2, 0)
    back(B - 1, 1)


def build(nc, A):
    ctx = ExitStack()
    with ctx:
        def sb(name, shape, dt=F32):
            return ctx.enter_context(nc.sbuf_tensor(name, shape, dt))

        def sem(name):
            return ctx.enter_context(nc.semaphore(name))

        x = sb("x", [P, NT, P])
        xc = sb("xc", [P, NT, P])
        wide = sb("wide", [P, NT, P])
        ident = sb("ident", [P, P])
        identb = sb("identb", [P, P], BF16)
        headmask = sb("headmask", [P, NH])
        row0 = sb("row0", [P, P], BF16)
        onesf = sb("onesf", [P, P])
        ctxT = sb("ctxT", [P, B, 2, SK])
        cols = sb("cols", [P, len(COLS)])
        rows = sb("rows", [P, len(ROWS), P])
        wx = sb("wx", [P, 4, 4, P])
        stat = sb("stat", [P, 8, NT])
        bias0 = sb("bias0", [P, B, SK], BF16)
        bias2 = sb("bias2", [P, B, SK], BF16)
        bias1 = sb("bias1", [P, QT, SK], BF16)
        keep0 = sb("keep0", [P, B])
        keep1 = sb("keep1", [P, QT * P])

        zeros = sb("zeros", [P, 4 * (P + 8)])
        arena = sb("arena", [P, ARENA])

        class Carve:

            def __init__(self, at=0):
                self.at = at

            def __call__(self, *shape, dt=F32):
                n = 1
                for d in shape:
                    n *= d
                words = n if dt in (F32, I32) else (n + 1) // 2
                v = arena[:, self.at:self.at + words]
                self.at += words
                assert self.at <= ARENA, self.at
                if dt != F32:
                    v = v.bitcast(dt)
                names = "abcdef"[:len(shape)]
                if len(shape) > 1:
                    v = v.rearrange(f"p ({' '.join(names)}) -> p {' '.join(names)}",
                                    **{c: d for c, d in zip(names, shape)})
                return v

        carve = Carve()
        kT = carve(B, SK)
        kblk = carve(2, NH, SK)
        v2 = carve(B, NH // 2, 2 * (HD + 1))
        xn = carve(2, QT, P)
        xnT = carve(2, SQ)
        qT = carve(2, SQ)
        prob = carve(2, NG, QT * HG * SK)
        pT = carve(2, 4 * P)
        mx = carve(2, NG * QT * HG)
        rs = carve(2, QT * NH)
        on = carve(2, QT, P)
        oT = carve(2, SQ)
        cx = carve(B * SK // P, P)
        cnT = carve(B, 2, SK)
        stat_c = carve(6, 8)

        bank = ctx.enter_context(nc.psum_tensor("bank", [P, 8, 512], F32))

        def col(name):
            n = COLS.index(name)
            return cols[:, n:n + 1]

        def row(name):
            return rows[:, ROWS.index(name), :]

        loaded = sem("loaded")
        LOADS = 10
        stored = sem("stored")
        x_done = sem("x_done")
        cast = sem("cast")
        masks = sem("masks")
        masks_ps = sem("masks_ps")
        SEMS = {}

        SHARED = {("F3", w): ("F0", v) for w, v in
                  dict(loaded=80, xn=B, flip_ps=B, flip=B, router=1, up=128, x_add=64, down=128, less_max=1,
                       exp=1).items()}
        SHARED.update({("F2", w): ("F1", v) for w, v in dict(xn=1, flip_ps=8, flip=8, x_add=NT, exp=4 * NT).items()})

        def at(layer, what):
            first, left = SHARED.get((layer, what), (None, 0))
            return left if first in PLAN else 0

        def S(layer, what):
            layer = SHARED.get((layer, what), (layer, 0))[0]
            name = f"{layer}_{what}"
            if name not in SEMS:
                SEMS[name] = sem(name)
            return SEMS[name]

        NORMS = [t for p in PLAN for t in (["X2c", "X2", "X2q"] if p == "X2" else [p])]

        def norm_stats_dve(tag, src, dst, squares, st, tiles):
            dve = nc.vector
            k = NORMS.index(tag)
            c = Count(S("norm", "ln"), 3 * k)
            c.inc(dve.tensor_reduce(st[:, 0, 0:tiles], src[:, :, :], AX.X, ALU.add))
            c.wait(dve)
            c.inc(dve.tensor_scalar(st[:, 1, 0:tiles], st[:, 0, 0:tiles], -1.0 / P, None, ALU.mult))
            c.wait(dve)
            dve.tensor_tensor(dst[:, :, :], src[:, :, :],
                              st[:, 1, 0:tiles].unsqueeze(2).to_broadcast([P, tiles, P]),
                              ALU.add).then_inc(S("norm", "centred"), 1)
            dve.wait_ge(S("norm", "squares"), k + 1)
            c.inc(dve.tensor_reduce(st[:, 2, 0:tiles], squares[:, :, :], AX.X, ALU.add))
            c.wait(dve)
            dve.tensor_scalar(st[:, 4, 0:tiles], st[:, 2, 0:tiles], 1.0 / P, LN_EPS, ALU.mult,
                              ALU.add).then_inc(S("norm", "var"), 1)
            dve.wait_ge(S("norm", "sd"), k + 1)
            dve.reciprocal(st[:, 3, 0:tiles], st[:, 5, 0:tiles]).then_inc(S("norm", "rstd"), 1)

        def norm_stats_act(tag, dst, squares, st, tiles):
            act = nc.scalar
            k = NORMS.index(tag)
            act.wait_ge(S("norm", "centred"), k + 1)
            act.activation(squares[:, :, :], dst[:, :, :], ACT.Square).then_inc(S("norm", "squares"), 1)
            act.wait_ge(S("norm", "var"), k + 1)
            act.activation(st[:, 5, 0:tiles], st[:, 4, 0:tiles], ACT.Sqrt).then_inc(S("norm", "sd"), 1)

        class Attn:
            def __init__(self, layer):
                self.layer = layer
                self.tag = f"X{layer}"
                self.scale = float(HD) ** -0.5
                self.masked = layer != 3
                self.turn = [p for p in PLAN if p[0] == "X"].index(self.tag)

            def at(self, what):
                return self.turn * PER_LAYER.get(what, 0)

        PER_LAYER = {"k_ps": 1, "v_ps": 1, "v2_zero": 1, "bo": 1, "kT": 3, "v2": 10, "xn": B, "xnT": B, "xnT_ps": B,
                     "q_ps": B, "qT": B, "kblk": B, "exp": B, "rs": B, "on": B, "oT": B, "x_add": B, "dve": 2 * B,
                     "scores": 2 * B, "sub": 2 * B, "pT": 4 * B, "values": 4 * B, "ring_ps": 6 * B}

        def s(a, what):
            return S("X", what)

        def attn_pe(a, before):
            pe = nc.tensor
            L = a.layer
            cT = ctxT
            pe.wait_ge(x_done, before)
            if L == 2:
                pe.wait_ge(s(a, "cn"), a.at("cn") + 1)
                for t in range(B * SK // P):
                    m = pe.transpose(bank[:, 3 + t // 4, (t % 4) * P:(t % 4 + 1) * P], wide[:, t, :], ident[:, :])
                m.then_inc(s(a, "cnT_ps"), 1)
                pe.wait_ge(s(a, "cnT"), a.at("cnT") + 4)
                cT = cnT
            for h in range(2):
                m = pe.matmul(bank[:, 1 + h, :], wx[:, L, 1, :], cT[:, 8 * h:8 * h + 8, 0, :],
                              start=True, stop=True)
            m.then_inc(s(a, "k_ps"), 1)
            for b in range(B):
                lhs = cT[:, b, :, :].rearrange("p c k -> p (c k)")
                m = pe.matmul(bank[:, 3 + b // 4, (b % 4) * P:(b % 4 + 1) * P], lhs, wx[:, L, 2, :],
                              start=True, stop=True)
            m.then_inc(s(a, "v_ps"), 1)

            pe.wait_ge(s(a, "v2"), a.at("v2") + 10)

            def flip(i, u):
                pe.wait_ge(s(a, "xn"), a.at("xn") + i + 1)
                wait(pe, s(a, "qT"), a.at("qT") + i)
                for t in range(QT):
                    m = pe.transpose(bank[:, 0, t * P:(t + 1) * P], xn[:, u, t, :], ident[:, :])
                m.then_inc(s(a, "xnT_ps"), 1)

            def queries(i, u):
                pe.wait_ge(s(a, "xnT"), a.at("xnT") + i + 1)
                pe.matmul(bank[:, 0, SQ:2 * SQ], wx[:, L, 0, :], xnT[:, u, :],
                          start=True, stop=True).then_inc(s(a, "q_ps"), 1)

            def scores(i, u, half):
                if half == 0:
                    pe.wait_ge(s(a, "qT"), a.at("qT") + i + 1)
                    pe.wait_ge(s(a, "kblk"), a.at("kblk") + i + 1)
                wait(pe, s(a, "sub"), a.at("sub") + i * 2 + half - 1)
                for g in (2 * half, 2 * half + 1) if a.masked else ():
                    if L == 1:
                        for t in range(QT):
                            pe.matmul(bank[:, 1 + g, t * SQ:(t + 1) * SQ], identb[:, :],
                                      bias1[:, t, :].unsqueeze(1).to_broadcast([P, HG, SK]),
                                      start=(t == 0), stop=False, skip_group_check=True)
                    else:
                        bias = (bias0 if L == 0 else bias2)[:, ds(i, 1), :]
                        pe.matmul(bank[:, 1 + g, :], row0[:, :], bias.to_broadcast([P, QT * HG, SK]),
                                  start=True, stop=False, skip_group_check=True)
                for g in (2 * half, 2 * half + 1):
                    for t in range(QT):
                        m = pe.matmul(bank[:, 1 + g, t * SQ:(t + 1) * SQ], qT[:, u, t * P:(t + 1) * P],
                                      kblk[:, u, HG * g:HG * g + HG, :].rearrange("p j k -> p (j k)"),
                                      start=(not a.masked), stop=True, skip_group_check=True)
                m.then_inc(s(a, "scores"), 1)

            def lot(i, u, n):
                t, r = n // 2, n % 2
                if n == 0:
                    pe.wait_ge(s(a, "exp"), a.at("exp") + i + 1)
                    wait(pe, s(a, "oT"), a.at("oT") + i)
                elif n == 1:
                    wait(pe, s(a, "x_add"), a.at("x_add") + i)
                else:
                    pe.wait_ge(s(a, "pT"), a.at("pT") + i * 4 + n - 1)
                for q in range(4):
                    p = 4 * r + q
                    g, jp = p // 2, p % 2
                    src = prob[:, u, g, (t * 2 + jp) * P:(t * 2 + jp + 1) * P]
                    m = pe.transpose(bank[:, 5 + n % 2, q * P:(q + 1) * P], src, ident[:, :])
                m.then_inc(s(a, "ring_ps"), 1)

            def values(i, u, n):
                t, r = n // 2, n % 2
                pe.wait_ge(s(a, "pT"), a.at("pT") + i * 4 + n + 1)
                if n == 0:
                    wait(pe, s(a, "on"), a.at("on") + i)
                for q in range(4):
                    p = 4 * r + q
                    c0 = (t * (NH // 2) + p) * 18
                    m = pe.matmul(bank[:, 7, c0:c0 + 18], pT[:, n % 2, q * P:(q + 1) * P],
                                  v2[:, ds(i, 1), p, :].rearrange("p o c -> p (o c)"), start=True, stop=True,
                                  skip_group_check=True)
                m.then_inc(s(a, "values"), 1)

            def heads_out(i, u):
                pe.wait_ge(s(a, "on"), a.at("on") + i + 1)
                for t in range(QT):
                    m = pe.transpose(bank[:, 5, t * P:(t + 1) * P], on[:, u, t, :], ident[:, :])
                m.then_inc(s(a, "ring_ps"), 1)

            def project(i, u):
                pe.wait_ge(s(a, "oT"), a.at("oT") + i + 1)
                for t in range(QT):
                    m = pe.matmul(bank[:, 6, t * P:(t + 1) * P], oT[:, u, t * P:(t + 1) * P], wx[:, L, 3, :],
                                  start=True, stop=True)
                m.then_inc(s(a, "ring_ps"), 1)

            def turn(i, u, rest):
                first = isinstance(i, int) and i == 0
                if rest >= 1:
                    scores(i + 1, 1 - u, 0)
                if not first:
                    heads_out(i - 1, 1 - u)
                if rest >= 1:
                    scores(i + 1, 1 - u, 1)
                if not first:
                    project(i - 1, 1 - u)
                if rest >= 2:
                    flip(i + 2, u)
                lot(i, u, 0)
                lot(i, u, 1)
                values(i, u, 0)
                lot(i, u, 2)
                if rest >= 2:
                    queries(i + 2, u)
                values(i, u, 1)
                lot(i, u, 3)
                values(i, u, 2)
                values(i, u, 3)

            flip(0, 0)
            queries(0, 0)
            scores(0, 0, 0)
            scores(0, 0, 1)
            flip(1, 1)
            queries(1, 1)
            turns(pe, turn)
            heads_out(B - 1, 1)
            project(B - 1, 1)

        def attn_dve(a, before):
            dve = nc.vector
            dve.wait_ge(x_done, before)
            L = a.layer
            if L == 2:
                dve.wait_ge(s(a, "cx"), a.at("cx") + 16)
                norm_stats_dve("X2c", cx, cc, csq, stat_c, B * SK // P)
                dve.wait_ge(S("norm", "rstd"), NORMS.index("X2c") + 1)
                dve.tensor_tensor(wide[:, 0:B * SK // P, :], cc[:, :, :],
                                  stat_c[:, 3, 0:8].unsqueeze(2).to_broadcast([P, 8, P]), ALU.mult).then_inc(s(a, "cn"), 1)
                dve.wait_ge(s(a, "cnT_ps"), a.at("cnT_ps") + 1)
                for h in range(2):
                    for c in range(2):
                        dve.tensor_scalar(cnT[:, 8 * h:8 * h + 8, c, :],
                                          bank[:, 3 + h, :].rearrange("p (b k) -> p b k", b=8),
                                          col("cn_w"), col("cn_b"), ALU.mult, ALU.add).then_inc(s(a, "cnT"), 1)
            norm_stats_dve(a.tag, x, xc, wide, stat, NT)
            if L == 2:
                dve.wait_ge(S("norm", "rstd"), NORMS.index(a.tag) + 1)
                dve.tensor_tensor(wide[:, :, :], xc[:, :, :],
                                  stat[:, 3, :].unsqueeze(2).to_broadcast([P, NT, P]), ALU.mult).then_inc(s(a, "again"), 1)
                dve.wait_ge(s(a, "again"), a.at("again") + 1)
                norm_stats_dve("X2q", wide, xc, wide, stat, NT)
            dve.wait_ge(s(a, "v_ps"), a.at("v_ps") + 1)
            dve.wait_ge(s(a, "v2_zero"), a.at("v2_zero") + 1)
            dve.memset(v2[0:64, :, :, HD:HD + 1], 1.0).then_inc(s(a, "v2"), 1)
            dve.memset(v2[64:128, :, :, 2 * HD + 1:2 * HD + 2], 1.0).then_inc(s(a, "v2"), 1)
            for q in range(4):
                for h in range(2):
                    src = bank[64 * h:64 * h + 64, 3 + q, :].rearrange("k (b p h d) -> k b p h d", b=4, p=8, h=2)[:, :, :, h, :]
                    dst = v2[64 * h:64 * h + 64, 4 * q:4 * q + 4, :, 9 * h:9 * h + 8]
                    if L == 0:
                        dve.tensor_copy(dst, src).then_inc(s(a, "v2"), 1)
                    else:
                        bv = row(f"L{L}_bv")[64 * h:64 * h + 64, :].rearrange("k (p h d) -> k p h d", p=8, h=2)[:, :, h, :]
                        dve.tensor_tensor(dst, src, bv.unsqueeze(1).to_broadcast([64, 4, 8, 8]),
                                          ALU.add).then_inc(s(a, "v2"), 1)
            if L == 0:
                dve.wait_ge(s(a, "kT"), a.at("kT") + 2)
                dve.tensor_tensor(kT[:, :, :], kT[:, :, :], keep0[:, :].unsqueeze(2).to_broadcast([P, B, SK]),
                                  ALU.mult).then_inc(s(a, "kT"), 1)

            def flip(i, u):
                dve.wait_ge(s(a, "xnT_ps"), a.at("xnT_ps") + i + 1)
                if L == 2:
                    dve.tensor_scalar(xnT[:, u, :], bank[:, 0, 0:SQ], col("qn_w"), col("qn_b"), ALU.mult,
                                      ALU.add).then_inc(s(a, "xnT"), 1)
                else:
                    dve.tensor_copy(xnT[:, u, :], bank[:, 0, 0:SQ]).then_inc(s(a, "xnT"), 1)

            def queries(i, u):
                if L == 1:
                    dve.wait_ge(s(a, "q_ps"), a.at("q_ps") + i + 1)
                    dve.scalar_tensor_tensor(qT[:, u, :], bank[:, 0, SQ:2 * SQ], col("L1_bq"), keep1[:, :],
                                             ALU.add, ALU.mult).then_inc(s(a, "qT"), 1)

            def scores(i, u, half):
                c = Count(s(a, "dve"), a.at("dve") + i * 2 + half)
                sc = bank[:, 1 + 2 * half:3 + 2 * half, :].rearrange("q g (h k) -> q (g h) k", k=SK)
                m = mx[:, u, 16 * half:16 * half + 16]
                dve.wait_ge(s(a, "scores"), a.at("scores") + i * 2 + half + 1)
                c.inc(dve.tensor_reduce(m, sc, AX.X, ALU.max))
                c.wait(dve)
                dve.tensor_tensor(prob[:, u, 2 * half:2 * half + 2, :].rearrange("q g (h k) -> q (g h) k", k=SK), sc,
                                  m.unsqueeze(2).to_broadcast([P, 16, SK]), ALU.subtract).then_inc(s(a, "sub"), 1)

            def heads(i, u):
                dve.wait_ge(s(a, "values"), a.at("values") + i * 4 + 4)
                o = bank[:, 7, 0:QT * 8 * 18].rearrange("q (h c) -> q h c", c=HD + 1)
                dve.reciprocal(rs[:, u, :], o[:, :, HD]).then_inc(s(a, "rs"), 1)
                dve.wait_ge(s(a, "rs"), a.at("rs") + i + 1)
                dve.tensor_tensor(on[:, u, :, :].rearrange("q t (h d) -> q (t h) d", d=HD), o[:, :, 0:HD],
                                  rs[:, u, :].unsqueeze(2).to_broadcast([P, QT * NH, HD]), ALU.mult).then_inc(s(a, "on"), 1)

            def heads_out(i, u):
                dve.wait_ge(s(a, "ring_ps"), a.at("ring_ps") + i * 6 + 5)
                dve.tensor_copy(oT[:, u, :], bank[:, 5, 0:SQ]).then_inc(s(a, "oT"), 1)

            def add(i, u):
                dve.wait_ge(s(a, "ring_ps"), a.at("ring_ps") + i * 6 + 6)
                xb = x[:, ds(i * 2, 2), :]
                dve.tensor_tensor(xb, bank[:, 6, 0:SQ].rearrange("q (t e) -> q t e", t=QT), xb, ALU.add).then_inc(s(a, "x_add"), 1)

            def turn(i, u, rest):
                first = isinstance(i, int) and i == 0
                if not first:
                    heads_out(i - 1, 1 - u)
                if rest >= 1:
                    scores(i + 1, 1 - u, 0)
                if not first:
                    add(i - 1, 1 - u)
                if rest >= 2:
                    flip(i + 2, u)
                if rest >= 1:
                    scores(i + 1, 1 - u, 1)
                if rest >= 2:
                    queries(i + 2, u)
                heads(i, u)

            flip(0, 0)
            queries(0, 0)
            scores(0, 0, 0)
            scores(0, 0, 1)
            flip(1, 1)
            queries(1, 1)
            dve.wait_ge(s(a, "bo"), a.at("bo") + 1)
            turns(dve, turn)
            heads_out(B - 1, 1)
            add(B - 1, 1)
            dve.wait_ge(s(a, "x_add"), a.at("x_add") + B)
            dve.sem_inc(x_done, 1)

        def attn_act(a, before):
            act = nc.scalar
            act.wait_ge(x_done, before)
            L = a.layer
            if L == 2:
                norm_stats_act("X2c", cc, csq, stat_c, B * SK // P)
            norm_stats_act(a.tag, xc, wide, stat, NT)
            if L == 2:
                norm_stats_act("X2q", xc, wide, stat, NT)
            act.wait_ge(s(a, "k_ps"), a.at("k_ps") + 1)
            for h in range(2):
                dst = kT[:, 8 * h:8 * h + 8, :].rearrange("p b k -> p (b k)")
                if L == 0:
                    act.activation(dst, bank[:, 1 + h, :], ACT.Identity).then_inc(s(a, "kT"), 1)
                else:
                    act.activation(dst, bank[:, 1 + h, :], ACT.Identity, bias=col(f"L{L}_bk")).then_inc(s(a, "kT"), 1 + h)

            def queries(i, u):
                if L != 1:
                    act.wait_ge(s(a, "q_ps"), a.at("q_ps") + i + 1)
                    kw = {} if L == 0 else {"bias": col(f"L{L}_bq")}
                    act.activation(qT[:, u, :], bank[:, 0, SQ:2 * SQ], ACT.Identity, **kw).then_inc(s(a, "qT"), 1)

            def soft(i, u, half):
                act.wait_ge(s(a, "sub"), a.at("sub") + i * 2 + half + 1)
                p = prob[:, u, 2 * half:2 * half + 2, :].rearrange("q g k -> q (g k)")
                e = act.activation(p, p, ACT.Exp, scale=a.scale)
                if half == 1:
                    e.then_inc(s(a, "exp"), 1)

            def lot(i, u, n):
                act.wait_ge(s(a, "ring_ps"), a.at("ring_ps") + i * 6 + n + 1)
                if n >= 2:
                    act.wait_ge(s(a, "values"), a.at("values") + i * 4 + n - 1)
                act.activation(pT[:, n % 2, :], bank[:, 5 + n % 2, :], ACT.Identity).then_inc(s(a, "pT"), 1)

            def turn(i, u, rest):
                lot(i, u, 0)
                lot(i, u, 1)
                if rest >= 1:
                    soft(i + 1, 1 - u, 0)
                lot(i, u, 2)
                if rest >= 2:
                    queries(i + 2, u)
                lot(i, u, 3)
                if rest >= 1:
                    soft(i + 1, 1 - u, 1)

            queries(0, 0)
            soft(0, 0, 0)
            soft(0, 0, 1)
            queries(1, 1)
            turns(act, turn)

        def attn_pool(a, before):
            pool = nc.gpsimd
            pool.wait_ge(x_done, before)
            pool.memset(v2, 0.0).then_inc(s(a, "v2_zero"), 1)
            L = a.layer
            pool.wait_ge(S("norm", "centred"), NORMS.index(a.tag) + 1)
            pool.tensor_tensor(x[:, :, :], x[:, :, :], row(f"L{L}_bo").unsqueeze(1).to_broadcast([P, NT, P]),
                               ALU.add).then_inc(s(a, "bo"), 1)
            pool.wait_ge(S("norm", "rstd"), NORMS.index("X2q" if L == 2 else a.tag) + 1)
            pool.wait_ge(s(a, "kT"), a.at("kT") + 3)

            def batch(i, u, first=False):
                if not first:
                    pool.wait_ge(s(a, "scores"), a.at("scores") + (i - 1) * 2)
                pool.tensor_tensor(xn[:, u, :, :], xc[:, ds(i * 2, 2), :],
                                   stat[:, 3, ds(i * 2, 2)].unsqueeze(2).to_broadcast([P, QT, P]), ALU.mult).then_inc(s(a, "xn"), 1)
                pool.tensor_tensor(kblk[:, u, :, :], kT[:, ds(i, 1), :].to_broadcast([P, NH, SK]),
                                   headmask[:, :].unsqueeze(2).to_broadcast([P, NH, SK]), ALU.mult).then_inc(s(a, "kblk"), 1)

            batch(0, 0, True)
            batch(1, 1, True)
            with pool.Fori(1, B // 2) as j:
                batch(j * 2, 0)
                batch(j * 2 + 1, 1)

        xnT_all = wide[:, :, :].rearrange("p t e -> p (t e)")

        class Flip:

            def __init__(self, tag, xn2, keep=None):
                self.tag, self.xn2, self.keep = tag, xn2, keep

            def dve(self, dve, before):
                dve.wait_ge(x_done, before)
                norm_stats_dve(self.tag, x, xc, wide, stat, NT)

            def pool(self, pool, before):
                pool.wait_ge(S("norm", "rstd"), NORMS.index(self.tag) + 1)

                def batch(i, u, first=False):
                    if not first:
                        pool.wait_ge(S(self.tag, "flip_ps"), at(self.tag, "flip_ps") + i - 1)
                    pool.tensor_tensor(self.xn2[:, u, :, :], xc[:, ds(i * 2, 2), :],
                                       stat[:, 3, ds(i * 2, 2)].unsqueeze(2).to_broadcast([P, QT, P]),
                                       ALU.mult).then_inc(S(self.tag, "xn"), 1)

                batch(0, 0, True)
                batch(1, 1, True)
                with pool.Fori(1, B // 2) as j:
                    batch(j * 2, 0)
                    batch(j * 2 + 1, 1)

            def pe(self, pe, before):
                def batch(i, u, first=False):
                    pe.wait_ge(S(self.tag, "xn"), at(self.tag, "xn") + i + 1)
                    if not first:
                        pe.wait_ge(S(self.tag, "flip"), at(self.tag, "flip") + i - 1)
                    for t in range(QT):
                        m = pe.transpose(bank[:, u, t * P:(t + 1) * P], self.xn2[:, u, t, :], ident[:, :])
                    m.then_inc(S(self.tag, "flip_ps"), 1)

                batch(0, 0, True)
                batch(1, 1, True)
                with pe.Fori(1, B // 2) as j:
                    batch(j * 2, 0)
                    batch(j * 2 + 1, 1)

            def act(self, act, before):
                act.wait_ge(x_done, before)
                norm_stats_act(self.tag, xc, wide, stat, NT)

                def batch(i, u):
                    act.wait_ge(S(self.tag, "flip_ps"), at(self.tag, "flip_ps") + i + 1)
                    act.activation(xnT_all[:, ds(i * SQ, SQ)], bank[:, u, 0:SQ],
                                   ACT.Identity).then_inc(S(self.tag, "flip"), 1)

                with act.Fori(0, B // 2) as j:
                    batch(j * 2, 0)
                    batch(j * 2 + 1, 1)

        class TopTwo:
            tag = "F0"
            E, IB, CH = 8, 2, 512
            c = Carve()
            wg = c(8)
            w11 = c(8, 2, P)
            w12 = c(8, 2, P)
            w2 = c(8, 2, P)
            tri = c(8, 8)
            xn2 = c(2, QT, P)
            score = c(NT, 8)
            ex = c(NT, 8)
            cmp = c(NT, 8, 8)
            same = c(NT, 8, 8)
            rank = c(NT, 8)
            gate = c(NT, 8)
            one = c(4, NT)
            sg = c(2, 512)
            fu = c(2, 512)
            flip = Flip("F0", xn2)

            def sp(self, sp, before):
                sp.wait_ge(x_done, before)
                for dst, src in ((self.wg, A["F0_wg"]), (self.tri, A["tri8"]), (self.w11, A["F0_w11"]),
                                 (self.w12, A["F0_w12"]), (self.w2, A["F0_w2"])):
                    sp.dma_start(dst, src).then_inc(S("F0", "loaded"), 16)

            def pe(self, pe, before):
                s = lambda what: S("F0", what)
                self.flip.pe(pe, before)
                pe.wait_ge(s("loaded"), 80)
                pe.wait_ge(s("flip"), B)
                for t in range(NT):
                    m = pe.matmul(bank[:, 2, t * 8:t * 8 + 8], xnT_all[:, t * P:(t + 1) * P], self.wg,
                                  start=True, stop=True)
                m.then_inc(s("router"), 1)

                with pe.Fori(0, NT * P // self.CH) as c:
                    def up(k):
                        e, ib = k // 2, k % 2
                        wait(pe, s("fused"), c * 16 + k - 1 if k else c * 16)
                        rhs = xnT_all[:, ds(c * self.CH, self.CH)]
                        pe.matmul(bank[:, 3 + 2 * (k % 2), :], self.w11[:, e, ib, :], rhs, start=True, stop=True)
                        pe.matmul(bank[:, 4 + 2 * (k % 2), :], self.w12[:, e, ib, :], rhs, start=True,
                                  stop=True).then_inc(s("up"), 1)

                    def down(k):
                        e, ib = k // 2, k % 2
                        pe.wait_ge(s("fused"), c * 16 + k + 1)
                        if ib == 0:
                            pe.wait_ge(s("x_add"), c * 8 + e - 1 if e else c * 8)
                        for t in range(4):
                            m = pe.matmul(bank[:, e % 2, t * P:(t + 1) * P], self.fu[:, k % 2, t * P:(t + 1) * P],
                                          self.w2[:, e, ib, :], start=(ib == 0 and t == 0), stop=(ib == 1),
                                          skip_group_check=True)
                        m.then_inc(s("down"), 1)

                    up(0)
                    for k in range(1, 16):
                        up(k)
                        down(k - 1)
                    down(15)

            def dve(self, dve, before):
                s = lambda what: S("F0", what)
                self.flip.dve(dve, before)
                dve.wait_ge(s("router"), 1)
                c = Count(s("gating"))
                one = self.one
                lg = bank[:, 2, 0:NT * 8].rearrange("p (t e) -> p t e", e=8)

                def op(f, *args):
                    c.inc(f(*args))
                    c.wait(dve)

                def wide8(v):
                    return v.unsqueeze(2).to_broadcast([P, NT, 8])

                op(dve.tensor_reduce, one[:, 0, :], lg, AX.X, ALU.max)
                dve.tensor_tensor(self.score, lg, wide8(one[:, 0, :]), ALU.subtract).then_inc(s("less_max"), 1)
                dve.wait_ge(s("exp"), 1)
                op(dve.tensor_reduce, one[:, 1, :], self.ex, AX.X, ALU.add)
                op(dve.reciprocal, one[:, 2, :], one[:, 1, :])
                op(dve.tensor_tensor, self.score, self.ex, wide8(one[:, 2, :]), ALU.mult)
                other = self.score.unsqueeze(2).to_broadcast([P, NT, 8, 8])
                own = self.score.unsqueeze(3).to_broadcast([P, NT, 8, 8])
                op(dve.tensor_tensor, self.cmp, other, own, ALU.is_gt)
                op(dve.tensor_tensor, self.same, other, own, ALU.is_equal)
                op(dve.tensor_tensor, self.same, self.same, self.tri.unsqueeze(1).to_broadcast([P, NT, 8, 8]), ALU.mult)
                op(dve.tensor_tensor, self.cmp, self.cmp, self.same, ALU.add)
                op(dve.tensor_reduce, self.rank, self.cmp, AX.X, ALU.add)
                op(dve.scalar_tensor_tensor, self.gate, self.rank, 2.0, self.score, ALU.is_lt, ALU.mult)
                op(dve.tensor_reduce, one[:, 0, :], self.gate, AX.X, ALU.add)
                op(dve.tensor_scalar, one[:, 1, :], one[:, 0, :], 1e-8, None, ALU.add)
                op(dve.reciprocal, one[:, 2, :], one[:, 1, :])
                op(dve.tensor_tensor, self.gate, self.gate, wide8(one[:, 2, :]), ALU.mult)

                with dve.Fori(0, NT * P // self.CH) as ch:
                    def add(e):
                        dve.wait_ge(s("down"), ch * 16 + 2 * e + 2)
                        for t in range(4):
                            xt = x[:, ds(ch * 4 + t, 1), :].rearrange("p o d -> p (o d)")
                            g = self.gate[:, ds(ch * 4 + t, 1), e:e + 1].rearrange("p o d -> p (o d)")
                            if t == 0:
                                dve.wait_ge(s("x_add"), ch * 8 + e)
                            a = dve.scalar_tensor_tensor(xt, bank[:, e % 2, t * P:(t + 1) * P], g, xt, ALU.mult, ALU.add)
                        a.then_inc(s("x_add"), 1)

                    for k in range(16):
                        dve.wait_ge(s("silu"), ch * 16 + k + 1)
                        dve.wait_ge(s("down"), ch * 16 + k - 1 if k else ch * 16)
                        dve.tensor_tensor(self.fu[:, k % 2, :], bank[:, 4 + 2 * (k % 2), :], self.sg[:, k % 2, :],
                                          ALU.mult).then_inc(s("fused"), 1)
                        if k >= 2 and k % 2 == 0:
                            add(k // 2 - 1)
                    add(7)
                dve.wait_ge(s("x_add"), NT * P // self.CH * 8)
                dve.sem_inc(x_done, 1)

            def act(self, act, before):
                s = lambda what: S("F0", what)
                self.flip.act(act, before)
                act.wait_ge(s("less_max"), 1)
                act.activation(self.ex, self.score, ACT.Exp).then_inc(s("exp"), 1)
                with act.Fori(0, NT * P // self.CH) as ch:
                    for k in range(16):
                        act.wait_ge(s("up"), ch * 16 + k + 1)
                        act.wait_ge(s("fused"), ch * 16 + k - 1 if k else ch * 16)
                        act.activation(self.sg[:, k % 2, :], bank[:, 3 + 2 * (k % 2), :], ACT.Silu).then_inc(s("silu"), 1)

            def pool(self, pool, before):
                pool.wait_ge(x_done, before)
                self.flip.pool(pool, before)

        class ExpertChoice:
            tag = "F3"
            E, FB, CH, K, BITS = 8, 4, 512, 256, 30
            c = Carve()
            rw = c(8)
            w1 = c(8, 4, P)
            w2 = c(8, 4, P)
            b1 = c(8, 4)
            rb = c(8)
            b2 = c(P)
            bits = c(30, dt=I32)
            xn2 = c(2, QT, P)
            score = c(NT, 8)
            ex = c(NT, 8)
            hit = c(NT, 8)
            part = c(8)
            okb = c(8, dt=I32)
            thr = c(8, dt=I32)
            cand = c(8, dt=I32)
            gate = c(NT, 8)
            eq = c(NT, 8)
            eqb = c(NT, 8, dt=BF16)
            tot = c(8, NT)
            run = c(8, NT)
            room = c(8)
            one = c(4, NT)
            ones8 = c(8, NT)
            triu = c(P, dt=BF16)
            oneb = c(P, dt=BF16)
            gT = c(NT * P)
            h = c(2, 512)
            flip = Flip("F3", xn2)

            def sp(self, sp, before):
                sp.wait_ge(x_done, before)
                for dst, src in ((self.rw, A["F3_rw"]), (self.rb, A["F3_rb"].partition_broadcast(P)),
                                 (self.b2[0:8, :], A["F3_b2"]), (self.b1, A["F3_b1"]),
                                 (self.bits, A["bits"].partition_broadcast(P)),
                                 (self.w1, A["F3_w1"]), (self.w2, A["F3_w2"])):
                    sp.dma_start(dst, src).then_inc(S("F3", "loaded"), 16)

            def pe(self, pe, before):
                s = lambda what: S("F3", what)
                self.flip.pe(pe, before)
                pe.wait_ge(s("loaded"), at("F3", "loaded") + 16 * 7)
                pe.wait_ge(s("flip"), at("F3", "flip") + B)
                for t in range(NT):
                    m = pe.matmul(bank[:, 2, t * 8:t * 8 + 8], xnT_all[:, t * P:(t + 1) * P], self.rw,
                                  start=True, stop=True)
                m.then_inc(s("router"), 1)
                with pe.Fori(0, self.BITS) as n:
                    pe.wait_ge(s("part"), n + 1)
                    pe.matmul(bank[:, 0, 0:8], onesf[:, :], self.part, start=True, stop=True).then_inc(s("count"), 1)
                pe.wait_ge(s("part"), self.BITS + 1)
                pe.matmul(bank[:, 0, 0:8], onesf[:, :], self.part, start=True, stop=True).then_inc(s("count"), 1)
                pe.wait_ge(s("eqb"), 1)
                pe.wait_ge(s("tri"), 3)
                eqb = self.eqb.rearrange("p t e -> p (t e)")
                pe.matmul(bank[:, 3, 0:NT * 8], self.triu, eqb, start=True, stop=True)
                pe.matmul(bank[:, 4, 0:NT * 8], self.oneb, eqb, start=True, stop=True).then_inc(s("eq_ps"), 1)
                pe.wait_ge(s("gate"), 1)
                for t in range(NT):
                    m = pe.transpose(bank[0:8, t // 4, (t % 4) * P:(t % 4 + 1) * P], self.gate[:, t, :], ident[:, :])
                m.then_inc(s("gT_ps"), 1)
                for q in range(8):
                    pe.wait_ge(s("gT"), q + 1)
                    for t in range(4 * q, 4 * q + 4):
                        m = pe.matmul(bank[:, t // 4, (t % 4) * P:(t % 4 + 1) * P], self.gT[0:8, t * P:(t + 1) * P],
                                      self.b2[0:8, :], start=True, stop=True)
                    m.then_inc(s("b2_ps"), 1)
                pe.wait_ge(s("b2_add"), 8)

                with pe.Fori(0, NT * P // self.CH) as c:
                    def up(k):
                        e, f = k // 4, k % 4
                        wait(pe, s("h"), c * 32 + k - 1 if k else c * 32)
                        pe.matmul(bank[:, 2 + k % 2, :], self.w1[:, e, f, :], xnT_all[:, ds(c * self.CH, self.CH)],
                                  start=True, stop=True).then_inc(s("up"), 1)

                    def down(k):
                        e, f = k // 4, k % 4
                        pe.wait_ge(s("h"), c * 32 + k + 1)
                        if f == 0:
                            pe.wait_ge(s("x_add"), at("F3", "x_add") + (c * 8 + e - 1 if e else c * 8))
                        for t in range(4):
                            m = pe.matmul(bank[:, e % 2, t * P:(t + 1) * P], self.h[:, k % 2, t * P:(t + 1) * P],
                                          self.w2[:, e, f, :], start=(f == 0 and t == 0), stop=(f == 3),
                                          skip_group_check=True)
                        m.then_inc(s("down"), 1)

                    up(0)
                    for k in range(1, 32):
                        up(k)
                        down(k - 1)
                    down(31)

            def dve(self, dve, before):
                s = lambda what: S("F3", what)
                self.flip.dve(dve, before)
                one = self.one
                lg = bank[:, 2, 0:NT * 8].rearrange("p (t e) -> p t e", e=8)
                c = Count(s("gating"))

                def op(f, *args):
                    c.inc(f(*args))
                    c.wait(dve)

                def wide8(v):
                    return v.unsqueeze(2).to_broadcast([P, NT, 8])

                def tiles(v):
                    return v.unsqueeze(1).to_broadcast([P, NT, 8])

                dve.wait_ge(s("router"), at("F3", "router") + 1)
                dve.wait_ge(s("loaded"), at("F3", "loaded") + 16 * 7)
                op(dve.tensor_tensor, self.ex, lg, tiles(self.rb), ALU.add)
                op(dve.tensor_reduce, one[:, 0, :], self.ex, AX.X, ALU.max)
                dve.tensor_tensor(self.score, self.ex, wide8(one[:, 0, :]), ALU.subtract).then_inc(s("less_max"), 1)
                op(dve.memset, self.thr, 0)
                dve.wait_ge(s("exp"), at("F3", "exp") + 1)
                op(dve.tensor_reduce, one[:, 1, :], self.ex, AX.X, ALU.add)
                op(dve.reciprocal, one[:, 2, :], one[:, 1, :])
                op(dve.tensor_tensor, self.score, self.ex, wide8(one[:, 2, :]), ALU.mult)

                by_expert = self.hit.rearrange("p t e -> p e t")
                with dve.Fori(0, self.BITS) as n:
                    b = Count(s("bit"), n * 5)
                    bit = self.bits[:, ds(n, 1)].to_broadcast([P, 8])
                    b.inc(dve.tensor_tensor(self.cand, self.thr, bit, ALU.bitwise_or))
                    b.wait(dve)
                    b.inc(dve.tensor_tensor(self.hit, self.score, tiles(self.cand.bitcast(F32)), ALU.is_ge))
                    b.wait(dve)
                    dve.tensor_reduce(self.part, by_expert, AX.X, ALU.add).then_inc(s("part"), 1)
                    dve.wait_ge(s("count"), n + 1)
                    b.inc(dve.tensor_scalar(self.okb, bank[:, 0, 0:8], float(self.K), None, ALU.is_ge))
                    b.wait(dve)
                    b.inc(dve.tensor_tensor(self.okb, self.okb, bit, ALU.mult))
                    b.wait(dve)
                    b.inc(dve.tensor_tensor(self.thr, self.thr, self.okb, ALU.bitwise_or))
                    b.wait(dve)
                thr = tiles(self.thr.bitcast(F32))
                op(dve.tensor_tensor, self.hit, self.score, thr, ALU.is_gt)
                dve.tensor_reduce(self.part, by_expert, AX.X, ALU.add).then_inc(s("part"), 1)
                op(dve.tensor_tensor, self.eq, self.score, thr, ALU.is_equal)
                op(dve.memset, self.ones8, 1.0)
                dve.tensor_copy(self.eqb, self.eq).then_inc(s("eqb"), 1)
                dve.wait_ge(s("count"), self.BITS + 1)
                op(dve.tensor_scalar, self.room, bank[:, 0, 0:8], -1.0, float(self.K), ALU.mult, ALU.add)
                dve.wait_ge(s("eq_ps"), 1)
                op(dve.tensor_copy, self.tot, bank[:, 4, 0:NT * 8].rearrange("p (t e) -> p e t", e=8))
                for e in range(8):
                    op(dve.tensor_tensor_scan, self.run[:, e, :], self.ones8[:, e, :], self.tot[:, e, :], 0.0,
                       ALU.mult, ALU.add)
                op(dve.tensor_tensor, self.run, self.run, self.tot, ALU.subtract)
                before_it = self.gate
                op(dve.tensor_tensor, before_it, bank[:, 3, 0:NT * 8].rearrange("p (t e) -> p t e", e=8),
                   self.run.rearrange("p e t -> p t e"), ALU.add)
                op(dve.tensor_tensor, self.gate, before_it, tiles(self.room), ALU.is_lt)
                op(dve.tensor_tensor, self.gate, self.gate, self.eq, ALU.mult)
                op(dve.tensor_tensor, self.gate, self.gate, self.hit, ALU.add)
                dve.tensor_tensor(self.gate, self.gate, self.score, ALU.mult).then_inc(s("gate"), 1)
                dve.wait_ge(s("gate"), 1)
                dve.wait_ge(s("gT_ps"), 1)
                for q in range(8):
                    dve.tensor_copy(self.gT[0:8, q * 512:(q + 1) * 512], bank[0:8, q, :]).then_inc(s("gT"), 1)
                for q in range(8):
                    dve.wait_ge(s("b2_ps"), q + 1)
                    xb = x[:, 4 * q:4 * q + 4, :]
                    dve.tensor_tensor(xb, bank[:, q, :].rearrange("p (t d) -> p t d", t=4), xb,
                                      ALU.add).then_inc(s("b2_add"), 1)

                dve.wait_ge(s("b2_add"), 8)
                with dve.Fori(0, NT * P // self.CH) as ch:
                    for e in range(8):
                        dve.wait_ge(s("down"), at("F3", "down") + ch * 32 + 4 * e + 4)
                        dve.wait_ge(s("x_add"), at("F3", "x_add") + ch * 8 + e)
                        for t in range(4):
                            xt = x[:, ds(ch * 4 + t, 1), :].rearrange("p o d -> p (o d)")
                            g = self.gate[:, ds(ch * 4 + t, 1), e:e + 1].rearrange("p o d -> p (o d)")
                            a = dve.scalar_tensor_tensor(xt, bank[:, e % 2, t * P:(t + 1) * P], g, xt, ALU.mult, ALU.add)
                        a.then_inc(s("x_add"), 1)
                dve.wait_ge(s("x_add"), at("F3", "x_add") + NT * P // self.CH * 8)
                dve.sem_inc(x_done, 1)

            def act(self, act, before):
                s = lambda what: S("F3", what)
                self.flip.act(act, before)
                act.wait_ge(s("less_max"), at("F3", "less_max") + 1)
                act.activation(self.ex, self.score, ACT.Exp).then_inc(s("exp"), 1)
                with act.Fori(0, NT * P // self.CH) as ch:
                    for k in range(32):
                        act.wait_ge(s("up"), at("F3", "up") + ch * 32 + k + 1)
                        act.wait_ge(s("down"), at("F3", "down") + (ch * 32 + k - 1 if k else ch * 32))
                        act.activation(self.h[:, k % 2, :], bank[:, 2 + k % 2, :], ACT.Relu,
                                       bias=self.b1[:, k // 4, k % 4:k % 4 + 1]).then_inc(s("h"), 1)

            def pool(self, pool, before):
                pool.wait_ge(x_done, before)
                pool.memset(self.triu, 1.0).then_inc(S("F3", "tri"), 1)
                pool.memset(self.oneb, 1.0).then_inc(S("F3", "tri"), 1)
                pool.wait_ge(S("F3", "tri"), 2)
                pool.affine_select(self.triu, self.triu, [[1, P]], ALU.is_gt, 0.0, base=0,
                                   channel_multiplier=-1).then_inc(S("F3", "tri"), 1)
                self.flip.pool(pool, before)

        class SoftSlots:
            tag = "F1"
            tag = "F1"
            NC, N4 = 16, 4
            c = Carve()
            phi = c(2048)
            bn = c(64)
            wc = c(2, 4, P)
            sT = c(B, P)
            yT = c(B, P)
            yo = c(B, P)
            top = c(2, 2, P)
            ssum = c(2, 2, P)
            rinv = c(2, 2, P)
            ex = c(2, 2, B, P)
            c = Carve(2048)
            xs = c(2, SQ)
            e2 = c(2, 2048)
            eT = c(2, 4, P)
            yb = c(2, 16, P)
            ntop = c(4)
            part = c(4, 4)
            tot = c(4)
            ri = c(4)

            def s(self, what):
                return S("F1", what)

            def sp(self, sp, before):
                s = self.s
                sp.wait_ge(x_done, before)
                sp.dma_start(self.phi, A["F1_phi"]).then_inc(s("loaded"), 16)
                sp.dma_start(self.bn, A["F1_b"]).then_inc(s("loaded"), 16)

                def chunk(c, u, first=False):
                    if not first:
                        sp.wait_ge(s("yT_ps"), (c - 1) * 4)
                    sp.dma_start(self.wc[:, u, :, :], A["F1_w"][ds(c, 1), :, :].rearrange("o p n -> p (o n)")).then_inc(
                        s("wc%d" % u), 16)

                def store(c):
                    sp.wait_ge(s("yo"), c * 4 + 4)
                    sp.dma_start(A["y_slots"][:, :, ds(c, 1), :].rearrange("b p o d -> p b (o d)"), self.yo).then_inc(s("y_out"), 16)

                chunk(0, 0, True)
                chunk(1, 1, True)
                with sp.Fori(0, self.NC // 2 - 1) as j:
                    chunk(j * 2 + 2, 0)
                    store(j * 2)
                    chunk(j * 2 + 3, 1)
                    store(j * 2 + 1)
                store(self.NC - 2)
                store(self.NC - 1)
                sp.wait_ge(s("y_out"), 16 * self.NC)

                def batch(b, u, first=False):
                    if not first:
                        sp.wait_ge(s("out"), (b - 1) * 2)
                    sp.dma_start(self.yb[:, u, :, :], A["y_slots"][ds(b, 1), :, :, :].rearrange("o p c d -> p (o c) d")).then_inc(
                        s("yb%d" % u), 16)

                sp.wait_ge(s("all_slots"), 1)
                batch(0, 0, True)
                batch(1, 1, True)
                with sp.Fori(1, B // 2) as j:
                    batch(j * 2, 0)
                    batch(j * 2 + 1, 1)

            def pe(self, pe, before):
                s = self.s
                pe.wait_ge(s("xn"), 1)
                for t in range(NT):
                    m = pe.transpose(bank[:, t // 4, (t % 4) * P:(t % 4 + 1) * P], xc[:, t, :], ident[:, :])
                    if t % 4 == 3:
                        m.then_inc(s("flip_ps"), 1)
                pe.wait_ge(s("flip"), 8)
                pe.wait_ge(s("loaded"), 32)

                def logits(c, h):
                    wait(pe, s("sub"), c * 2 + h)
                    for b in range(B):
                        t = 2 * b + h
                        m = pe.matmul(bank[:, b // 4, (b % 4) * P:(b % 4 + 1) * P], xnT_all[:, t * P:(t + 1) * P],
                                      self.phi[:, ds(c * P, P)], start=True, stop=True)
                    m.then_inc(s("logits"), 1)

                def slots(c, u):
                    pe.wait_ge(s("disp"), c * 2 + 2)
                    wait(pe, s("yo"), c * 4)
                    for b in range(B):
                        for h in range(2):
                            m = pe.matmul(bank[:, 4 + b // 4, (b % 4) * P:(b % 4 + 1) * P], xc[:, 2 * b + h, :],
                                          self.ex[:, u, h, b, :], start=(h == 0), stop=(h == 1))
                        if b % 4 == 3:
                            m.then_inc(s("slots"), 1)

                def experts(c, u):
                    pe.wait_ge(s("sT"), c * 4 + 4)
                    pe.wait_ge(s("wc%d" % u), (c // 2 + 1) * 16 if isinstance(c, int) else c * 8 + (16 - 8 * u))
                    for n in range(4):
                        pe.matmul(bank[:, 4 + n, :], self.wc[:, u, n, :], self.sT[:, :, 32 * n:32 * n + 32],
                                  start=True, stop=True).then_inc(s("yT_ps"), 1)
                    pe.wait_ge(s("yT"), c * 4 + 4)
                    for b in range(B):
                        m = pe.transpose(bank[:, 4 + b // 4, (b % 4) * P:(b % 4 + 1) * P], self.yT[:, b, :], ident[:, :])
                        if b % 4 == 3:
                            m.then_inc(s("yo_ps"), 1)

                logits(0, 0)
                logits(0, 1)
                with pe.Fori(0, self.NC // 2 - 1) as j:
                    for u in range(2):
                        c = j * 2 + u
                        logits(c + 1, 0)
                        slots(c, u)
                        logits(c + 1, 1)
                        experts(c, u)
                logits(self.NC - 1, 0)
                slots(self.NC - 2, 0)
                logits(self.NC - 1, 1)
                experts(self.NC - 2, 0)
                slots(self.NC - 1, 1)
                experts(self.NC - 1, 1)

                pe.wait_ge(s("yo"), self.NC * 4)

                def front(t, q):
                    b2 = (q // 2) % 2
                    pe.wait_ge(s("xs"), t // 2 + 1 if isinstance(t, int) else (t - q % 2) // 2 + 1)
                    wait(pe, s("exp"), t * 4)
                    for k in range(4):
                        m = pe.matmul(bank[:, k, :], self.xs[:, b2, (q % 2) * P:(q % 2 + 1) * P],
                                      self.phi[:, k * 512:(k + 1) * 512], start=True, stop=True)
                    m.then_inc(s("lt"), 1)

                def back(t, q):
                    b2 = q // 2
                    if q % 2 == 0:
                        pe.wait_ge(s("yb%d" % b2), ((t // 4 if isinstance(t, int) else (t - q) // 4) + 1) * 16)

                    def lot(k):
                        pe.wait_ge(s("exp"), t * 4 + k + 1)
                        wait(pe, s("eT"), t * 4 + k - 1)
                        for r in range(4):
                            ch = 4 * k + r
                            m = pe.transpose(bank[:, 4 + k % 2, r * P:(r + 1) * P], self.e2[:, q % 2, ch * P:(ch + 1) * P],
                                             ident[:, :])
                        m.then_inc(s("eT_ps"), 1)

                    def mix(k):
                        pe.wait_ge(s("eT"), t * 4 + k + 1)
                        if k == 0:
                            wait(pe, s("x_add"), t - 1)
                        for r in range(4):
                            ch = 4 * k + r
                            m = pe.matmul(bank[:, 6 + q % 2, 0:P], self.eT[:, k % 2, r, :], self.yb[:, b2, ch, :],
                                          start=(ch == 0), stop=(ch == 15))
                        m.then_inc(s("mix"), 1)
                        return m

                    lot(0)
                    for k in range(1, 4):
                        lot(k)
                        mix(k - 1)
                    mix(3)
                    pe.wait_ge(s("mix"), t * 4 + 4)
                    pe.sem_inc(s("out"), 1)

                front(0, 0)
                for q in range(4):
                    front(q + 1, (q + 1) % 4)
                    back(q, q)
                with pe.Fori(1, NT // 4 - 1) as j:
                    for q in range(4):
                        front(j * 4 + q + 1, (q + 1) % 4)
                        back(j * 4 + q, q)
                for q in range(4):
                    if q < 3:
                        front(NT - 4 + q + 1, q + 1)
                    back(NT - 4 + q, q)

            def dve(self, dve, before):
                s = self.s
                dve.wait_ge(x_done, before)
                norm_stats_dve("F1", x, xc, wide, stat, NT)
                dve.wait_ge(S("norm", "rstd"), NORMS.index(self.tag) + 1)
                dve.tensor_tensor(xc[:, :, :], xc[:, :, :], stat[:, 3, :].unsqueeze(2).to_broadcast([P, NT, P]),
                                  ALU.mult).then_inc(s("xn"), 1)
                for q in range(8):
                    dve.wait_ge(s("flip_ps"), q + 1)
                    dve.tensor_copy(xnT_all[:, q * 512:(q + 1) * 512], bank[:, q, :]).then_inc(s("flip"), 1)

                def softmax(c, u, h):
                    d = Count(s("batch_max"), c * 2 + h)
                    lg = bank[:, 0:4, :].rearrange("p k (b n) -> p (k b) n", n=P)
                    dve.wait_ge(s("logits"), c * 2 + h + 1)
                    d.inc(dve.tensor_reduce(self.top[:, u, h, :], lg.rearrange("p b n -> p n b"), AX.X, ALU.max))
                    d.wait(dve)
                    wait(dve, s("slots"), (c - 1) * 4)
                    dve.tensor_tensor(self.ex[:, u, h, :, :], lg, self.top[:, u, h, :].unsqueeze(1).to_broadcast([P, B, P]),
                                      ALU.subtract).then_inc(s("sub"), 1)

                def weights(c, u, h):
                    d = Count(s("batch_sum"), c * 2 + h)
                    dve.wait_ge(s("bexp"), c * 2 + h + 1)
                    d.inc(dve.tensor_reduce(self.ssum[:, u, h, :], self.ex[:, u, h, :, :].rearrange("p b n -> p n b"),
                                            AX.X, ALU.add))
                    d.wait(dve)
                    dve.reciprocal(self.rinv[:, u, h, :], self.ssum[:, u, h, :]).then_inc(s("rinv"), 1)

                softmax(0, 0, 0)
                softmax(0, 0, 1)
                weights(0, 0, 0)
                weights(0, 0, 1)
                softmax(1, 1, 0)
                softmax(1, 1, 1)
                weights(1, 1, 0)
                weights(1, 1, 1)
                with dve.Fori(1, self.NC // 2) as j:
                    for u in range(2):
                        for h in range(2):
                            softmax(j * 2 + u, u, h)
                        for h in range(2):
                            weights(j * 2 + u, u, h)

                def front(t, q):
                    dve.wait_ge(s("lt"), t + 1)
                    dve.tensor_reduce(self.ntop[:, q:q + 1], bank[:, 0:4, :].rearrange("p k n -> p (k n)"), AX.X, ALU.max,
                                      negate=True).then_inc(s("ntop"), 1)

                def back(t, q):
                    for k in (1, 3):
                        dve.wait_ge(s("eT_ps"), t * 4 + k + 1)
                        if k == 3 or not (isinstance(t, int) and t == 0):
                            dve.wait_ge(s("mix"), t * 4 + k - 1)
                        dve.wait_ge(s("eT"), t * 4 + k)
                        dve.tensor_copy(self.eT[:, k % 2, :, :].rearrange("p r m -> p (r m)"),
                                        bank[:, 4 + k % 2, :]).then_inc(s("eT"), 1)
                    d = Count(s("norm"), t * 2)
                    dve.wait_ge(s("exp"), t * 4 + 4)
                    d.inc(dve.tensor_reduce(self.tot[:, q:q + 1], self.part[:, q, :], AX.X, ALU.add))
                    d.wait(dve)
                    d.inc(dve.reciprocal(self.ri[:, q:q + 1], self.tot[:, q:q + 1]))
                    d.wait(dve)
                    dve.wait_ge(s("out"), t + 1)
                    xt = x[:, ds(t, 1), :].rearrange("p o d -> p (o d)")
                    dve.scalar_tensor_tensor(xt, bank[:, 6 + q % 2, 0:P], self.ri[:, q:q + 1], xt, ALU.mult,
                                             ALU.add).then_inc(s("x_add"), 1)

                front(0, 0)
                for q in range(4):
                    front(q + 1, (q + 1) % 4)
                    back(q, q)
                with dve.Fori(1, NT // 4 - 1) as j:
                    for q in range(4):
                        front(j * 4 + q + 1, (q + 1) % 4)
                        back(j * 4 + q, q)
                for q in range(4):
                    if q < 3:
                        front(NT - 4 + q + 1, q + 1)
                    back(NT - 4 + q, q)
                dve.wait_ge(s("x_add"), NT)
                dve.sem_inc(x_done, 1)

            def act(self, act, before):
                s = self.s
                act.wait_ge(x_done, before)
                norm_stats_act("F1", xc, wide, stat, NT)

                def exps(c, u):
                    for h in range(2):
                        act.wait_ge(s("sub"), c * 2 + h + 1)
                        e = self.ex[:, u, h, :, :].rearrange("p b n -> p (b n)")
                        act.activation(e, e, ACT.Exp).then_inc(s("bexp"), 1)

                def evac(c, u):
                    for k in range(4):
                        act.wait_ge(s("slots"), c * 4 + k + 1)
                        act.activation(self.sT[:, 4 * k:4 * k + 4, :].rearrange("p b n -> p (b n)"), bank[:, 4 + k, :],
                                       ACT.Identity).then_inc(s("sT"), 1)
                    for n in range(4):
                        act.wait_ge(s("yT_ps"), c * 4 + n + 1)
                        act.activation(self.yT[:, :, 32 * n:32 * n + 32], bank[:, 4 + n, :].rearrange("p (b q) -> p b q", q=32),
                                       ACT.Identity, bias=self.bn[:, ds(c * 4 + n, 1)]).then_inc(s("yT"), 1)
                    wait(act, s("y_out"), c * 16)
                    for k in range(4):
                        act.wait_ge(s("yo_ps"), c * 4 + k + 1)
                        act.activation(self.yo[:, 4 * k:4 * k + 4, :].rearrange("p b n -> p (b n)"), bank[:, 4 + k, :],
                                       ACT.Identity).then_inc(s("yo"), 1)

                exps(0, 0)
                with act.Fori(0, self.NC // 2 - 1) as j:
                    for u in range(2):
                        exps(j * 2 + u + 1, 1 - u)
                        evac(j * 2 + u, u)
                exps(self.NC - 1, 1)
                evac(self.NC - 2, 0)
                evac(self.NC - 1, 1)

                def front(t, q):
                    act.wait_ge(s("ntop"), t + 1)
                    wait(act, s("eT_ps"), (t - 1) * 4)
                    wait(act, s("x_add"), t - 3)
                    for k in range(4):
                        act.activation(self.e2[:, q % 2, k * 512:(k + 1) * 512], bank[:, k, :], ACT.Exp,
                                       bias=self.ntop[:, q:q + 1], accum_out=self.part[:, q, k:k + 1]).then_inc(s("exp"), 1)

                def back(t, q):
                    for k in (0, 2):
                        act.wait_ge(s("eT_ps"), t * 4 + k + 1)
                        if k == 2 or not (isinstance(t, int) and t == 0):
                            act.wait_ge(s("mix"), t * 4 + k - 1)
                            act.wait_ge(s("eT"), t * 4 + k)
                        act.activation(self.eT[:, k % 2, :, :].rearrange("p r m -> p (r m)"), bank[:, 4 + k % 2, :],
                                       ACT.Identity).then_inc(s("eT"), 1)

                front(0, 0)
                for q in range(4):
                    back(q, q)
                    front(q + 1, (q + 1) % 4)
                with act.Fori(1, NT // 4 - 1) as j:
                    for q in range(4):
                        back(j * 4 + q, q)
                        front(j * 4 + q + 1, (q + 1) % 4)
                for q in range(4):
                    back(NT - 4 + q, q)
                    if q < 3:
                        front(NT - 4 + q + 1, q + 1)

            def pool(self, pool, before):
                s = self.s

                def weights(c, u):
                    for h in range(2):
                        pool.wait_ge(s("rinv"), c * 2 + h + 1)
                        pool.tensor_tensor(self.ex[:, u, h, :, :], self.ex[:, u, h, :, :],
                                           self.rinv[:, u, h, :].unsqueeze(1).to_broadcast([P, B, P]),
                                           ALU.mult).then_inc(s("disp"), 1)

                with pool.Fori(0, self.NC // 2) as j:
                    weights(j * 2, 0)
                    weights(j * 2 + 1, 1)
                pool.wait_ge(s("yo"), self.NC * 4)
                pool.wait_ge(s("y_out"), self.NC * 16)
                pool.sem_inc(s("all_slots"), 1)

                def batch(b, u, first=False):
                    if not first:
                        pool.wait_ge(s("lt"), (b - 1) * 2)
                    pool.tensor_copy(self.xs[:, u, :], xnT_all[:, ds(b * SQ, SQ)]).then_inc(s("xs"), 1)

                batch(0, 0, True)
                batch(1, 1, True)
                with pool.Fori(1, B // 2) as j:
                    batch(j * 2, 0)
                    batch(j * 2 + 1, 1)

        class Trees:
            tag = "F2"
            LEAF, GROUPS, NBLK, IT = 8, 32, 64, 16
            XW = P + 8
            c = Carve()
            w1 = c(GROUPS * P)
            w2 = c(GROUPS * P)
            b1 = c(GROUPS * P)
            b2 = c(GROUPS * P)
            xm = c(NT, XW)
            nw = c(2, 256)
            nb = c(2, 256)
            slot = c(4, NT, dt=I32)
            grp = c(4, NBLK, dt=I32)
            iota = c(NBLK)
            tri = c(P, dt=BF16)
            oneb = c(P, dt=BF16)
            r0 = c.at
            bits = c(NT, 256, dt=BF16)
            G = c(NT, 32, dt=BF16)
            oa = c(NT * 32)
            ob = c(NT * 32)
            tmp = Carve(c.at)(NT * P, dt=BF16)
            totg = c(32, NT)
            incl = c(32, NT)
            sub = c(NT, 7)
            p1 = c(NT, 2)
            p2 = c(NT, 4)
            sm = c(8, 32)
            nbi = c(32, dt=I32)
            slotf = c(NT)
            c = Carve(r0)
            xin = c(4, 4, XW)
            xT = c(2, 512)
            mT = c(4, 512)
            gl = c(2, 512)
            hm = c(2, 512)
            hT = c(2, 512)
            yo = c(2, 4, P)
            c = Carve(r0)
            va = c(NT, P)
            qk = c(2, 2, QT, P)
            qkT = c(2, 512)
            e = c(2, QT, SQ)
            eT = c(2, 512)
            yb = c(2, QT, P)
            small = c(8, 2, 2)
            c = Carve(r0)
            out = c(NT, P)

            def weights(self, n):
                if n == 1:
                    return xc[:, :, :].rearrange("p t e -> p (t e)"), xnT_all
                return self.w1, self.w2

            def s(self, what):
                return S("F2", what)

            def sp(self, sp, before):
                s = self.s
                sp.wait_ge(x_done, before)
                sp.dma_start(self.iota, A["iota64"].partition_broadcast(P)).then_inc(s("const"), 16)

                def nodes(n):
                    sp.dma_start(self.nw[:, n % 2, 0:255], A["F2_nw"][n, :, :]).then_inc(s("nw%d" % (n % 2)), 16)
                    sp.dma_start(self.nb[:, n % 2, 0:255], A["F2_nb"][n, :].partition_broadcast(P)).then_inc(s("nw%d" % (n % 2)), 16)

                def leaves(n):
                    for dst, src in zip(self.weights(n), ("w1", "w2")):
                        sp.dma_start(dst, A["F2_" + src][n, :, :]).then_inc(s("w%d" % (n % 2)), 16)

                def biases(n):
                    for dst, src in ((self.b1[0:8, :], "b1"), (self.b2[0:8, :], "b2")):
                        sp.dma_start(dst, A["F2_" + src][n, :, :]).then_inc(s("b"), 16)

                nodes(0)
                nodes(1)
                leaves(0)
                for n in range(2):
                    sp.wait_ge(s("slots"), n + 1)
                    nodes(n + 2)
                sp.wait_ge(s("slots"), 3)
                for n in range(4):
                    if n:
                        sp.wait_ge(s("y"), 16 * n)
                    biases(n)
                    if n < 2:
                        leaves(n + 1)
                    if n == 3:
                        leaves(3)
                        sp.wait_ge(s("slots"), 4)
                    xs = A["xs%d" % (n % 3)]
                    sp.wait_ge(s("scattered"), 16 * NT * (n + 1))

                    def load(i, q):
                        sp.dma_start(self.xin[:, q, :, :], xs[ds(i * 4, 4), :, :].rearrange("k p w -> p k w")).then_inc(
                            s("xin%d" % q), 16)

                    def store(i, u):
                        sp.wait_ge(s("yo"), n * 16 + i + 1)
                        sp.dma_start(A["ys%d" % n][ds(i * 4, 4), :, :].rearrange("k p w -> p k w"), self.yo[:, u, :, :]).then_inc(
                            s("ys%d" % u), 16)

                    for q in range(4):
                        load(q, q)
                    with sp.Fori(0, 3) as j:
                        for q in range(4):
                            sp.wait_ge(s("hm"), j * 4 + (n * 16 + q + 1))
                            load(j * 4 + 4 + q, q)
                            store(j * 4 + q, q % 2)
                    for q in range(4):
                        store(12 + q, q % 2)
                    sp.wait_ge(s("ys0"), 128 * (n + 1))
                    sp.wait_ge(s("ys1"), 128 * (n + 1))

            def pe(self, pe, before):
                s = self.s
                pe.wait_ge(s("xn"), at("F2", "xn") + 1)
                for t in range(NT):
                    m = pe.transpose(bank[:, t // 4, (t % 4) * P:(t % 4 + 1) * P], xc[:, t, :], ident[:, :])
                    if t % 4 == 3:
                        m.then_inc(s("flip_ps"), 1)
                pe.wait_ge(s("flip"), at("F2", "flip") + 8)
                pe.wait_ge(s("tri"), 3)
                for n in range(3):
                    self.route_pe(pe, n)
                for n in range(3):
                    self.blocks_pe(pe, n)
                self.attend_pe(pe)
                self.route_pe(pe, 3)
                self.blocks_pe(pe, 3)

            def route_pe(self, pe, n):
                s = self.s
                pe.wait_ge(s("nw%d" % (n % 2)), 32 * (n // 2 + 1))
                for tp in range(16):
                    wait(pe, s("bits"), n * 16 + tp - 7)
                    if tp == 4:
                        wait(pe, s("slots"), n)
                    for h in range(2):
                        t = 2 * tp + h
                        m = pe.matmul(bank[:, (tp + 4) % 8, h * 255:(h + 1) * 255], xnT_all[:, t * P:(t + 1) * P],
                                      self.nw[:, n % 2, 0:255], start=True, stop=True)
                    m.then_inc(s("nodes"), 1)
                pe.wait_ge(s("G"), n + 1)
                Gf = self.G.rearrange("p t g -> p (t g)")
                for k in range(2):
                    pe.matmul(bank[:, k, :], self.tri, Gf[:, k * 512:(k + 1) * 512], start=True, stop=True)
                    m = pe.matmul(bank[:, 2 + k, :], self.oneb, Gf[:, k * 512:(k + 1) * 512], start=True, stop=True)
                m.then_inc(s("rank"), 1)

            def blocks_pe(self, pe, n):
                s = self.s
                w1, w2 = self.weights(n)
                pe.wait_ge(s("w%d" % (n % 2)), 32 * (n // 2 + 1))
                pe.wait_ge(s("b"), 32 * (n + 1))
                pe.wait_ge(s("slots"), max(n + 1, 3))

                def groups(i):
                    return [pe.value_load(self.grp[0:1, n, ds(i * 4 + k, 1)], min_val=0, max_val=31 * P) for k in range(4)]

                def flip(i, q):
                    pe.wait_ge(s("xin%d" % q), n * 64 + (part(i, q, 4) + 1) * 16)
                    for k in range(4):
                        pe.transpose(bank[:, 0, k * P:(k + 1) * P], self.xin[:, q, k, 0:P], ident[:, :])
                    for k in range(4):
                        m = pe.transpose(bank[0:8, 1, k * P:(k + 1) * P], self.xin[:, q, k, P:P + 8], ident[:, :])
                    m.then_inc(s("t1"), 1)

                def hidden(i, q):
                    off = groups(i)
                    pe.wait_ge(s("xT"), n * 16 + i + 1)
                    pe.wait_ge(s("mT"), n * 16 + i + 1)
                    wait(pe, s("act"), n * 16 + i)
                    for k in range(4):
                        o = bank[:, 2, k * P:(k + 1) * P]
                        pe.matmul(o, self.xT[:, q % 2, k * P:(k + 1) * P], w1[:, ds(off[k], P)], start=True, stop=False)
                        m = pe.matmul(o, self.mT[0:8, q, k * P:(k + 1) * P], self.b1[0:8, ds(off[k], P)],
                                      start=False, stop=True)
                    m.then_inc(s("h"), 1)

                def flip_hidden(i, q):
                    pe.wait_ge(s("hm"), n * 16 + i + 1)
                    for k in range(4):
                        m = pe.transpose(bank[:, 3, k * P:(k + 1) * P], self.hm[:, q % 2, k * P:(k + 1) * P], ident[:, :])
                    m.then_inc(s("t2"), 1)

                def output(i, q):
                    off = groups(i)
                    pe.wait_ge(s("hT"), n * 16 + i + 1)
                    wait(pe, s("yo"), n * 16 + i)
                    for k in range(4):
                        o = bank[:, 4, k * P:(k + 1) * P]
                        pe.matmul(o, self.hT[:, q % 2, k * P:(k + 1) * P], w2[:, ds(off[k], P)], start=True, stop=False)
                        m = pe.matmul(o, self.mT[0:8, q, k * P:(k + 1) * P], self.b2[0:8, ds(off[k], P)],
                                      start=False, stop=True)
                    m.then_inc(s("y"), 1)

                def turn(i, q, rest):
                    if rest >= 1:
                        hidden(i + 1, (q + 1) % 4)
                    flip_hidden(i, q)
                    if rest >= 2:
                        flip(i + 2, (q + 2) % 4)
                    output(i, q)

                flip(0, 0)
                hidden(0, 0)
                flip(1, 1)
                turns4(pe, turn)

            def attend_pe(self, pe):
                s = self.s
                pe.wait_ge(s("yo"), 48)
                def front(i, q4):
                    u = q4 % 2
                    pe.wait_ge(s("qk"), i * 2 + 2)
                    for k in range(2):
                        for t in range(QT):
                            m = pe.transpose(bank[:, 0, (k * 2 + t) * P:(k * 2 + t + 1) * P], self.qk[:, u, k, t, :],
                                             ident[:, :])
                    m.then_inc(s("qk_ps"), 1)
                    pe.wait_ge(s("qkT"), i + 1)
                    wait(pe, s("ae"), i)
                    for t in range(QT):
                        m = pe.matmul(bank[:, 1, t * SQ:(t + 1) * SQ], self.qkT[:, u, t * P:(t + 1) * P],
                                      self.qkT[:, u, SQ:2 * SQ], start=True, stop=True)
                    m.then_inc(s("as_ps"), 1)

                def back(i, q4):
                    u = q4 % 2
                    pe.wait_ge(s("ae"), i + 1)
                    for k in range(QT):
                        for t in range(QT):
                            m = pe.transpose(bank[:, 2, (k * 2 + t) * P:(k * 2 + t + 1) * P],
                                             self.e[:, u, t, k * P:(k + 1) * P], ident[:, :])
                    m.then_inc(s("aeT_ps"), 1)
                    pe.wait_ge(s("aeT"), i + 1)
                    wait(pe, s("yb"), i)
                    pe.wait_ge(s("v%d" % q4), (part(i, q4, 4) + 1) * 32)
                    for t in range(QT):
                        for k in range(QT):
                            m = pe.matmul(bank[:, 3, t * P:(t + 1) * P], self.eT[:, u, (k * 2 + t) * P:(k * 2 + t + 1) * P],
                                          self.va[:, ds(i * 2 + k, 1), :].rearrange("p o d -> p (o d)"),
                                          start=(k == 0), stop=(k == 1))
                    m.then_inc(s("ao_ps"), 1)
                    pe.wait_ge(s("yb"), i + 1)
                    wait(pe, s("yT"), i)
                    for t in range(QT):
                        m = pe.transpose(bank[:, 4, t * P:(t + 1) * P], self.yb[:, u, t, :], ident[:, :])
                    m.then_inc(s("yT_ps"), 1)

                def turn(i, q4, rest):
                    if rest >= 1:
                        front(i + 1, (q4 + 1) % 4)
                    back(i, q4)

                front(0, 0)
                turns4(pe, turn)
                pe.wait_ge(s("yT"), B)

            def dve(self, dve, before):
                s = self.s
                dve.wait_ge(x_done, before)
                norm_stats_dve("F2", x, xc, wide, stat, NT)
                dve.wait_ge(S("norm", "rstd"), NORMS.index(self.tag) + 1)
                dve.tensor_tensor(wide[:, :, :], xc[:, :, :], stat[:, 3, :].unsqueeze(2).to_broadcast([P, NT, P]),
                                  ALU.mult).then_inc(s("again"), 1)
                dve.wait_ge(s("again"), 1)
                c = self.chain = Count(s("chain"))

                def op(f, *args):
                    c.inc(f(*args))
                    c.wait(dve)

                self.op = op
                op(dve.tensor_reduce, stat[:, 0, :], wide[:, :, :], AX.X, ALU.add)
                op(dve.tensor_scalar, stat[:, 1, :], stat[:, 0, :], -1.0 / P, None, ALU.mult)
                dve.tensor_tensor(xc[:, :, :], wide[:, :, :], stat[:, 1, :].unsqueeze(2).to_broadcast([P, NT, P]),
                                  ALU.add).then_inc(s("centred2"), 1)
                dve.wait_ge(s("squares2"), 1)
                op(dve.tensor_reduce, stat[:, 2, :], wide[:, :, :], AX.X, ALU.add)
                dve.tensor_scalar(stat[:, 4, :], stat[:, 2, :], 1.0 / (P - 1), None, ALU.mult).then_inc(s("var2"), 1)
                dve.wait_ge(s("sd2"), 1)
                dve.tensor_scalar(stat[:, 6, :], stat[:, 5, :], LN_EPS, None, ALU.add).then_inc(s("var2"), 1)
                dve.wait_ge(s("sd2"), 2)
                op(dve.reciprocal, stat[:, 3, :], stat[:, 7, :])
                dve.tensor_tensor(xc[:, :, :], xc[:, :, :], stat[:, 3, :].unsqueeze(2).to_broadcast([P, NT, P]),
                                  ALU.mult).then_inc(s("xn"), 1)
                for q in range(8):
                    dve.wait_ge(s("flip_ps"), at("F2", "flip_ps") + q + 1)
                    dve.tensor_copy(xnT_all[:, q * 512:(q + 1) * 512], bank[:, q, :]).then_inc(s("flip"), 1)
                for n in range(3):
                    self.route_dve(dve, n)
                for n in range(3):
                    self.blocks_dve(dve, n)
                self.attend_dve(dve)
                self.route_dve(dve, 3)
                self.blocks_dve(dve, 3)
                dve.wait_ge(s("gathered"), 16 * NT)
                op(dve.tensor_tensor, x[:, :, :], x[:, :, :], self.out, ALU.add)
                dve.sem_inc(x_done, 1)

            def route_dve(self, dve, n):
                s, op = self.s, self.op
                dve.wait_ge(s("nw%d" % (n % 2)), 32 * (n // 2 + 1))
                nbn = self.nb[:, n % 2, 0:255]
                op(dve.tensor_scalar, nbn, nbn, -1.0, None, ALU.mult)
                for tp in range(16):
                    dve.wait_ge(s("nodes"), n * 16 + tp + 1)
                    dve.tensor_tensor(self.bits[:, 2 * tp:2 * tp + 2, 0:255],
                                      bank[:, (tp + 4) % 8, 0:510].rearrange("p (t n) -> p t n", t=2),
                                      nbn.unsqueeze(1).to_broadcast([P, 2, 255]), ALU.is_gt).then_inc(s("bits"), 1)
                dve.wait_ge(s("bits"), 16 * (n + 1))

                def split(dst, src, bit, w):
                    d = dst.rearrange("p t (j o) -> p t j o", o=2)
                    op(dve.tensor_tensor, d[:, :, :, 1], src, bit, ALU.mult)
                    op(dve.tensor_tensor, d[:, :, :, 0], src, d[:, :, :, 1], ALU.subtract)

                def ind(buf, w):
                    return buf[:, 0:NT * w].rearrange("p (t j) -> p t j", j=w)

                one = onesf[:, 0:1].unsqueeze(1).to_broadcast([P, NT, 1])
                split(ind(self.oa, 2), one, self.bits[:, :, 0:1], 1)
                src, dst = self.oa, self.ob
                for l in range(1, 5):
                    w = 1 << l
                    out = self.G if l == 4 else ind(dst, 2 * w)
                    split(out, ind(src, w), self.bits[:, :, w - 1:2 * w - 1], w)
                    src, dst = dst, src
                dve.sem_inc(s("G"), 1)
                for l, (c0, w) in enumerate(((0, 1), (1, 2), (3, 4))):
                    n0 = 31 * w + (w - 1)
                    lev = self.bits[:, :, n0:n0 + 32 * w].rearrange("p t (g c) -> p t c g", c=w)
                    tm = self.tmp[:, 0:NT * w * 32].rearrange("p (t c g) -> p t c g", t=NT, c=w)
                    op(dve.tensor_tensor, tm, lev, self.G.unsqueeze(2).to_broadcast([P, NT, w, 32]), ALU.mult)
                    op(dve.tensor_reduce, self.sub[:, :, c0:c0 + w], tm, AX.X, ALU.add)
                if n:
                    dve.wait_ge(s("scattered"), 16 * NT * n)
                split(self.p1, one, self.sub[:, :, 0:1], 1)
                split(self.p2, self.p1, self.sub[:, :, 1:3], 2)
                split(self.xm[:, :, P:P + 8], self.p2, self.sub[:, :, 3:7], 4)
                dve.wait_ge(s("rank"), n + 1)
                op(dve.tensor_copy, self.totg, bank[:, 2:4, :].rearrange("p k (t g) -> p g (k t)", g=32))
                tf, inf = self.totg.rearrange("p g t -> p (g t)"), self.incl.rearrange("p g t -> p (g t)")
                op(dve.tensor_tensor_scan, inf, onesf[:, 0:1].to_broadcast([P, 1024]), tf, 0.0, ALU.mult, ALU.add)
                op(dve.tensor_tensor, tf, inf, tf, ALU.subtract)
                sm = self.sm
                op(dve.tensor_tensor, sm[:, 0, :], self.incl[:, :, NT - 1], self.totg[:, :, 0], ALU.subtract)
                op(dve.tensor_scalar, self.nbi, sm[:, 0, :], 127.0, None, ALU.add)
                op(dve.tensor_scalar, self.nbi, self.nbi, 7, None, ALU.logical_shift_right)
                op(dve.tensor_copy, sm[:, 1, :], self.nbi)
                op(dve.tensor_tensor_scan, sm[:, 2, :], onesf[:, 0:1].to_broadcast([P, 32]), sm[:, 1, :], 0.0,
                   ALU.mult, ALU.add)
                op(dve.tensor_tensor, sm[:, 3, :], sm[:, 2, :], sm[:, 1, :], ALU.subtract)
                op(dve.scalar_tensor_tensor, sm[:, 4, :], sm[:, 3, :], 128.0, self.totg[:, :, 0], ALU.mult, ALU.subtract)
                op(dve.tensor_tensor, self.incl, self.totg, sm[:, 4, :].unsqueeze(2).to_broadcast([P, 32, NT]), ALU.add)
                sl = ind(self.oa, 32)
                op(dve.tensor_tensor, sl, bank[:, 0:2, :].rearrange("p k (t g) -> p (k t) g", g=32),
                   self.incl.rearrange("p g t -> p t g"), ALU.add)
                op(dve.tensor_tensor, sl, sl, self.G, ALU.mult)
                op(dve.tensor_reduce, self.slotf, sl, AX.X, ALU.add)
                op(dve.tensor_copy, self.slot[:, n, :], self.slotf)
                cmp = self.tmp[0:1, 0:64 * 32].rearrange("p (j g) -> p j g", g=32)
                dve.wait_ge(s("const"), 16)
                op(dve.tensor_tensor, cmp, self.iota[0:1, :].unsqueeze(2).to_broadcast([1, 64, 32]),
                   sm[0:1, 2, :].unsqueeze(1).to_broadcast([1, 64, 32]), ALU.is_ge)
                op(dve.tensor_reduce, self.ob[0:1, 0:64], cmp, AX.X, ALU.add)
                dve.tensor_scalar(self.grp[0:1, n, :], self.ob[0:1, 0:64], 31.0, float(P), ALU.min, ALU.mult).then_inc(s("slots"), 1)
                dve.wait_ge(s("slots"), n + 1)

            def blocks_dve(self, dve, n):
                s = self.s

                def flip(i, q):
                    dve.wait_ge(s("t1"), n * 16 + i + 1)
                    dve.tensor_copy(self.xT[:, q % 2, :], bank[:, 0, :]).then_inc(s("xT"), 1)

                def hidden(i, q):
                    mask = self.xin[:, q, :, P:P + 8].unsqueeze(3).to_broadcast([P, 4, 8, 16])
                    out = self.hm[:, q % 2, :].rearrange("p (k l j) -> p k l j", k=4, l=8)
                    dve.wait_ge(s("act"), n * 16 + i + 1)
                    dve.tensor_tensor(out, self.gl[:, q % 2, :].rearrange("p (k l j) -> p k l j", k=4, l=8), mask,
                                      ALU.mult).then_inc(s("hm"), 1)

                def output(i, q):
                    dve.wait_ge(s("y"), n * 16 + i + 1)
                    wait(dve, s("ys%d" % (q % 2)), n * 128 + part(i, q % 2, 2) * 16)
                    dve.tensor_copy(self.yo[:, q % 2, :, :].rearrange("p k d -> p (k d)"), bank[:, 4, :]).then_inc(s("yo"), 1)

                def turn(i, q, rest):
                    if rest >= 1:
                        hidden(i + 1, (q + 1) % 4)
                    if rest >= 2:
                        flip(i + 2, (q + 2) % 4)
                    output(i, q)

                flip(0, 0)
                hidden(0, 0)
                flip(1, 1)
                turns4(dve, turn)
                dve.wait_ge(s("ys0"), 128 * (n + 1))
                dve.wait_ge(s("ys1"), 128 * (n + 1))

            def attend_dve(self, dve):
                s = self.s
                sc = float(P) ** -0.5
                sm = self.small

                def front(i, u):
                    dve.wait_ge(s("qk_ps"), i + 1)
                    dve.tensor_copy(self.qkT[:, u, :], bank[:, 0, :]).then_inc(s("qkT"), 1)
                    c = Count(s("amax"), i * 2)
                    dve.wait_ge(s("as_ps"), i + 1)
                    c.inc(dve.tensor_reduce(sm[:, 0, u, :], bank[:, 1, :].rearrange("p (t k) -> p t k", t=QT), AX.X, ALU.max))
                    c.wait(dve)
                    c.inc(dve.tensor_scalar(sm[:, 1, u, :], sm[:, 0, u, :], -sc, None, ALU.mult))

                def back(i, u):
                    dve.wait_ge(s("aeT_ps"), i + 1)
                    dve.tensor_copy(self.eT[:, u, :], bank[:, 2, :]).then_inc(s("aeT"), 1)
                    dve.reciprocal(sm[:, 3, u, :], sm[:, 2, u, :]).then_inc(s("arec"), 1)
                    dve.wait_ge(s("arec"), i + 1)
                    dve.wait_ge(s("ao_ps"), i + 1)
                    for t in range(QT):
                        m = dve.scalar_tensor_tensor(self.yb[:, u, t, :], bank[:, 3, t * P:(t + 1) * P],
                                                     sm[:, 3, u, t:t + 1],
                                                     self.xm[:, ds(i * 2 + t, 1), 0:P].rearrange("p o d -> p (o d)"), ALU.mult, ALU.add)
                    m.then_inc(s("yb"), 1)
                    dve.wait_ge(s("yb"), i + 1)
                    dve.tensor_tensor(x[:, ds(i * 2, 2), :], x[:, ds(i * 2, 2), :], self.yb[:, u, :, :], ALU.add).then_inc(s("xy"), 1)
                    dve.tensor_copy(self.xm[:, ds(i * 2, 2), 0:P], self.yb[:, u, :, :]).then_inc(s("xy"), 1)

                piped(dve, front, back)
                dve.wait_ge(s("xy"), 2 * B)
                dve.wait_ge(s("yT"), B)

            def act(self, act, before):
                s = self.s
                act.wait_ge(x_done, before)
                norm_stats_act("F2", xc, wide, stat, NT)
                act.wait_ge(s("centred2"), 1)
                act.activation(wide[:, :, :], xc[:, :, :], ACT.Square).then_inc(s("squares2"), 1)
                act.wait_ge(s("var2"), 1)
                act.activation(stat[:, 5, :], stat[:, 4, :], ACT.Sqrt).then_inc(s("sd2"), 1)
                act.wait_ge(s("var2"), 2)
                act.activation(stat[:, 7, :], stat[:, 6, :], ACT.Sqrt).then_inc(s("sd2"), 1)
                for n in range(4):
                    if n == 3:
                        self.attend_act(act)

                    def flip(i, q):
                        act.wait_ge(s("t1"), n * 16 + i + 1)
                        if n == 0 and isinstance(i, int) and i == 0:
                            act.wait_ge(s("slots"), 3)
                        act.activation(self.mT[0:8, q, :], bank[0:8, 1, :], ACT.Identity).then_inc(s("mT"), 1)

                    def hidden(i, q):
                        act.wait_ge(s("h"), n * 16 + i + 1)
                        act.activation(self.gl[:, q % 2, :], bank[:, 2, :], ACT.Gelu if n == 3 else ACT.Relu).then_inc(s("act"), 1)

                    def flip_hidden(i, q):
                        act.wait_ge(s("t2"), n * 16 + i + 1)
                        act.activation(self.hT[:, q % 2, :], bank[:, 3, :], ACT.Identity).then_inc(s("hT"), 1)

                    def turn(i, q, rest):
                        if rest >= 1:
                            hidden(i + 1, (q + 1) % 4)
                        flip_hidden(i, q)
                        if rest >= 2:
                            flip(i + 2, (q + 2) % 4)

                    flip(0, 0)
                    hidden(0, 0)
                    flip(1, 1)
                    turns4(act, turn)

            def attend_act(self, act):
                s = self.s
                sm = self.small

                act.wait_ge(s("yo"), 48)
                act.wait_ge(s("queries_keys"), 2 * NT * 16)

                def load(i, u):
                    wait(act, s("qk_ps"), i - 1)
                    for k, src in enumerate((xc, wide)):
                        act.activation(self.qk[:, u, k, :, :], src[:, ds(i * 2, 2), :], ACT.Identity).then_inc(s("qk"), 1)

                def front(i, u):
                    act.wait_ge(s("amax"), i * 2 + 2)
                    for t in range(QT):
                        m = act.activation(self.e[:, u, t, :], bank[:, 1, t * SQ:(t + 1) * SQ], ACT.Exp,
                                           bias=sm[:, 1, u, t:t + 1], scale=float(P) ** -0.5,
                                           accum_out=sm[:, 2, u, t:t + 1])
                    m.then_inc(s("ae"), 1)

                def back(i, u):
                    act.wait_ge(s("yT_ps"), i + 1)
                    act.activation(xnT_all[:, ds(i * SQ, SQ)], bank[:, 4, 0:SQ], ACT.Identity).then_inc(s("yT"), 1)

                def turn(i, u, rest):
                    if rest >= 1:
                        front(i + 1, 1 - u)
                    if rest >= 2:
                        load(i + 2, u)
                    back(i, u)

                load(0, 0)
                front(0, 0)
                load(1, 1)
                turns(act, turn)

            def pool(self, pool, before):
                s = self.s
                pool.wait_ge(x_done, before)
                pool.memset(self.tri, 1.0).then_inc(s("tri"), 1)
                pool.memset(self.oneb, 1.0).then_inc(s("tri"), 1)
                pool.wait_ge(s("tri"), 2)
                pool.affine_select(self.tri, self.tri, [[1, P]], ALU.is_gt, 0.0, base=0,
                                   channel_multiplier=-1).then_inc(s("tri"), 1)
                pool.wait_ge(s("xn"), at("F2", "xn") + 1)
                pool.tensor_copy(self.xm[:, :, 0:P], xc[:, :, :]).then_inc(s("xm"), 1)
                pool.wait_ge(s("xm"), 1)
                pool.wait_ge(s("zeroed"), 3 * 16 * 16)

                def gather(dst, n, t, done):
                    ys = A["ys%d" % n].rearrange("k p w -> (k p) w")
                    pool.indirect_dma_start(dst, None, ys, bass.IndirectOffsetOnAxis(ap=self.slot[:, n, t:t + 1], axis=0)).then_inc(done, 16)

                for n in range(4):
                    if n == 3:
                        pool.wait_ge(s("ys0"), 128 * 3)
                        pool.wait_ge(s("ys1"), 128 * 3)
                        for i in range(B):
                            if i >= 4:
                                pool.wait_ge(s("v%d" % (i % 4)), i // 4 * 32)
                            for t in range(QT):
                                gather(self.va[:, 2 * i + t, :], 2, 2 * i + t, s("v%d" % (i % 4)))
                    pool.wait_ge(s("slots"), n + 1)
                    xs = A["xs%d" % (n % 3)].rearrange("k p w -> (k p) w")
                    for t in range(NT):
                        pool.indirect_dma_start(xs, bass.IndirectOffsetOnAxis(ap=self.slot[:, n, t:t + 1], axis=0),
                                                self.xm[:, t, :], None).then_inc(s("scattered"), 16)
                    if n == 2:
                        pool.wait_ge(s("ys0"), 128 * 2)
                        pool.wait_ge(s("ys1"), 128 * 2)
                        for m, dst in enumerate((xc, wide)):
                            for t in range(NT):
                                gather(dst[:, t, :], m, t, s("queries_keys"))
                pool.wait_ge(s("ys0"), 128 * 4)
                pool.wait_ge(s("ys1"), 128 * 4)
                for t in range(NT):
                    gather(self.out[:, t, :], 3, t, s("gathered"))

        FEED = {"F0": TopTwo(), "F1": SoftSlots(), "F2": Trees(), "F3": ExpertChoice()}

        cc = prob[:, 0, :, :].rearrange("p a b -> p (a b)")[:, 0:1024].rearrange("p (t e) -> p t e", t=8)
        csq = prob[:, 1, :, :].rearrange("p a b -> p (a b)")[:, 0:1024].rearrange("p (t e) -> p t e", t=8)

        wflat = wide[:, :, :].rearrange("p t e -> p (t e)")
        m0_raw = wflat[:, 0:1024].bitcast(I32)
        m1_raw = wflat[:, 1024:1152].bitcast(I32).rearrange("p (t k) -> p t k", t=QT)
        m2_raw = wflat[:, 1152:1408].bitcast(U8)
        mf0 = wflat[:, 1408:2432].rearrange("p (b k) -> p b k", b=B)
        mf2 = wflat[:, 2432:3456].rearrange("p (b k) -> p b k", b=B)
        mf1 = wflat[:, 3456:3584].rearrange("p (t k) -> p t k", t=QT)
        al = wflat[:, 3584:3584 + 64]
        diag = wflat[:, 3712:3968].rearrange("p (t q) -> p t q", t=QT)

        block = ctx.enter_context(nc.Block())

        @block.sync
        def _(sp):
            def load(dst, src):
                sp.dma_start(dst, src).then_inc(loaded, 16)

            load(x[:, :, :], A["x"].rearrange("b (t p) d -> p (b t) d", p=P))
            load(ident[:, :], A["ident"])
            load(headmask[:, :], A["headmask"])
            load(ctxT[:, :, :], A["ctxT"])
            load(cols[:, :], A["cols"])
            load(rows[:, :, :].rearrange("p n d -> p (n d)"), A["rows"].rearrange("n d -> (n d)").partition_broadcast(P))
            load(wx[:, :, :, :].rearrange("p l m e -> p (l m e)"), A["wx"])
            load(m0_raw, A["itok"].rearrange("b k -> (b k)").partition_broadcast(P))
            load(m1_raw, A["mask_qk"].rearrange("(t p) k -> p t k", p=P))
            load(m2_raw, A["mask_bk"].rearrange("b k -> (b k)").partition_broadcast(P))
            sp.wait_ge(cast, 3)
            for n in range(3):
                for k in range(16):
                    sp.dma_start(A["xs%d" % n][4 * k:4 * k + 4, :, :].rearrange("k p w -> p k w"),
                                 zeros[:, :].rearrange("p (k w) -> p k w", k=4)).then_inc(S("F2", "zeroed"), 16)
            for n, stage in enumerate(PLAN):
                if stage == "X2":
                    sp.wait_ge(x_done, n + 1)
                    sp.dma_start(cx, A["ctx"].rearrange("(t p) d -> p t d", p=P)).then_inc(S("X", "cx"), 16)
                elif stage[0] == "F":
                    FEED[stage].sp(sp, n + 1)
            sp.wait_ge(x_done, len(PLAN) + 1)
            sp.dma_start(A["out"].rearrange("b (t p) d -> p (b t) d", p=P), x[:, :, :]).then_inc(stored, 16)
            sp.wait_ge(stored, 16)

        def prepare_dve(dve):
            dve.memset(row0[:, :], 0.0).then_inc(cast, 1)
            dve.memset(onesf[:, :], 1.0).then_inc(cast, 1)
            dve.memset(zeros[:, :], 0.0).then_inc(cast, 1)
            dve.wait_ge(cast, 3)
            dve.memset(row0[0:1, :], 1.0).then_inc(cast, 1)
            dve.wait_ge(loaded, 16 * LOADS)
            dve.tensor_copy(identb[:, :], ident[:, :]).then_inc(cast, 1)
            c = Count(masks)

            def op(f, *args):
                c.inc(f(*args))
                c.wait(dve)

            op(dve.tensor_scalar, mf0.rearrange("p b k -> p (b k)"), m0_raw, 0.0, None, ALU.is_equal)
            op(dve.tensor_reduce, al[:, 0:B], mf0, AX.X, ALU.min)
            op(dve.tensor_scalar, keep0[:, :], al[:, 0:B], -1.0, 1.0, ALU.mult, ALU.add)
            op(dve.tensor_tensor, mf0, mf0, keep0[:, :].unsqueeze(2).to_broadcast([P, B, SK]), ALU.mult)
            op(dve.tensor_scalar, bias0[:, :, :], mf0, MASKED, None, ALU.mult)
            op(dve.tensor_copy, mf2.rearrange("p b k -> p (b k)"), m2_raw)
            op(dve.tensor_reduce, al[:, 16:32], mf2, AX.X, ALU.min)
            op(dve.tensor_tensor, mf2[:, :, 0], mf2[:, :, 0], al[:, 16:32], ALU.subtract)
            op(dve.tensor_scalar, bias2[:, :, :], mf2, MASKED, None, ALU.mult)
            op(dve.tensor_scalar, mf1, m1_raw, 0.0, None, ALU.is_equal)
            op(dve.tensor_reduce, al[:, 32:34], mf1, AX.X, ALU.min)
            op(dve.tensor_scalar, al[:, 34:36], al[:, 32:34], -1.0, 1.0, ALU.mult, ALU.add)
            op(dve.tensor_tensor, mf1, mf1, al[:, 34:36].unsqueeze(2).to_broadcast([P, QT, SK]), ALU.mult)
            op(dve.tensor_scalar, bias1[:, :, :], mf1, MASKED, None, ALU.mult)
            for t in range(QT):
                op(dve.tensor_scalar, diag[:, t, :], ident[:, :], al[:, 34 + t:35 + t], None, ALU.mult)
            dve.sem_inc(masks_ps, 1)
            dve.wait_ge(masks_ps, 2)
            dve.tensor_copy(keep1[:, :], bank[:, 0, 0:SQ]).then_inc(masks_ps, 1)
            dve.wait_ge(masks_ps, 3)
            dve.sem_inc(x_done, 1)

        @block.tensor
        def _(pe):
            pe.wait_ge(masks_ps, 1)
            for t in range(QT):
                m = pe.matmul(bank[:, 0, t * P:(t + 1) * P], onesf[:, :], diag[:, t, :], start=True, stop=True,
                              skip_group_check=True)
            m.then_inc(masks_ps, 1)
            for n, stage in enumerate(PLAN):
                if stage[0] == "X":
                    attn_pe(Attn(int(stage[1])), n + 1)
                else:
                    FEED[stage].pe(pe, n + 1)

        @block.vector
        def _(dve):
            prepare_dve(dve)
            for n, stage in enumerate(PLAN):
                if stage[0] == "X":
                    attn_dve(Attn(int(stage[1])), n + 1)
                else:
                    FEED[stage].dve(dve, n + 1)

        @block.scalar
        def _(act):
            act.wait_ge(loaded, 16 * LOADS)
            for n, stage in enumerate(PLAN):
                if stage[0] == "X":
                    attn_act(Attn(int(stage[1])), n + 1)
                else:
                    FEED[stage].act(act, n + 1)

        @block.gpsimd
        def _(pool):
            pool.wait_ge(loaded, 16 * LOADS)
            for n, stage in enumerate(PLAN):
                if stage[0] == "X":
                    attn_pool(Attn(int(stage[1])), n + 1)
                else:
                    FEED[stage].pool(pool, n + 1)


def _in_layout(inputs):
    i = {k: np.asarray(v) for k, v in inputs.items()}
    f = np.float32
    arrays = {"x": i["x"], "itok": i["itok_BxS2_0_99"]}
    arrays["mask_qk"] = i["mask_1x1xSxS2_ik0"].reshape(SQ, SK)
    arrays["mask_bk"] = i["mask_BxS2_bk0"]
    ctx = i["ctx_1024"].reshape(B * SK, P)
    arrays["ctx"] = ctx
    arrays["ctxT"] = np.repeat(ctx.T.reshape(P, B, 1, SK), 2, 2)
    arrays["ident"] = np.eye(P, dtype=f)
    arrays["headmask"] = (np.arange(P)[:, None] // HD == np.arange(NH)[None, :]).astype(f)
    X = {0: "L0_xattn_", 1: "L1_xattn_", 2: "L2_xattn_", 3: "L3_xattn_"}
    mats = []
    for L in range(4):
        for m in "qkvo":
            w = i[X[L] + ("w" if L == 1 else "W") + m]
            mats.append(w.T if L else w)
    arrays["wx"] = np.stack(mats, 1).reshape(P, 16 * P)
    arrays["tri8"] = np.broadcast_to(np.tril(np.ones((8, 8), f), -1).reshape(1, 64), (P, 64))
    arrays["F0_wg"] = i["L0_ffn_Wg"]
    arrays["F0_w11"] = i["L0_ffn_W11"].transpose(1, 0, 2).reshape(P, -1)
    arrays["F0_w12"] = i["L0_ffn_W12"].transpose(1, 0, 2).reshape(P, -1)
    arrays["F0_w2"] = i["L0_ffn_W2"].reshape(8, 2, P, P).transpose(2, 0, 1, 3).reshape(P, -1)

    arrays["F3_rw"] = i["L3_ffn_router_w"]
    arrays["F3_rb"] = i["L3_ffn_router_b"]
    arrays["F3_w1"] = i["L3_ffn_w1"].transpose(1, 0, 2).reshape(P, -1)
    arrays["F3_b1"] = i["L3_ffn_b1"].reshape(32, P).T
    arrays["F3_w2"] = i["L3_ffn_w2"].reshape(8, 4, P, P).transpose(2, 0, 1, 3).reshape(P, -1)
    arrays["F3_b2"] = i["L3_ffn_b2"]
    arrays["bits"] = (1 << np.arange(29, -1, -1)).astype(np.int32)

    arrays["F1_phi"] = i["L1_ffn_phi"].reshape(P, -1)
    arrays["F1_w"] = i["L1_ffn_W"].reshape(16, 4, P, P).transpose(0, 2, 1, 3).reshape(16, P, 4 * P)
    arrays["F1_b"] = i["L1_ffn_b"].T

    arrays["iota64"] = np.arange(64, dtype=f)
    T = ["L2_ffn_%s_" % t for t in "qkvf"]
    arrays["F2_nw"] = np.stack([i[t + "nw"].T for t in T])
    arrays["F2_nb"] = np.stack([i[t + "nb"] for t in T])
    arrays["F2_w1"] = np.stack([i[t + "w1"].transpose(1, 0, 2).reshape(P, -1) for t in T])
    arrays["F2_w2"] = np.stack([i[t + "w2"].reshape(32, P, P).transpose(1, 0, 2).reshape(P, -1) for t in T])
    b1 = np.zeros((4, 8, 32, 8, 16), f)
    for n, t in enumerate(T):
        for l in range(8):
            b1[n, l, :, l, :] = i[t + "b1"].reshape(32, 8, 16)[:, l, :]
    arrays["F2_b1"] = b1.reshape(4, 8, -1)
    arrays["F2_b2"] = np.stack([i[t + "b2"].reshape(32, 8, P).transpose(1, 0, 2).reshape(8, -1) for t in T])

    def vec(name):
        if name[:2] in ("qn", "cn"):
            return i["L2_xattn_" + name]
        return i[name[:2] + "_xattn_" + name[3:]]
    arrays["cols"] = np.stack([vec(n) for n in COLS], 1)
    arrays["rows"] = np.stack([vec(n) for n in ROWS], 0)
    return {k: np.ascontiguousarray(v) for k, v in arrays.items()}


def kernel(**inputs):
    import concourse.bacc as _bacc
    from concourse.bass_utils import run_bass_kernel_spmd as _run

    nc = _bacc.Bacc("TRN2", target_bir_lowering=False, num_devices=1)
    arrays = _in_layout(inputs)
    A = {}
    for name, a in arrays.items():
        A[name] = nc.dram_tensor(f"in_{name}", a.shape, mybir.dt.from_np(a.dtype), kind="ExternalInput").ap()
    A["out"] = nc.dram_tensor("out_x", (B, SQ, P), F32, kind="ExternalOutput").ap()
    A["y_slots"] = nc.dram_tensor("y_slots", (B, P, 16, P), F32, kind="Internal").ap()
    for n in range(3):
        A["xs%d" % n] = nc.dram_tensor("xs%d" % n, (64, P, P + 8), F32, kind="Internal").ap()
    for n in range(4):
        A["ys%d" % n] = nc.dram_tensor("ys%d" % n, (64, P, P), F32, kind="Internal").ap()
    build(nc, A)
    r = _run(nc, [{f"in_{k}": a for k, a in arrays.items()}], core_ids=[0])
    return r.results[0]["out_x"]
```
